# Optimizing a Trainium2 kernel written in Bass

```python
import numpy as np
import jax
import jax.numpy as jnp

def _softmax(x, axis=-1):
    return jax.nn.softmax(x, axis=axis)

def _gelu(x):
    return jax.nn.gelu(x, approximate=True)

def _silu(x):
    return jax.nn.silu(x)

def _sigmoid(x):
    return jax.nn.sigmoid(x)

def _layernorm(x, axis=-1, eps=1e-05):
    m = jnp.mean(x, axis=axis, keepdims=True)
    v = jnp.var(x, axis=axis, keepdims=True)
    return (x - m) / jnp.sqrt(v + eps)

def _scatter_add(tgt, idx, src, axis=0):
    return tgt.at[idx].add(src)

def _segment_sum(src, seg, n):
    return jax.ops.segment_sum(src, seg, n)
kernel_name = 'mk_decoder_postln_d2_seqx_r8_b9938a'

def setup_inputs(seed: int=0):
    np.random.seed(seed)
    _w = jnp.asarray

    def _rec_inputs():
        import jax
        import jax.numpy as jnp
        _rk = jax.random.key(seed)
        x = -0.0002928 + 1 * jax.random.normal(jax.random.fold_in(_rk, 1), (32, 64, 128), jnp.float32)
        _lenS = 64 - jax.random.randint(jax.random.fold_in(_rk, 7), (32,), 0, max(1, 64 // 4) + 1, jnp.int32)
        _lenS2 = 64 - jax.random.randint(jax.random.fold_in(_rk, 8), (32,), 0, max(1, 64 // 4) + 1, jnp.int32)
        _ctx_1024P = jax.random.normal(jax.random.fold_in(_rk, 11), (32, 16, 128), jnp.float32)
        _ctx_1024c = jax.random.dirichlet(jax.random.fold_in(_rk, 511), 0.3 * jnp.ones((16,), jnp.float32), (32, 64))
        _ctx_1024t = jnp.einsum('bsk,bkd->bsd', _ctx_1024c, _ctx_1024P)
        _ctx_1024t = _ctx_1024t * jax.lax.rsqrt(jnp.mean(jnp.square(_ctx_1024t)) + 1e-12) * 0.953939
        ctx_1024 = 4.13588e-05 + 0.999923 * (_ctx_1024t + 0.3 * jax.random.normal(jax.random.fold_in(_rk, 611), (32, 64, 128), jnp.float32))
        _validS = jnp.arange(64)[None, :] < _lenS[:, None]
        _validS2 = jnp.arange(64)[None, :] < _lenS2[:, None]
        _causal = jnp.tril(jnp.ones((64, 64), dtype=bool))
        mask_BxS2_bf1 = jnp.ones((32, 64), dtype=bool)
        return (x, ctx_1024, mask_BxS2_bf1)
    x, ctx_1024, mask_BxS2_bf1 = _rec_inputs()

    def _L0_attn_setup():
        import jax, jax.numpy as jnp
        import numpy as np
        B, T, C = (2, 256, 128)
        H = 16
        HS = C // H
        key = jax.random.key(seed)
        k1, k2, k3 = jax.random.split(key, 3)
        x = jax.random.normal(k1, (B, T, C), dtype=jnp.float32)
        w_qkv = jax.random.normal(k2, (3 * C, C), dtype=jnp.float32) * C ** (-0.5)
        w_proj = jax.random.normal(k3, (C, C), dtype=jnp.float32) * C ** (-0.5)
        b_proj = jnp.zeros((C,), dtype=jnp.float32)
        return {'x': x, 'w_qkv': w_qkv, 'w_proj': w_proj, 'b_proj': b_proj}
    _L0_attn_all = _L0_attn_setup()
    _L0_attn_in = {k: v for k, v in _L0_attn_all.items() if k in ('w_qkv', 'w_proj', 'b_proj')}
    del _L0_attn_all

    def _L0_xattn_setup():
        import math
        import jax, jax.numpy as jnp
        import numpy as np
        DIM = 128
        HEADS = 16
        DIM_HEAD = DIM // HEADS
        SCALE = DIM_HEAD ** (-0.5)

        def _apply_rotary_emb(x, seq_len):
            pos = jnp.arange(seq_len, dtype=jnp.float32)[:, None]
            div = jnp.exp(jnp.arange(0, DIM_HEAD, 2, dtype=jnp.float32) * (-math.log(10000.0) / DIM_HEAD))
            freqs = pos * div
            emb = jnp.concatenate([freqs, freqs], axis=-1)[None, None].astype(x.dtype)
            x1, x2 = (x[..., :DIM_HEAD // 2], x[..., DIM_HEAD // 2:])
            x_rot = jnp.concatenate([-x2, x1], axis=-1)
            return x * jnp.cos(emb) + x_rot * jnp.sin(emb)
        key = jax.random.key(seed)
        ks = jax.random.split(key, 5)
        b, n_q, n_kv = (2, 256, 512)
        q_x = jax.random.normal(ks[0], (b, n_q, DIM), dtype=jnp.float32)
        kv_x = jax.random.normal(ks[1], (b, n_kv, DIM), dtype=jnp.float32)
        mask = jnp.ones((b, n_kv), dtype=bool)

        def xavier(k, shape):
            bound = math.sqrt(6.0 / (shape[0] + shape[1]))
            return jax.random.uniform(k, shape, jnp.float32, -bound, bound)
        Wq = xavier(ks[2], (DIM, DIM))
        Wkv = xavier(ks[3], (DIM, 2 * DIM))
        Wout = xavier(ks[4], (DIM, DIM))
        return {'q_x': q_x, 'kv_x': kv_x, 'mask': mask, 'Wq': Wq, 'Wkv': Wkv, 'Wout': Wout}
    _L0_xattn_all = _L0_xattn_setup()
    _L0_xattn_in = {k: v for k, v in _L0_xattn_all.items() if k in ('Wq', 'Wkv', 'Wout')}
    del _L0_xattn_all

    def _L0_ffn_setup():
        import jax, jax.numpy as jnp
        import numpy as np
        H = 128
        I = 64
        IS = 128
        E = 16
        G = 4
        TOPK_G = 2
        TOPK = 4
        SCALE = 2.5
        B, S = (2, 128)

        def _relu2(x):
            r = jax.nn.relu(x)
            return r * r

        def _route(scores, bias_corr):
            T = scores.shape[0]
            s_choice = scores + bias_corr
            gs = s_choice.reshape(T, G, E // G)
            group_scores = jnp.sum(jax.lax.top_k(gs, 2)[0], axis=-1)
            gidx = jax.lax.top_k(group_scores, TOPK_G)[1]
            gmask = jnp.sum(jax.nn.one_hot(gidx, G, dtype=scores.dtype), axis=1)
            smask = jnp.repeat(gmask, E // G, axis=1)
            masked = jnp.where(smask > 0, s_choice, 0.0)
            topk_idx = jax.lax.top_k(masked, TOPK)[1]
            topk_w = jnp.take_along_axis(scores, topk_idx, axis=1)
            topk_w = topk_w / (jnp.sum(topk_w, axis=-1, keepdims=True) + 1e-20)
            topk_w = topk_w * SCALE
            return (topk_idx, topk_w)
        key = jax.random.key(seed)
        ks = jax.random.split(key, 8)
        sd = 0.02
        return {'hidden_states': jax.random.normal(ks[0], (B, S, H), jnp.float32), 'Wg': jax.random.normal(ks[1], (E, H), jnp.float32) * sd, 'bias_corr': jax.random.normal(ks[2], (E,), jnp.float32) * 0.01, 'W1': jax.random.normal(ks[3], (E, I, H), jnp.float32) * sd, 'W2': jax.random.normal(ks[4], (E, H, I), jnp.float32) * sd, 'Ws1': jax.random.normal(ks[5], (IS, H), jnp.float32) * sd, 'Ws2': jax.random.normal(ks[6], (H, IS), jnp.float32) * sd}
    _L0_ffn_all = _L0_ffn_setup()
    _L0_ffn_in = {k: v for k, v in _L0_ffn_all.items() if k in ('Wg', 'bias_corr', 'W1', 'W2', 'Ws1', 'Ws2')}
    del _L0_ffn_all

    def _L1_attn_setup():
        import jax, jax.numpy as jnp
        import numpy as np
        import math
        D_MODEL, N_HEADS, D_K, D_C, D_HR = (128, 8, 128, 32, 32)
        B, S = (4, 256)
        key = jax.random.key(seed)
        ks = jax.random.split(key, 17)

        def lin(k, fan_in, fan_out):
            lim = 1.0 / math.sqrt(fan_in)
            kw, kb = jax.random.split(k)
            W = jax.random.uniform(kw, (fan_in, fan_out), jnp.float32, -lim, lim)
            b = jax.random.uniform(kb, (fan_out,), jnp.float32, -lim, lim)
            return (W, b)
        W_DQ, b_DQ = lin(ks[0], D_MODEL, D_C)
        W_UQ, b_UQ = lin(ks[1], D_C, N_HEADS * D_K)
        W_DKV, b_DKV = lin(ks[2], D_MODEL, D_C)
        W_UK, b_UK = lin(ks[3], D_C, N_HEADS * D_K)
        W_UV, b_UV = lin(ks[4], D_C, N_HEADS * D_K)
        W_QR, b_QR = lin(ks[5], D_C, N_HEADS * D_HR)
        W_KR, b_KR = lin(ks[6], D_MODEL, D_HR)
        W_O, b_O = lin(ks[7], N_HEADS * D_K, D_MODEL)
        h_t = jax.random.normal(ks[8], (B, S, D_MODEL), jnp.float32)
        return {'h_t': h_t, 'W_DQ': W_DQ, 'b_DQ': b_DQ, 'W_UQ': W_UQ, 'b_UQ': b_UQ, 'W_DKV': W_DKV, 'b_DKV': b_DKV, 'W_UK': W_UK, 'b_UK': b_UK, 'W_UV': W_UV, 'b_UV': b_UV, 'W_QR': W_QR, 'b_QR': b_QR, 'W_KR': W_KR, 'b_KR': b_KR, 'W_O': W_O, 'b_O': b_O}
    _L1_attn_all = _L1_attn_setup()
    _L1_attn_in = {k: v for k, v in _L1_attn_all.items() if k in ('W_DQ', 'b_DQ', 'W_UQ', 'b_UQ', 'W_DKV', 'b_DKV', 'W_UK', 'b_UK', 'W_UV', 'b_UV', 'W_QR', 'b_QR', 'W_KR', 'b_KR', 'W_O', 'b_O')}
    del _L1_attn_all

    def _L1_xattn_setup():
        import jax, jax.numpy as jnp
        import numpy as np
        D_MODEL = 128
        NUM_HEADS = 16
        HEAD_DIM = D_MODEL // NUM_HEADS
        MAX_SEQ = 64

        def rope_tables(seq_len, dim):
            inv_freq = 1.0 / 10000.0 ** (jnp.arange(0, dim, 2, dtype=jnp.float32) / dim)
            t = jnp.arange(seq_len, dtype=jnp.float32)
            freqs = jnp.einsum('i,j->ij', t, inv_freq)
            emb = jnp.concatenate([freqs, freqs], axis=-1)
            return (jnp.cos(emb), jnp.sin(emb))

        def rotate_half(x):
            x1, x2 = jnp.split(x, 2, axis=-1)
            return jnp.concatenate([-x2, x1], axis=-1)
        key = jax.random.key(seed)
        ks = jax.random.split(key, 12)
        B, S, D = (16, 64, D_MODEL)
        s = 1.0 / np.sqrt(D)
        inp = {'query': jax.random.normal(ks[0], (B, S, D), jnp.float32), 'key': jax.random.normal(ks[1], (B, S, D), jnp.float32), 'value': jax.random.normal(ks[2], (B, S, D), jnp.float32), 'Wq': jax.random.normal(ks[3], (D, D), jnp.float32) * s, 'bq': jnp.zeros((D,), jnp.float32), 'Wk': jax.random.normal(ks[4], (D, D), jnp.float32) * s, 'bk': jnp.zeros((D,), jnp.float32), 'Wv': jax.random.normal(ks[5], (D, D), jnp.float32) * s, 'bv': jnp.zeros((D,), jnp.float32), 'Wo': jax.random.normal(ks[6], (D, D), jnp.float32) * s, 'bo': jnp.zeros((D,), jnp.float32)}
        return inp
    _L1_xattn_all = _L1_xattn_setup()
    _L1_xattn_in = {k: v for k, v in _L1_xattn_all.items() if k in ('Wq', 'bq', 'Wk', 'bk', 'Wv', 'bv', 'Wo', 'bo')}
    del _L1_xattn_all

    def _L1_ffn_setup():
        import jax, jax.numpy as jnp
        import numpy as np
        BLOCK = 32
        W_BITS = 4
        ACT_BITS = 16

        def act_qdq(x):
            qmax = 2.0 ** (ACT_BITS - 1) - 1.0
            scale = jnp.maximum(jnp.max(jnp.abs(x)) / qmax, 1e-12)
            return jnp.clip(jnp.round(x / scale), -qmax - 1.0, qmax) * scale

        def fixed_qdq_u16(x):
            scale = 1.0 / 65536.0
            return jnp.clip(jnp.round(x / scale), 0.0, 65535.0) * scale

        def lpbq_dequant(w):
            O, I = w.shape
            qmax = 2.0 ** (W_BITS - 1) - 1.0
            wb = w.reshape(O, I // BLOCK, BLOCK)
            s = jnp.maximum(jnp.max(jnp.abs(wb), axis=-1, keepdims=True) / qmax, 1e-12)
            wq = jnp.clip(jnp.round(wb / s), -qmax - 1.0, qmax) * s
            return wq.reshape(O, I)
        key = jax.random.key(seed)
        k1, k2, k3, k4 = jax.random.split(key, 4)
        B, S, H, I = (2, 512, 128, 384)
        x = jax.random.normal(k1, (B, S, H), jnp.float32)
        w_gate = jax.random.normal(k2, (I, H), jnp.float32) * 0.02
        w_up = jax.random.normal(k3, (I, H), jnp.float32) * 0.02
        w_down = jax.random.normal(k4, (H, I), jnp.float32) * 0.02
        return {'x': x, 'w_gate': w_gate, 'w_up': w_up, 'w_down': w_down}
    _L1_ffn_all = _L1_ffn_setup()
    _L1_ffn_in = {k: v for k, v in _L1_ffn_all.items() if k in ('w_gate', 'w_up', 'w_down')}
    del _L1_ffn_all
    return {'x': x, 'ctx_1024': ctx_1024, 'mask_BxS2_bf1': mask_BxS2_bf1, 'L0_attn_w_qkv': _L0_attn_in['w_qkv'], 'L0_attn_w_proj': _L0_attn_in['w_proj'], 'L0_attn_b_proj': _L0_attn_in['b_proj'], 'L0_xattn_Wq': _L0_xattn_in['Wq'], 'L0_xattn_Wkv': _L0_xattn_in['Wkv'], 'L0_xattn_Wout': _L0_xattn_in['Wout'], 'L0_ffn_Wg': _L0_ffn_in['Wg'], 'L0_ffn_bias_corr': _L0_ffn_in['bias_corr'], 'L0_ffn_W1': _L0_ffn_in['W1'], 'L0_ffn_W2': _L0_ffn_in['W2'], 'L0_ffn_Ws1': _L0_ffn_in['Ws1'], 'L0_ffn_Ws2': _L0_ffn_in['Ws2'], 'L1_attn_W_DQ': _L1_attn_in['W_DQ'], 'L1_attn_b_DQ': _L1_attn_in['b_DQ'], 'L1_attn_W_UQ': _L1_attn_in['W_UQ'], 'L1_attn_b_UQ': _L1_attn_in['b_UQ'], 'L1_attn_W_DKV': _L1_attn_in['W_DKV'], 'L1_attn_b_DKV': _L1_attn_in['b_DKV'], 'L1_attn_W_UK': _L1_attn_in['W_UK'], 'L1_attn_b_UK': _L1_attn_in['b_UK'], 'L1_attn_W_UV': _L1_attn_in['W_UV'], 'L1_attn_b_UV': _L1_attn_in['b_UV'], 'L1_attn_W_QR': _L1_attn_in['W_QR'], 'L1_attn_b_QR': _L1_attn_in['b_QR'], 'L1_attn_W_KR': _L1_attn_in['W_KR'], 'L1_attn_b_KR': _L1_attn_in['b_KR'], 'L1_attn_W_O': _L1_attn_in['W_O'], 'L1_attn_b_O': _L1_attn_in['b_O'], 'L1_xattn_Wq': _L1_xattn_in['Wq'], 'L1_xattn_bq': _L1_xattn_in['bq'], 'L1_xattn_Wk': _L1_xattn_in['Wk'], 'L1_xattn_bk': _L1_xattn_in['bk'], 'L1_xattn_Wv': _L1_xattn_in['Wv'], 'L1_xattn_bv': _L1_xattn_in['bv'], 'L1_xattn_Wo': _L1_xattn_in['Wo'], 'L1_xattn_bo': _L1_xattn_in['bo'], 'L1_ffn_w_gate': _L1_ffn_in['w_gate'], 'L1_ffn_w_up': _L1_ffn_in['w_up'], 'L1_ffn_w_down': _L1_ffn_in['w_down']}

def reference(x, ctx_1024, mask_BxS2_bf1, L0_attn_w_qkv, L0_attn_w_proj, L0_attn_b_proj, L0_xattn_Wq, L0_xattn_Wkv, L0_xattn_Wout, L0_ffn_Wg, L0_ffn_bias_corr, L0_ffn_W1, L0_ffn_W2, L0_ffn_Ws1, L0_ffn_Ws2, L1_attn_W_DQ, L1_attn_b_DQ, L1_attn_W_UQ, L1_attn_b_UQ, L1_attn_W_DKV, L1_attn_b_DKV, L1_attn_W_UK, L1_attn_b_UK, L1_attn_W_UV, L1_attn_b_UV, L1_attn_W_QR, L1_attn_b_QR, L1_attn_W_KR, L1_attn_b_KR, L1_attn_W_O, L1_attn_b_O, L1_xattn_Wq, L1_xattn_bq, L1_xattn_Wk, L1_xattn_bk, L1_xattn_Wv, L1_xattn_bv, L1_xattn_Wo, L1_xattn_bo, L1_ffn_w_gate, L1_ffn_w_up, L1_ffn_w_down):
    import jax
    import jax.numpy as jnp

    def _L0_attn_ref(x, w_qkv, w_proj, b_proj):
        import jax, jax.numpy as jnp
        import numpy as np
        B, T, C = (2, 256, 128)
        H = 16
        HS = C // H
        b, t, c = x.shape
        hs = c // H
        qkv = jnp.einsum('btc,fc->btf', x, w_qkv)
        qkv = qkv.reshape(b, t, 3, H, hs)
        q = jnp.transpose(qkv[:, :, 0], (0, 2, 1, 3))
        k = jnp.transpose(qkv[:, :, 1], (0, 2, 1, 3))
        v = jnp.transpose(qkv[:, :, 2], (0, 2, 1, 3))
        scores = jnp.einsum('bhqd,bhkd->bhqk', q, k) * hs ** (-0.5)
        p = jax.nn.softplus(scores)
        p = p * p
        causal = jnp.tril(jnp.ones((t, t), dtype=p.dtype))
        p = p * causal
        attn = p / (jnp.sum(p, axis=-1, keepdims=True) + 1e-09)
        out = jnp.einsum('bhqk,bhkd->bhqd', attn, v)
        out = jnp.transpose(out, (0, 2, 1, 3)).reshape(b, t, c)
        return jnp.einsum('btc,oc->bto', out, w_proj) + b_proj

    def _L0_xattn_ref(q_x, kv_x, mask, Wq, Wkv, Wout):
        import math
        import jax, jax.numpy as jnp
        import numpy as np
        DIM = 128
        HEADS = 16
        DIM_HEAD = DIM // HEADS
        SCALE = DIM_HEAD ** (-0.5)

        def _apply_rotary_emb(x, seq_len):
            pos = jnp.arange(seq_len, dtype=jnp.float32)[:, None]
            div = jnp.exp(jnp.arange(0, DIM_HEAD, 2, dtype=jnp.float32) * (-math.log(10000.0) / DIM_HEAD))
            freqs = pos * div
            emb = jnp.concatenate([freqs, freqs], axis=-1)[None, None].astype(x.dtype)
            x1, x2 = (x[..., :DIM_HEAD // 2], x[..., DIM_HEAD // 2:])
            x_rot = jnp.concatenate([-x2, x1], axis=-1)
            return x * jnp.cos(emb) + x_rot * jnp.sin(emb)
        b, n_q, _ = q_x.shape
        _, n_kv, _ = kv_x.shape
        q = (q_x @ Wq).reshape(b, n_q, HEADS, DIM_HEAD).transpose(0, 2, 1, 3)
        kv = kv_x @ Wkv
        k, v = jnp.split(kv, 2, axis=-1)
        k = k.reshape(b, n_kv, HEADS, DIM_HEAD).transpose(0, 2, 1, 3)
        v = v.reshape(b, n_kv, HEADS, DIM_HEAD).transpose(0, 2, 1, 3)
        q = _apply_rotary_emb(q, n_q)
        k = _apply_rotary_emb(k, n_kv)
        dots = jnp.einsum('bhqd,bhkd->bhqk', q, k) * SCALE
        neg = jnp.finfo(dots.dtype).min
        dots = jnp.where(mask[:, None, None, :], dots, neg)
        attn = jax.nn.softmax(dots, axis=-1)
        out = jnp.einsum('bhqk,bhkd->bhqd', attn, v)
        out = out.transpose(0, 2, 1, 3).reshape(b, n_q, DIM)
        return out @ Wout

    def _L0_ffn_ref(hidden_states, Wg, bias_corr, W1, W2, Ws1, Ws2):
        import jax, jax.numpy as jnp
        import numpy as np
        H = 128
        I = 64
        IS = 128
        E = 16
        G = 4
        TOPK_G = 2
        TOPK = 4
        SCALE = 2.5
        B, S = (2, 128)

        def _relu2(x):
            r = jax.nn.relu(x)
            return r * r

        def _route(scores, bias_corr):
            T = scores.shape[0]
            s_choice = scores + bias_corr
            gs = s_choice.reshape(T, G, E // G)
            group_scores = jnp.sum(jax.lax.top_k(gs, 2)[0], axis=-1)
            gidx = jax.lax.top_k(group_scores, TOPK_G)[1]
            gmask = jnp.sum(jax.nn.one_hot(gidx, G, dtype=scores.dtype), axis=1)
            smask = jnp.repeat(gmask, E // G, axis=1)
            masked = jnp.where(smask > 0, s_choice, 0.0)
            topk_idx = jax.lax.top_k(masked, TOPK)[1]
            topk_w = jnp.take_along_axis(scores, topk_idx, axis=1)
            topk_w = topk_w / (jnp.sum(topk_w, axis=-1, keepdims=True) + 1e-20)
            topk_w = topk_w * SCALE
            return (topk_idx, topk_w)
        b, s, h = hidden_states.shape
        flat = hidden_states.reshape(-1, h)
        T = flat.shape[0]
        logits = flat.astype(jnp.float32) @ Wg.T
        scores = jax.nn.sigmoid(logits)
        topk_idx, topk_w = _route(scores, bias_corr)
        topk_w = topk_w.astype(hidden_states.dtype)
        cw = jnp.zeros((T, E), flat.dtype)
        cw = cw.at[jnp.arange(T)[:, None], topk_idx].add(topk_w)
        hid = _relu2(jnp.einsum('th,eih->eti', flat, W1))
        y = jnp.einsum('eti,ehi->eth', hid, W2)
        out = jnp.einsum('eth,te->th', y, cw)
        shared = _relu2(flat @ Ws1.T) @ Ws2.T
        return (out + shared).reshape(b, s, h)

    def _L1_attn_ref(h_t, W_DQ, b_DQ, W_UQ, b_UQ, W_DKV, b_DKV, W_UK, b_UK, W_UV, b_UV, W_QR, b_QR, W_KR, b_KR, W_O, b_O):
        import jax, jax.numpy as jnp
        import numpy as np
        import math
        D_MODEL, N_HEADS, D_K, D_C, D_HR = (128, 8, 128, 32, 32)
        B, S = (4, 256)
        b, s, _ = h_t.shape
        c_q = h_t @ W_DQ + b_DQ
        c_kv = h_t @ W_DKV + b_DKV
        q_c = (c_q @ W_UQ + b_UQ).reshape(b, s, N_HEADS, D_K).transpose(0, 2, 1, 3)
        k_c = (c_kv @ W_UK + b_UK).reshape(b, s, N_HEADS, D_K).transpose(0, 2, 1, 3)
        v_c = (c_kv @ W_UV + b_UV).reshape(b, s, N_HEADS, D_K).transpose(0, 2, 1, 3)
        q_r = (c_q @ W_QR + b_QR).reshape(b, s, N_HEADS, D_HR).transpose(0, 2, 1, 3)
        k_r = (h_t @ W_KR + b_KR)[:, None, :, :]
        k_r = jnp.broadcast_to(k_r, (b, N_HEADS, s, D_HR))
        q = jnp.concatenate([q_c, q_r], axis=-1)
        k = jnp.concatenate([k_c, k_r], axis=-1)
        scale = 1.0 / math.sqrt(D_K + D_HR)
        scores = jnp.einsum('bhsd,bhtd->bhst', q, k) * scale
        attn = jax.nn.softmax(scores, axis=-1)
        o = jnp.einsum('bhst,bhtd->bhsd', attn, v_c)
        o = o.transpose(0, 2, 1, 3).reshape(b, s, N_HEADS * D_K)
        return o @ W_O + b_O

    def _L1_xattn_ref(query, key, value, Wq, bq, Wk, bk, Wv, bv, Wo, bo):
        import jax, jax.numpy as jnp
        import numpy as np
        D_MODEL = 128
        NUM_HEADS = 16
        HEAD_DIM = D_MODEL // NUM_HEADS
        MAX_SEQ = 64

        def rope_tables(seq_len, dim):
            inv_freq = 1.0 / 10000.0 ** (jnp.arange(0, dim, 2, dtype=jnp.float32) / dim)
            t = jnp.arange(seq_len, dtype=jnp.float32)
            freqs = jnp.einsum('i,j->ij', t, inv_freq)
            emb = jnp.concatenate([freqs, freqs], axis=-1)
            return (jnp.cos(emb), jnp.sin(emb))

        def rotate_half(x):
            x1, x2 = jnp.split(x, 2, axis=-1)
            return jnp.concatenate([-x2, x1], axis=-1)
        B, S, D = query.shape
        H, Hd = (NUM_HEADS, HEAD_DIM)
        scale = Hd ** (-0.5)

        def proj(x, W, b):
            y = jnp.einsum('bsd,ed->bse', x, W) + b
            return y.reshape(B, S, H, Hd).transpose(0, 2, 1, 3)
        q = proj(query, Wq, bq)
        k = proj(key, Wk, bk)
        v = proj(value, Wv, bv)
        cos, sin = rope_tables(S, Hd)
        cos = cos[None, None]
        sin = sin[None, None]
        q = q * cos + rotate_half(q) * sin
        k = k * cos + rotate_half(k) * sin
        attn = jnp.einsum('bhqd,bhkd->bhqk', q, k) * scale
        attn_w = jax.nn.softmax(attn, axis=-1)
        out = jnp.einsum('bhqk,bhkd->bhqd', attn_w, v)
        out = out.transpose(0, 2, 1, 3).reshape(B, S, D)
        out = jnp.einsum('bsd,ed->bse', out, Wo) + bo
        return out

    def _L1_ffn_ref(x, w_gate, w_up, w_down):
        import jax, jax.numpy as jnp
        import numpy as np
        BLOCK = 32
        W_BITS = 4
        ACT_BITS = 16

        def act_qdq(x):
            qmax = 2.0 ** (ACT_BITS - 1) - 1.0
            scale = jnp.maximum(jnp.max(jnp.abs(x)) / qmax, 1e-12)
            return jnp.clip(jnp.round(x / scale), -qmax - 1.0, qmax) * scale

        def fixed_qdq_u16(x):
            scale = 1.0 / 65536.0
            return jnp.clip(jnp.round(x / scale), 0.0, 65535.0) * scale

        def lpbq_dequant(w):
            O, I = w.shape
            qmax = 2.0 ** (W_BITS - 1) - 1.0
            wb = w.reshape(O, I // BLOCK, BLOCK)
            s = jnp.maximum(jnp.max(jnp.abs(wb), axis=-1, keepdims=True) / qmax, 1e-12)
            wq = jnp.clip(jnp.round(wb / s), -qmax - 1.0, qmax) * s
            return wq.reshape(O, I)
        x = act_qdq(x)
        up = act_qdq(x @ lpbq_dequant(w_up).T)
        gate = act_qdq(x @ lpbq_dequant(w_gate).T)
        sig = fixed_qdq_u16(jax.nn.sigmoid(gate))
        gate = act_qdq(gate * sig)
        o = act_qdq(gate * up)
        return o @ lpbq_dequant(w_down).T
    x = _layernorm(x + _L0_attn_ref(x, L0_attn_w_qkv, L0_attn_w_proj, L0_attn_b_proj), axis=-1)
    x = _layernorm(x + _L0_xattn_ref(x, ctx_1024, mask_BxS2_bf1, L0_xattn_Wq, L0_xattn_Wkv, L0_xattn_Wout), axis=-1)
    x = _layernorm(x + _L0_ffn_ref(x, L0_ffn_Wg, L0_ffn_bias_corr, L0_ffn_W1, L0_ffn_W2, L0_ffn_Ws1, L0_ffn_Ws2), axis=-1)
    x = _layernorm(x + _L1_attn_ref(x, L1_attn_W_DQ, L1_attn_b_DQ, L1_attn_W_UQ, L1_attn_b_UQ, L1_attn_W_DKV, L1_attn_b_DKV, L1_attn_W_UK, L1_attn_b_UK, L1_attn_W_UV, L1_attn_b_UV, L1_attn_W_QR, L1_attn_b_QR, L1_attn_W_KR, L1_attn_b_KR, L1_attn_W_O, L1_attn_b_O), axis=-1)
    x = _layernorm(x + _L1_xattn_ref(x, ctx_1024, ctx_1024, L1_xattn_Wq, L1_xattn_bq, L1_xattn_Wk, L1_xattn_bk, L1_xattn_Wv, L1_xattn_bv, L1_xattn_Wo, L1_xattn_bo), axis=-1)
    x = _layernorm(x + _L1_ffn_ref(x, L1_ffn_w_gate, L1_ffn_w_up, L1_ffn_w_down), axis=-1)
    return x

_drawn_inputs = setup_inputs


def setup_inputs(seed=0):
    import zlib

    import numpy as np

    out = dict(_drawn_inputs(seed))
    spreads = {'L0_attn_b_proj': (0.0, 0.1),
     'L1_xattn_bq': (0.0, 0.395),
     'L1_xattn_bk': (0.0, 0.797),
     'L1_xattn_bv': (0.0, 0.1),
     'L1_xattn_bo': (0.0, 0.1)}
    factors = {'L0_ffn_Wg': 5.878,
     'L0_ffn_bias_corr': 8.0,
     'L0_ffn_W1': 5.589,
     'L0_ffn_W2': 5.028,
     'L0_ffn_Ws1': 4.929,
     'L0_ffn_Ws2': 4.426,
     'L1_attn_W_DQ': 8.0,
     'L1_attn_b_DQ': 8.0,
     'L1_attn_W_UQ': 8.0,
     'L1_attn_b_UQ': 8.0,
     'L1_attn_b_DKV': 4.793,
     'L1_attn_W_UK': 8.0,
     'L1_attn_b_UK': 8.0,
     'L1_attn_W_QR': 8.0,
     'L1_attn_b_QR': 8.0,
     'L1_attn_W_KR': 8.0,
     'L1_attn_b_KR': 8.0,
     'L1_attn_b_O': 3.379,
     'L1_ffn_w_gate': 5.376,
     'L1_ffn_w_up': 5.209,
     'L1_ffn_w_down': 5.252}
    for name, (base, spread) in spreads.items():
        noise = np.random.default_rng([zlib.crc32(name.encode()), seed]).standard_normal(out[name].shape)
        drawn = base * np.exp(spread * noise) if base else spread * noise
        out[name] = jnp.asarray(drawn.astype(out[name].dtype))
    for name, factor in factors.items():
        out[name] = (out[name] * factor).astype(out[name].dtype)
    return out
```

```python
from contextlib import ExitStack

import concourse.bass as bass
from concourse import mybir

F32 = mybir.dt.float32
BF16 = mybir.dt.bfloat16
U8 = mybir.dt.uint8
ALU = mybir.AluOpType
ACT = mybir.ActivationFunctionType
AX = mybir.AxisListType

P = 128
D = 128
T = 64
NSEQ = 32
NT = NSEQ * T // P
SB = P // T
HD = 8
NI = 4
EPS = 1e-5
SMALL_SCALE = HD ** -0.5
BIG = 3.3895313892515355e38

PHASES = 4
PEEL = 5
SLOTS = NT + PHASES - 1
PAIRS = (SLOTS - PEEL) // 2 - 2


def run_slots(eng, slot):
    for s in range(PEEL):
        slot(s, s % 2)
    with eng.Fori(0, PAIRS) as i:
        for j in range(2):
            slot(i * 2 + (PEEL + j), (PEEL + j) % 2)
    for s in range(PEEL + 2 * PAIRS, SLOTS):
        slot(s, s % 2)


def has(s, phase):
    return not isinstance(s, int) or 0 <= s - phase < NT


def wait(eng, sem, value):
    if not isinstance(value, int) or value > 0:
        eng.wait_ge(sem, value)


class Names:
    pass


class Stages:

    def __init__(self, nc):
        self.nc, self.last, self.spent = nc, [], []

    def semaphores(self, prefix, names):
        for h in self.spent:
            self.nc.release_semaphore(h)
        self.spent = self.last
        self.last = [self.nc.alloc_semaphore(prefix + n) for n in names.split()]
        return dict(zip(names.split(), self.last))

    def zero_spent(self, pool):
        nums = sorted(h.num for h in self.spent)
        while nums:
            run = 1
            while run < len(nums) and nums[run] == nums[0] + run:
                run += 1
            pool.sem_clear(range(nums[0], nums[0] + run))
            nums = nums[run:]



def norm_statistics(dve, nc, m, s, t, par, y):
    wait(dve, s["xb_ready"], t + 1)
    wait(dve, s["y_psum"], t + 1)
    wait(dve, s["x_new"], t)
    nc.vector.tensor_tensor(m.r[:, :], y, m.xb[:, par, :], ALU.add).then_inc(s["r_done"], 1)
    dve.wait_ge(s["r_done"], t + 1)
    nc.vector.bn_stats(m.bn6[:, :], m.r[:, :]).then_inc(s["bn6_done"], 1)
    dve.wait_ge(s["bn6_done"], 1)
    dve.wait_ge(s["bn6_done"], t + 1)
    nc.vector.bn_aggr(m.meanvar[:, :], m.bn6[:, :]).then_inc(s["var_ready"], 1)


def norm_rstd(act, nc, m, s, t):
    act.wait_ge(s["var_ready"], t + 1)
    nc.scalar.activation(m.lnvar[:, :], m.meanvar[:, 1:2], ACT.Ln, bias=m.eps[:, 0:1]).then_inc(s["lnvar_done"], 1)
    act.wait_ge(s["lnvar_done"], t + 1)
    nc.scalar.activation(m.rstd[:, :], m.lnvar[:, :], ACT.Exp, scale=-0.5).then_inc(s["rstd_ready"], 1)


def norm_apply(dve, nc, m, s, t):
    dve.wait_ge(s["rstd_ready"], t + 1)
    nc.vector.tensor_scalar(m.X[:, t, :], m.r[:, :], m.meanvar[:, 0:1], m.rstd[:, 0:1],
                            ALU.subtract, ALU.mult).then_inc(s["x_new"], 1)



def small_attention(nc, m, w, kind, prefix):
    causal = kind == "causal"
    with ExitStack() as ctx:
        s = m.stages.semaphores(prefix,
                       "kv_load0 kv_load1 x_copied xb_ready xT_psum xT_ready qk_psum qk_ready v_psum rope_parts"
                       " qk_sum q_exp k_exp v_ready s_psum max_done shifted clamped exp_done ln_done soft_done"
                       " prob_ready pT_psum pT_ready o_psum den_done rden_done o_ready oT_psum oT_ready"
                       " y_psum r_done bn6_done var_ready lnvar_done rstd_ready x_new")
        def sb(name, shape, dt=F32):
            return ctx.enter_context(nc.sbuf_tensor(prefix + name, shape, dt))

        m.rope = sb("rope", [P, 2, 2, 2, P])
        m.stat = sb("stat", [P, 2, SB, 4, T])
        m.mov = sb("mov", [P, 2, SB, NI, T])
        m.prob = sb("prob", [P, 2, SB, NI, 2, T])
        m.probT = sb("probT", [P, SB, NI, P])
        m.soft = sb("soft", [P, SB, 512])
        m.score = sb("score", [P, SB, 512])
        kv_load = [s["kv_load0"], s["kv_load1"]]
        psS = [m.bank[0], m.bank[1]]
        psT = [m.bank[2], m.bank[3]]
        psQK, psXV, psO, psOY = m.bank[4], m.bank[5], m.bank[6], m.bank[7]
        psY = psOY[:, 256:384]
        block = ctx.enter_context(nc.Block())

        if not causal:
            @block.sync
            def _(sp):
                def load(t, par):
                    wait(sp, s["v_psum"], t - 1)
                    for a in range(2):
                        sp.dma_start(m.kvT[:, par, :, a, :], m.ctxT_dram[:, bass.ds(t * SB, SB), :]).then_inc(kv_load[par], 16)
                load(0, 0)
                load(1, 1)
                load(2, 0)
                load(3, 1)
                with sp.Fori(2, NT // 2) as i:
                    load(i * 2, 0)
                    load(i * 2 + 1, 1)

        @block.gpsimd
        def _(pool):
            m.stages.zero_spent(pool)

            def slot(at, cur):
                if has(at, 0):
                    t, par = at, cur
                    wait(pool, s["xT_psum"], t - 1)
                    nc.gpsimd.tensor_copy(m.xs[:, par, :], m.X[:, t, :]).then_inc(s["x_copied"], 1)
                if has(at, 2):
                    t, par = at - 2, cur
                    wait(pool, s["r_done"], t - 1)
                    nc.gpsimd.tensor_tensor(m.xb[:, par, :], m.X[:, t, :], w.bias_tile, ALU.add).then_inc(s["xb_ready"], 1)
                if has(at, 0):
                    t, par = at, cur
                    if causal:
                        pool.wait_ge(s["qk_ready"], t + 1)
                    else:
                        pool.wait_ge(s["rope_parts"], t + 1)
                        nc.gpsimd.tensor_tensor(m.qk[:, par, :, :], m.rope[:, par, :, 0, :], m.rope[:, par, :, 1, :],
                                                ALU.add).then_inc(s["qk_sum"], 1)
                        pool.wait_ge(s["qk_sum"], t + 1)
                    stat, mov = (1, 0) if causal else (0, 1)
                    wait(pool, s["s_psum"], 2 * (t - 1))
                    nc.gpsimd.tensor_tensor(
                        m.stat[:, par, :, :, :],
                        m.qk[:, par, stat, :].rearrange("p (b k) -> p b k", b=SB).unsqueeze(2).broadcast_to([P, SB, 4, T]),
                        (m.mask_ca if causal else m.mask_ac).unsqueeze(1).unsqueeze(3).broadcast_to([P, SB, 4, T]), ALU.mult).then_inc(s["q_exp"], 1)
                    nc.gpsimd.tensor_tensor(
                        m.mov[:, par, :, :, :],
                        m.qk[:, par, mov, :].rearrange("p (b k) -> p b k", b=SB).unsqueeze(2).broadcast_to([P, SB, NI, T]),
                        m.mask_i.unsqueeze(1).unsqueeze(3).broadcast_to([P, SB, NI, T]), ALU.mult).then_inc(s["k_exp"], 1)
            run_slots(pool, slot)

        @block.tensor
        def _(pe):
            def scores(t, par):
                pe.wait_ge(s["q_exp"], t + 1)
                pe.wait_ge(s["k_exp"], t + 1)
                for b in range(SB):
                    wait(pe, s["shifted"], 2 * t + b - 1)
                    if not causal and w.mask_row is not None:
                        nc.tensor.matmul(psS[b][:, :], m.ones_bf[0:1, :],
                                         w.mask_row[0:1, bass.ds(t * P + b * T, T)].unsqueeze(1).broadcast_to([1, 8, T]),
                                         start=True, stop=False, skip_group_check=True)
                    for half in range(2):
                        lhsT = m.stat[:, par, b, 2 * half:2 * half + 2, :]
                        masked = not causal and w.mask_row is not None
                        mm = nc.tensor.matmul(psS[b][:, 256 * half:256 * half + 256], lhsT, m.mov[:, par, b, :, :],
                                              start=not masked, stop=True, skip_group_check=masked)
                    mm.then_inc(s["s_psum"], 1)

            def transpose_probs(t, par):
                for b in range(SB):
                    wait(pe, s["pT_ready"], 2 * t + b - 1)
                    pe.wait_ge(s["exp_done"], 2 * t + b + 1)
                    for i in range(NI):
                        mm = nc.tensor.transpose(psT[b][:, i * P:(i + 1) * P], m.prob[:, par, b, i, :, :], m.ident)
                    mm.then_inc(s["pT_psum"], 1)

            def values(t, par):
                wait(pe, s["o_ready"], t)
                pe.wait_ge(s["v_ready"], t + 1)
                for b in range(SB):
                    if causal:
                        pe.wait_ge(s["prob_ready"], 2 * t + b + 1)
                    else:
                        pe.wait_ge(s["pT_ready"], 2 * t + b + 1)
                    for i in range(NI):
                        lhsT = m.prob[:, par, b, i, :, :] if causal else m.probT[:, b, i, :]
                        at = 36 * (NI * b + i)
                        mm = nc.tensor.matmul(psO[:, at:at + 36], lhsT, m.vals[:, par, b, i, :, :, :],
                                              start=True, stop=True)
                mm.then_inc(s["o_psum"], 1)

            def slot(at, cur):
                if has(at, 1):
                    scores(at - 1, 1 - cur)
                if has(at, 3):
                    t, par = at - 3, 1 - cur
                    wait(pe, s["r_done"], t)
                    pe.wait_ge(s["o_ready"], t + 1)
                    nc.tensor.transpose(psOY[:, 0:P], m.o[:, par, :, :], m.ident).then_inc(s["oT_psum"], 1)
                if has(at, 2) and not causal:
                    transpose_probs(at - 2, cur)
                if has(at, 0):
                    t, par = at, cur
                    pe.wait_ge(s["x_copied"], t + 1)
                    wait(pe, s["v_ready"], t)
                    nc.tensor.transpose(psXV[:, 0:P], m.xs[:, par, :], m.ident).then_inc(s["xT_psum"], 1)
                if has(at, 3):
                    t = at - 3
                    pe.wait_ge(s["oT_ready"], t + 1)
                    for c in range(2):
                        mm = nc.tensor.matmul(psY, m.oT[0:T, c, :], w.wo[:, c, :], start=(c == 0), stop=(c == 1))
                    mm.then_inc(s["y_psum"], 1)
                if has(at, 0):
                    t, par = at, cur
                    pe.wait_ge(s["xT_ready"], t + 1)
                    if causal:
                        wait(pe, s["qk_ready"], t)
                        nc.tensor.matmul(psQK[:, 0:128], w.wq, m.xT[:, par, :, 0, :], start=True, stop=True)
                        nc.tensor.matmul(psQK[:, 128:256], w.wk, m.xT[:, par, :, 0, :], start=True, stop=True).then_inc(s["qk_psum"], 1)
                        kvT = m.xT[:, par, :, :, :]
                    else:
                        wait(pe, s["rope_parts"], t)
                        wait(pe, kv_load[par], 16 * (t - par) + 32)
                        kvT = m.kvT[:, par, :, :, :]
                        nc.tensor.matmul(psQK[:, 0:128], w.wq, m.xT[:, par, :, 0, :], start=True, stop=True)
                        nc.tensor.matmul(psQK[:, 128:256], w.wqr, m.xT[:, par, :, 0, :], start=True, stop=True)
                        nc.tensor.matmul(psQK[:, 256:384], w.wk, kvT[:, :, 0, :], start=True, stop=True)
                        nc.tensor.matmul(psQK[:, 384:512], w.wkr, kvT[:, :, 0, :], start=True, stop=True).then_inc(s["qk_psum"], 1)
                if has(at, 2):
                    values(at - 2, cur)
                if has(at, 0):
                    for b in range(SB):
                        mm = nc.tensor.matmul(psXV[:, 256 + b * P:256 + (b + 1) * P], kvT[:, b, :, :], w.wv, start=True, stop=True)
                    mm.then_inc(s["v_psum"], 1)
            run_slots(pe, slot)

        @block.scalar
        def _(act):
            act.preload_act_table_set("natural_log_exp_and_others")

            def slot(at, cur):
                if has(at, 3):
                    t = at - 3
                    act.wait_ge(s["oT_psum"], t + 1)
                    wait(act, s["y_psum"], t)
                    for b in range(SB):
                        op = nc.scalar.activation(m.oT[0:T, :, b * T:(b + 1) * T],
                                                  psOY[b * T:(b + 1) * T, 0:P].rearrange("p (c q) -> p c q", c=2), ACT.Copy)
                    op.then_inc(s["oT_ready"], 1)
                if has(at, 2) and not causal:
                    t = at - 2
                    wait(act, s["o_psum"], t)
                    for b in range(SB):
                        act.wait_ge(s["pT_psum"], 2 * t + b + 1)
                        nc.scalar.activation(m.probT[:, b, :, :].rearrange("p i q -> p (i q)"), psT[b][:, :],
                                             ACT.Copy).then_inc(s["pT_ready"], 1)
                if has(at, 0):
                    t, par = at, cur
                    act.wait_ge(s["xT_psum"], t + 1)
                    wait(act, s["v_psum"], t - 1)
                    nc.scalar.activation(m.xT[:, par, :, :, :],
                                         psXV[:, 0:P].rearrange("p (b k) -> p b k", b=SB).unsqueeze(2).broadcast_to([P, SB, 2, T]),
                                         ACT.Copy).then_inc(s["xT_ready"], 1)
                if has(at, 1):
                    t, par = at - 1, 1 - cur
                    for b in range(SB):
                        sc = m.prob[:, par, b, :, :, :].rearrange("p i a k -> p (i a k)")
                        if causal:
                            act.wait_ge(s["clamped"], 2 * t + b + 1)
                            nc.scalar.activation(m.soft[:, b, :], m.soft[:, b, :], ACT.Exp).then_inc(s["exp_done"], 1)
                            act.wait_ge(s["exp_done"], 2 * t + b + 1)
                            nc.scalar.activation(m.soft[:, b, :], m.soft[:, b, :], ACT.Ln, bias=m.one[:, 0:1]).then_inc(s["ln_done"], 1)
                        else:
                            act.wait_ge(s["shifted"], 2 * t + b + 1)
                            nc.scalar.activation(sc, sc, ACT.Exp, scale=SMALL_SCALE).then_inc(s["exp_done"], 1)
                if causal and has(at, 0):
                    t, par = at, cur
                    act.wait_ge(s["qk_psum"], t + 1)
                    wait(act, s["k_exp"], t - 1)
                    nc.scalar.activation(m.qk[:, par, :, :], psQK[:, 0:256].rearrange("p (x t) -> p x t", x=2),
                                         ACT.Copy).then_inc(s["qk_ready"], 1)
                if has(at, 3):
                    norm_rstd(act, nc, m, s, at - 3)
                if causal and has(at, 1):
                    t, par = at - 1, 1 - cur
                    wait(act, s["o_psum"], t - 1)
                    for b in range(SB):
                        act.wait_ge(s["soft_done"], 2 * t + b + 1)
                        nc.scalar.activation(m.prob[:, par, b, :, :, :].rearrange("p i c q -> p c i q"),
                                             m.soft[:, b, :].rearrange("p (c i q) -> p c i q", c=2, i=NI), ACT.Square).then_inc(s["prob_ready"], 1)
                if has(at, 0):
                    t, par = at, cur
                    act.wait_ge(s["v_psum"], t + 1)
                    wait(act, s["o_psum"], t - 1)
                    for a in range(2):
                        half = slice(a * T, a * T + T)
                        op = nc.scalar.activation(
                            m.vals[half, par, :, :, a, :, 0:HD].rearrange("p b i c d -> p (b i) c d"),
                            psXV[half, 256:512].rearrange("p (bi a c d) -> p bi a c d", a=2, c=2, d=HD)[:, :, a, :, :],
                            ACT.Copy)
                    op.then_inc(s["v_ready"], 1)
            run_slots(act, slot)

        @block.vector
        def _(dve):
            def slot(at, cur):
                if has(at, 1):
                    t, par = at - 1, 1 - cur
                    for b in range(SB):
                        n = 2 * t + b
                        ps = psS[b][:, :].rearrange("p (x k) -> p x k", k=T)
                        dve.wait_ge(s["s_psum"], n + 1)
                        if causal:
                            sc = m.score[:, b, :].rearrange("p (x k) -> p x k", k=T)
                            wait(dve, s["soft_done"], n - 1)
                            nc.vector.scalar_tensor_tensor(
                                out=sc, in0=ps, scalar=SMALL_SCALE, in1=m.causal.unsqueeze(1).broadcast_to([P, 8, T]),
                                op0=ALU.mult, op1=ALU.add).then_inc(s["shifted"], 1)
                            dve.wait_ge(s["shifted"], n + 1)
                            wait(dve, s["prob_ready"], n - 1)
                            nc.vector.tensor_scalar(m.soft[:, b, :], m.score[:, b, :], 40.0, None,
                                                    ALU.min).then_inc(s["clamped"], 1)
                        else:
                            wait(dve, s["pT_psum"], 2 * (t - 1))
                            wait(dve, s["shifted"], n - 1)
                            nc.vector.tensor_reduce(m.rowmax[:, b, :], ps, AX.X, ALU.max).then_inc(s["max_done"], 1)
                            dve.wait_ge(s["max_done"], n + 1)
                            nc.vector.tensor_tensor(m.prob[:, par, b, :, :, :].rearrange("p i a k -> p a i k"),
                                                    ps.rearrange("p (a i) k -> p a i k", a=2),
                                                    m.rowmax[:, b, :].rearrange("p (a i) -> p a i", a=2).unsqueeze(3)
                                                    .broadcast_to([P, 2, NI, T]),
                                                    ALU.subtract).then_inc(s["shifted"], 1)
                if has(at, 3):
                    norm_statistics(dve, nc, m, s, at - 3, 1 - cur, psY)
                if causal and has(at, 1):
                    t, par = at - 1, 1 - cur
                    for b in range(SB):
                        n = 2 * t + b
                        dve.wait_ge(s["ln_done"], n + 1)
                        nc.vector.tensor_tensor(m.soft[:, b, :], m.soft[:, b, :], m.score[:, b, :], ALU.max).then_inc(s["soft_done"], 1)
                if not causal and has(at, 0):
                    t, par = at, cur
                    dve.wait_ge(s["qk_psum"], t + 1)
                    wait(dve, s["qk_sum"], t - 1)
                    for n, (bias, table) in enumerate(((w.bq, m.cos), (w.bqr, m.sin), (w.bk, m.cos), (w.bkr, m.sin))):
                        op = nc.vector.scalar_tensor_tensor(
                            out=m.rope[:, par, n // 2, n % 2, :].rearrange("p (b t) -> p b t", b=SB),
                            in0=psQK[:, n * P:(n + 1) * P].rearrange("p (b t) -> p b t", b=SB),
                            scalar=bias, in1=table.unsqueeze(1).broadcast_to([P, SB, T]), op0=ALU.add, op1=ALU.mult)
                    op.then_inc(s["rope_parts"], 1)
                if has(at, 2):
                    t, par = at - 2, cur
                    dve.wait_ge(s["o_psum"], t + 1)
                    wait(dve, s["o_ready"], t)
                    o = psO[:, 0:288].rearrange("p (bia c e) -> p bia c e", c=2, e=HD + 1)
                    for c in range(2):
                        half = slice(c * T, c * T + T)
                        if causal:
                            op = nc.vector.tensor_scalar(m.den[half, :], o[half, :, c, HD], 1e-9, None, ALU.add)
                        else:
                            op = nc.vector.reciprocal(m.rden[half, :], o[half, :, c, HD])
                    if causal:
                        op.then_inc(s["den_done"], 1)
                        dve.wait_ge(s["den_done"], t + 1)
                        op = nc.vector.reciprocal(m.rden[:, :], m.den[:, :])
                    op.then_inc(s["rden_done"], 1)
                    dve.wait_ge(s["rden_done"], t + 1)
                    wait(dve, s["oT_psum"], t - 1)
                    for c in range(2):
                        half = slice(c * T, c * T + T)
                        op = nc.vector.tensor_tensor(
                            m.o[half, par, :, :].rearrange("p b (ia d) -> p (b ia) d", d=HD), o[half, :, c, 0:HD],
                            m.rden[half, :].unsqueeze(2).broadcast_to([T, 16, HD]), ALU.mult)
                    op.then_inc(s["o_ready"], 1)
                if has(at, 3):
                    norm_apply(dve, nc, m, s, at - 3)
            run_slots(dve, slot)



LH, LC, LR = 8, 32, 32
LF = LC + LR + 1
LATENT_SCALE = (D + LR) ** -0.5


def latent_attention(nc, m, w, prefix):
    with ExitStack() as ctx:
        s = m.stages.semaphores(prefix,
                       "x_copied xb_ready xT_psum xT_ready low_psum q_ready f_ready v_ready g_psum g_ready"
                       " s_psum max_done shifted exp_done pT_psum pT_ready o_psum rden_done o_ready oT_psum"
                       " oT_ready y_psum r_done bn6_done var_ready lnvar_done rstd_ready x_new")
        psS = [m.bank[0], m.bank[1]]
        psG = [m.bank[2], m.bank[3]]
        psT, psXV, psO, psOY = m.bank[4], m.bank[5], m.bank[6], m.bank[7]
        psY = psOY[:, 256:384]
        block = ctx.enter_context(nc.Block())

        @block.gpsimd
        def _(pool):
            m.stages.zero_spent(pool)

            def slot(at, cur):
                if has(at, 0):
                    t, par = at, cur
                    wait(pool, s["xT_psum"], t - 1)
                    nc.gpsimd.tensor_copy(m.xs[:, par, :], m.X[:, t, :]).then_inc(s["x_copied"], 1)
                if has(at, 2):
                    t, par = at - 2, cur
                    wait(pool, s["r_done"], t - 1)
                    nc.gpsimd.tensor_tensor(m.xb[:, par, :], m.X[:, t, :], w.bias_tile, ALU.add).then_inc(s["xb_ready"], 1)
            run_slots(pool, slot)

        @block.tensor
        def _(pe):
            def slot(at, cur):
                if has(at, 1):
                    t, par = at - 1, 1 - cur
                    pe.wait_ge(s["g_ready"], 2 * t + 2)
                    wait(pe, s["shifted"], t - 1)
                    for b in range(SB):
                        for ia in range(4):
                            mm = nc.tensor.matmul(psS[par][:, (4 * b + ia) * T:(4 * b + ia + 1) * T],
                                                  m.g[:, par, b, 2 * ia:2 * ia + 2, :], m.f[:, par, b * T:(b + 1) * T],
                                                  start=True, stop=True)
                    mm.then_inc(s["s_psum"], 1)
                if has(at, 3):
                    t, par = at - 3, 1 - cur
                    wait(pe, s["r_done"], t)
                    pe.wait_ge(s["o_ready"], t + 1)
                    for b in range(SB):
                        mm = nc.tensor.transpose(psOY[:, b * P:(b + 1) * P], m.lo[:, par, b, :], m.ident)
                    mm.then_inc(s["oT_psum"], 1)
                if has(at, 2):
                    t, par = at - 2, cur
                    wait(pe, s["pT_ready"], t)
                    pe.wait_ge(s["exp_done"], t + 1)
                    for b in range(SB):
                        for i in range(2):
                            mm = nc.tensor.transpose(psT[:, (2 * b + i) * P:(2 * b + i + 1) * P],
                                                     m.lprob[:, par, b, i, :], m.ident)
                    mm.then_inc(s["pT_psum"], 1)
                if has(at, 0):
                    t, par = at, cur
                    pe.wait_ge(s["x_copied"], t + 1)
                    wait(pe, s["v_ready"], t)
                    nc.tensor.transpose(psXV[:, 0:P], m.xs[:, par, :], m.ident).then_inc(s["xT_psum"], 1)
                if has(at, 3):
                    t = at - 3
                    pe.wait_ge(s["oT_ready"], t + 1)
                    for c in range(2):
                        mm = nc.tensor.matmul(psY, m.oT[:, c, :], w.out[:, c, :], start=(c == 0), stop=(c == 1))
                    mm.then_inc(s["y_psum"], 1)
                if has(at, 0):
                    t, par = at, cur
                    pe.wait_ge(s["xT_ready"], t + 1)
                    xT = m.xT[:, par, :, 0, :]
                    nc.tensor.matmul(psXV[0:LC, 128:256], w.dq, xT, start=True, stop=True)
                    nc.tensor.matmul(psXV[0:LC + LR, 256:384], w.df, xT, start=True, stop=True)
                    for b in range(SB):
                        at_ = 384 + b * LC
                        nc.tensor.matmul(psXV[:, at_:at_ + LC], m.xT[:, par, b, :, :], w.df[:, 0:LC], start=True, stop=False)
                        mm = nc.tensor.matmul(psXV[:, at_:at_ + LC], m.ones_row[0:1, :], w.b_latent, start=False, stop=True)
                    mm.then_inc(s["low_psum"], 1)
                if has(at, 2):
                    t, par = at - 2, cur
                    wait(pe, s["o_ready"], t)
                    pe.wait_ge(s["pT_ready"], t + 1)
                    for b in range(SB):
                        for i in range(2):
                            n = 2 * b + i
                            mm = nc.tensor.matmul(psO[:, n * 66:(n + 1) * 66], m.lprobT[:, n * P:(n + 1) * P],
                                                  m.lvals[:, par, b, :, :], start=True, stop=True)
                    mm.then_inc(s["o_psum"], 1)
                if has(at, 0):
                    t, par = at, cur
                    pe.wait_ge(s["q_ready"], t + 1)
                    for half in range(2):
                        wait(pe, s["g_ready"], 2 * t + half - 1)
                        for h in range(4):
                            mm = nc.tensor.matmul(psG[half][0:LF, h * P:(h + 1) * P], w.score[:, 4 * half + h, :],
                                                  m.cq[:, par, :], start=True, stop=True)
                        mm.then_inc(s["g_psum"], 1)
            run_slots(pe, slot)

        @block.scalar
        def _(act):
            act.preload_act_table_set("natural_log_exp_and_others")

            def slot(at, cur):
                if has(at, 3):
                    t = at - 3
                    act.wait_ge(s["oT_psum"], t + 1)
                    wait(act, s["y_psum"], t)
                    nc.scalar.activation(m.oT[:, :, :].rearrange("p c (b q) -> p c b q", b=SB),
                                         psOY[:, 0:256].rearrange("p (b c q) -> p c b q", b=SB, c=2),
                                         ACT.Copy).then_inc(s["oT_ready"], 1)
                if has(at, 0):
                    t, par = at, cur
                    act.wait_ge(s["xT_psum"], t + 1)
                    wait(act, s["low_psum"], t - 1)
                    nc.scalar.activation(m.xT[:, par, :, :, :],
                                         psXV[:, 0:P].rearrange("p (b k) -> p b k", b=SB).unsqueeze(2).broadcast_to([P, SB, 2, T]),
                                         ACT.Copy).then_inc(s["xT_ready"], 1)
                if has(at, 1):
                    t, par = at - 1, 1 - cur
                    act.wait_ge(s["shifted"], t + 1)
                    sc = m.lprob[:, par, :, :, :].rearrange("p b i k -> p (b i k)")
                    nc.scalar.activation(sc, sc, ACT.Exp, scale=LATENT_SCALE).then_inc(s["exp_done"], 1)
                if has(at, 0):
                    t, par = at, cur
                    act.wait_ge(s["low_psum"], t + 1)
                    wait(act, s["g_psum"], 2 * (t - 1))
                    nc.scalar.activation(m.cq[0:LC, par, :], psXV[0:LC, 128:256], ACT.Identity,
                                         bias=w.b_q).then_inc(s["q_ready"], 1)
                    wait(act, s["s_psum"], t - 1)
                    nc.scalar.activation(m.f[0:LC + LR, par, :], psXV[0:LC + LR, 256:384], ACT.Identity,
                                         bias=w.b_f).then_inc(s["f_ready"], 1)
                    wait(act, s["o_psum"], t - 1)
                    for a in range(2):
                        half = slice(a * T, a * T + T)
                        op = nc.scalar.activation(m.lvals[half, par, :, a, 0:LC],
                                                  psXV[half, 384:448].rearrange("p (b l) -> p b l", b=SB), ACT.Copy)
                    op.then_inc(s["v_ready"], 1)
                if has(at, 3):
                    norm_rstd(act, nc, m, s, at - 3)
                if has(at, 0):
                    t, par = at, cur
                    for half in range(2):
                        act.wait_ge(s["g_psum"], 2 * t + half + 1)
                        nc.scalar.activation(m.g[:, par, :, 4 * half:4 * half + 4, :].rearrange("p b h q -> p h b q"),
                                             psG[half][0:LF, :].rearrange("p (h b q) -> p h b q", h=4, b=SB),
                                             ACT.Copy).then_inc(s["g_ready"], 1)
            run_slots(act, slot)

        @block.vector
        def _(dve):
            def slot(at, cur):
                if has(at, 1):
                    t, par = at - 1, 1 - cur
                    ps = psS[par][:, :].rearrange("p (x k) -> p x k", k=T)
                    dve.wait_ge(s["s_psum"], t + 1)
                    wait(dve, s["shifted"], t)
                    nc.vector.tensor_reduce(m.rowmax[:, 0, :], ps, AX.X, ALU.max).then_inc(s["max_done"], 1)
                    dve.wait_ge(s["max_done"], t + 1)
                    wait(dve, s["pT_psum"], t - 1)
                    nc.vector.tensor_tensor(m.lprob[:, par, :, :, :].rearrange("p b i (a k) -> p (b i a) k", k=T), ps,
                                            m.rowmax[:, 0, :].unsqueeze(2).broadcast_to([P, 8, T]),
                                            ALU.subtract).then_inc(s["shifted"], 1)
                if has(at, 3):
                    norm_statistics(dve, nc, m, s, at - 3, 1 - cur, psY)
                if has(at, 2):
                    t, par = at - 2, cur
                    dve.wait_ge(s["pT_psum"], t + 1)
                    wait(dve, s["o_psum"], t)
                    nc.vector.tensor_copy(m.lprobT[:, :], psT[:, :]).then_inc(s["pT_ready"], 1)
                if has(at, 3):
                    norm_apply(dve, nc, m, s, at - 3)
                if has(at, 2):
                    t, par = at - 2, cur
                    dve.wait_ge(s["o_psum"], t + 1)
                    o = psO[:, 0:264].rearrange("p (x e) -> p x e", e=LC + 1)
                    wait(dve, s["o_ready"], t)
                    nc.vector.reciprocal(m.rden[:, 0:8], o[:, :, LC]).then_inc(s["rden_done"], 1)
                    dve.wait_ge(s["rden_done"], t + 1)
                    wait(dve, s["oT_psum"], t - 1)
                    nc.vector.tensor_tensor(m.lo[:, par, :, :].rearrange("p b (x l) -> p (b x) l", l=LC), o[:, :, 0:LC],
                                            m.rden[:, 0:8].unsqueeze(2).broadcast_to([P, 8, LC]),
                                            ALU.mult).then_inc(s["o_ready"], 1)
            run_slots(dve, slot)



NE, NG, TOPG, TOPK = 16, 4, 2, 4
NM = NE // 2
CH = 512
NC = NSEQ * T // CH
CT = CH // P
CW = 96


class Chain:

    def __init__(self, eng, sem):
        self.eng, self.sem, self.n = eng, sem, 0

    def link(self, op):
        op.then_inc(self.sem, 1)
        self.n += 1
        self.eng.wait_ge(self.sem, self.n)


def experts(nc, m, w, prefix):
    with ExitStack() as ctx:
        s = m.stages.semaphores(prefix,
                       "xT_psum xT_ready logit_psum exp_ready route cw_ready cwT_psum cwT_ready z_psum gate_psum relu_ready"
                       " gated hid_ready y_psum r_done var_ready ln_done rstd_ready x_new")
        psX, psL, psC = m.bank[0], m.bank[1], m.bank[2]
        psZ, psW, psY = [m.bank[3], m.bank[4]], [m.bank[5], m.bank[6]], m.bank[7]
        block = ctx.enter_context(nc.Block())
        MM = NM + 1

        @block.tensor
        def _(pe):
            def turn(c):
                wait(pe, s["xT_ready"], c)
                for t in range(CT):
                    mm = nc.tensor.transpose(psX[:, t * P:(t + 1) * P], m.X[:, CT * c + t, :], m.ident)
                mm.then_inc(s["xT_psum"], 1)

            def logits(c):
                pe.wait_ge(s["xT_ready"], c + 1)
                for t in range(CT):
                    mm = nc.tensor.matmul(psL[:, t * NE:(t + 1) * NE], m.xTc[:, c % 2, t * P:(t + 1) * P], w.router,
                                          start=True, stop=True)
                mm.then_inc(s["logit_psum"], 1)

            def turn_weights(c):
                pe.wait_ge(s["cw_ready"], c + 1)
                wait(pe, s["cwT_ready"], c)
                ps = psC[:, :].bitcast(BF16)
                for t in range(CT):
                    mm = nc.tensor.transpose(ps[0:CW, t * P:(t + 1) * P], m.cw3[:, t, :], m.ident_bf[:, :])
                mm.then_inc(s["cwT_psum"], 1)

            def hidden(c, j):
                n = MM * c + j
                wait(pe, s["relu_ready"], n - 1)
                w1 = w.w1[:, j * P:(j + 1) * P] if j < NM else w.shared1
                nc.tensor.matmul(psZ[n % 2][:, :], w1, m.xTc[:, c % 2, :], start=True, stop=True).then_inc(s["z_psum"], 1)
                if j < NM:
                    g = NM * c + j
                    if j == 0:
                        pe.wait_ge(s["cwT_ready"], c + 1)
                    wait(pe, s["gated"], g - 1)
                    nc.tensor.matmul(psW[g % 2][:, :], m.spread[:, j, :], m.cwT[:, c % 2, :],
                                     start=True, stop=True).then_inc(s["gate_psum"], 1)

            def down(c, j):
                n = MM * c + j
                pe.wait_ge(s["hid_ready"], n + 1)
                if j == 0:
                    wait(pe, s["r_done"], c)
                w2 = w.w2[:, j * D:(j + 1) * D] if j < NM else w.shared2
                for t in range(CT):
                    mm = nc.tensor.matmul(psY[:, t * D:(t + 1) * D], m.hid[:, n % 2, t * P:(t + 1) * P], w2,
                                          start=(j == 0 and t == 0), stop=(j == MM - 1), skip_group_check=True)
                mm.then_inc(s["y_psum"], 1)

            turn(0)
            logits(0)
            turn_weights(0)
            for c in range(NC):
                for j in range(MM + 2):
                    if j < MM:
                        hidden(c, j)
                    if j >= 2:
                        down(c, j - 2)
                    if c + 1 < NC:
                        if j == 0:
                            turn(c + 1)
                        if j == 1:
                            logits(c + 1)
                        if j == MM:
                            turn_weights(c + 1)

        @block.scalar
        def _(act):
            act.preload_act_table_set("natural_log_exp_and_others")

            def copy_turned(c):
                act.wait_ge(s["xT_psum"], c + 1)
                wait(act, s["z_psum"], MM * (c - 1))
                nc.scalar.activation(m.xTc[:, c % 2, :], psX[:, :], ACT.Copy).then_inc(s["xT_ready"], 1)

            def exponentials(c):
                act.wait_ge(s["logit_psum"], c + 1)
                wait(act, s["cw_ready"], c)
                nc.scalar.activation(m.route_e[:, :], psL[:, 0:CT * NE], ACT.Exp, scale=-1.0).then_inc(s["exp_ready"], 1)

            def copy_weights(c):
                act.wait_ge(s["cwT_psum"], c + 1)
                wait(act, s["gate_psum"], NM * (c - 1))
                nc.scalar.activation(m.cwT[0:CW, c % 2, :], psC[:, :].bitcast(BF16)[0:CW, 0:CH], ACT.Copy).then_inc(s["cwT_ready"], 1)

            def rstd(c):
                act.wait_ge(s["var_ready"], c + 1)
                nc.scalar.activation(m.lnvar4[:, :], m.meanvar4[:, :, 1], ACT.Ln, bias=m.eps[:, 0:1]).then_inc(s["ln_done"], 1)
                act.wait_ge(s["ln_done"], c + 1)
                nc.scalar.activation(m.rstd4[:, :], m.lnvar4[:, :], ACT.Exp, scale=-0.5).then_inc(s["rstd_ready"], 1)

            copy_turned(0)
            exponentials(0)
            copy_weights(0)
            for c in range(NC):
                for j in range(MM):
                    n = MM * c + j
                    act.wait_ge(s["z_psum"], n + 1)
                    wait(act, s["hid_ready"], n - 1)
                    nc.scalar.activation(m.relu[:, n % 2, :], psZ[n % 2][:, :], ACT.Relu).then_inc(s["relu_ready"], 1)
                    if j == 1 and c > 0:
                        rstd(c - 1)
                    if c + 1 < NC:
                        if j == 1:
                            copy_turned(c + 1)
                        if j == 2:
                            exponentials(c + 1)
                if c + 1 < NC:
                    copy_weights(c + 1)
            rstd(NC - 1)

        @block.gpsimd
        def _(pool):
            m.stages.zero_spent(pool)

            for c in range(NC):
                for j in range(MM):
                    n = MM * c + j
                    wait(pool, s["y_psum"], n - 1)
                    if j < NM:
                        g = NM * c + j
                        pool.wait_ge(s["gated"], g + 1)
                        a = m.gated[:, g % 2, :]
                    else:
                        pool.wait_ge(s["relu_ready"], n + 1)
                        a = m.relu[:, n % 2, :]
                    nc.gpsimd.tensor_tensor(m.hid[:, n % 2, :], a, m.relu[:, n % 2, :], ALU.mult).then_inc(s["hid_ready"], 1)

        @block.vector
        def _(dve):
            steps = Chain(dve, s["route"])
            link = steps.link
            v = nc.vector
            ch = m.choice[:, :]
            groups = "p (x e) -> p x e"

            def route_groups(c):
                dve.wait_ge(s["exp_ready"], c + 1)
                link(v.tensor_scalar(m.route_s[:, :], m.route_e[:, :], 1.0, None, ALU.add))
                link(v.reciprocal(m.score16[:, :], m.route_s[:, :]))
                link(v.tensor_tensor(ch.rearrange("p (t e) -> p t e", e=NE), m.score16[:, :].rearrange("p (t e) -> p t e", e=NE),
                                     w.bias16.unsqueeze(1).broadcast_to([P, CT, NE]), ALU.add))
                pair = ch.rearrange("p (x z) -> p x z", z=2)
                v.tensor_tensor(m.pair_hi[:, :], pair[:, :, 0], pair[:, :, 1], ALU.max)
                link(v.tensor_tensor(m.pair_lo[:, :], pair[:, :, 0], pair[:, :, 1], ALU.min))
                hi = m.pair_hi[:, :].rearrange("p (x z) -> p x z", z=2)
                lo = m.pair_lo[:, :].rearrange("p (x z) -> p x z", z=2)
                v.tensor_tensor(m.top1[:, :], hi[:, :, 0], hi[:, :, 1], ALU.max)
                v.tensor_tensor(m.second_a[:, :], hi[:, :, 0], hi[:, :, 1], ALU.min)
                link(v.tensor_tensor(m.second_b[:, :], lo[:, :, 0], lo[:, :, 1], ALU.max))
                link(v.tensor_tensor(m.second_a[:, :], m.second_a[:, :], m.second_b[:, :], ALU.max))
                link(v.tensor_tensor(m.group_score[:, :], m.top1[:, :], m.second_a[:, :], ALU.add))
                gs = m.group_score[:, :].rearrange("p (t g) -> p t g", g=NG)
                theirs = gs.unsqueeze(2).broadcast_to([P, CT, NG, NG])
                own = gs.unsqueeze(3).broadcast_to([P, CT, NG, NG])
                v.tensor_tensor(m.above[:, :].rearrange("p (t g j) -> p t g j", g=NG, j=NG), theirs, own, ALU.is_gt)
                link(v.tensor_tensor(m.level[:, :].rearrange("p (t g j) -> p t g j", g=NG, j=NG), theirs, own, ALU.is_equal))
                link(v.tensor_tensor(m.level[:, :].rearrange("p (t gj) -> p t gj", t=CT), m.level[:, :].rearrange("p (t gj) -> p t gj", t=CT),
                                     w.ahead.unsqueeze(1).broadcast_to([P, CT, NG * NG]), ALU.mult))
                link(v.tensor_tensor(m.above[:, :], m.above[:, :], m.level[:, :], ALU.add))
                link(v.tensor_reduce(m.rank[:, :], m.above[:, :].rearrange("p (x j) -> p x j", j=NG), AX.X, ALU.add))
                link(v.tensor_scalar(m.rank[:, :], m.rank[:, :], TOPG - 0.5, None, ALU.is_lt))
                link(v.tensor_tensor(m.masked[:, :].rearrange("p (x e) -> p x e", e=NE // NG),
                                     ch.rearrange("p (x e) -> p x e", e=NE // NG),
                                     m.rank[:, :].unsqueeze(2).broadcast_to([P, CT * NG, NE // NG]), ALU.mult))

            def route_experts(c):
                masked = m.masked[:, :].rearrange("p (t e) -> p t e", e=NE)
                for t in range(CT):
                    op = v.max(m.top8[:, t, :], masked[:, t, :])
                link(op)
                fourth = m.top8[:, :, TOPK - 1:TOPK].broadcast_to([P, CT, NE])
                v.tensor_tensor(m.picked[:, :, :], masked, fourth, ALU.is_gt)
                link(v.tensor_tensor(m.count[:, 0, :, NE // 2:], masked, fourth, ALU.is_equal))
                link(v.tensor_reduce(m.room[:, :], m.picked[:, :, :], AX.X, ALU.add))
                link(v.tensor_scalar(m.room[:, :], m.room[:, :], -1.0, float(TOPK), ALU.mult, ALU.add))
                src = 0
                for shift in (1, 2, 4, 8):
                    dst = 1 if src != 1 else 2
                    link(v.tensor_tensor(m.count[:, dst, :, NE // 2:], m.count[:, src, :, NE // 2:],
                                         m.count[:, src, :, NE // 2 - shift:NE // 2 - shift + NE], ALU.add))
                    src = dst
                link(v.tensor_tensor(m.fits[:, :, :], m.count[:, src, :, NE // 2:],
                                     m.room[:, :].unsqueeze(2).broadcast_to([P, CT, NE]), ALU.is_le))
                link(v.tensor_tensor(m.fits[:, :, :], m.fits[:, :, :], m.count[:, 0, :, NE // 2:], ALU.mult))
                link(v.tensor_tensor(m.picked[:, :, :], m.picked[:, :, :], m.fits[:, :, :], ALU.add))

            def route_weights(c):
                sc = m.score16[:, :].rearrange("p (t e) -> p t e", e=NE)
                link(v.tensor_tensor(m.picked[:, :, :], m.picked[:, :, :], sc, ALU.mult))
                link(v.tensor_reduce(m.total[:, :], m.picked[:, :, :], AX.X, ALU.add))
                link(v.tensor_scalar(m.total[:, :], m.total[:, :], 1e-20, None, ALU.add))
                link(v.reciprocal(m.total[:, :], m.total[:, :]))
                link(v.scalar_tensor_tensor(out=m.cw[:, :, :], in0=m.picked[:, :, :], scalar=2.5,
                                            in1=m.total[:, :].unsqueeze(2).broadcast_to([P, CT, NE]),
                                            op0=ALU.mult, op1=ALU.mult))
                wait(dve, s["cwT_psum"], c)
                link(v.tensor_copy(m.cw3[:, :, 0:NE], m.cw[:, :, :]))
                link(v.tensor_tensor(m.cw[:, :, :], m.cw[:, :, :], m.cw3[:, :, 0:NE], ALU.subtract))
                link(v.tensor_copy(m.cw3[:, :, 32:32 + NE], m.cw[:, :, :]))
                v.tensor_tensor(m.cw3[:, :, 64:64 + NE], m.cw[:, :, :], m.cw3[:, :, 32:32 + NE],
                                ALU.subtract).then_inc(s["cw_ready"], 1)

            def residual(c):
                dve.wait_ge(s["y_psum"], MM * (c + 1))
                wait(dve, s["x_new"], c)
                v.tensor_tensor(m.r4[:, :, :].rearrange("p t d -> p (t d)"), psY[:, :],
                                m.X[:, CT * c:CT * (c + 1), :].rearrange("p t d -> p (t d)"), ALU.add).then_inc(s["r_done"], 1)
                dve.wait_ge(s["r_done"], c + 1)
                for t in range(CT):
                    op = v.bn_stats(m.bn24[:, t, :], m.r4[:, t, :])
                link(op)
                for t in range(CT):
                    op = v.bn_aggr(m.meanvar4[:, t, :], m.bn24[:, t, :])
                op.then_inc(s["var_ready"], 1)

            def apply(c):
                dve.wait_ge(s["rstd_ready"], c + 1)
                for t in range(CT):
                    op = v.tensor_scalar(m.X[:, CT * c + t, :], m.r4[:, t, :], m.meanvar4[:, t, 0:1], m.rstd4[:, t:t + 1],
                                         ALU.subtract, ALU.mult)
                op.then_inc(s["x_new"], 1)

            route_groups(0)
            route_experts(0)
            route_weights(0)
            for c in range(NC):
                for j in range(NM):
                    g, n = NM * c + j, MM * c + j
                    dve.wait_ge(s["gate_psum"], g + 1)
                    dve.wait_ge(s["relu_ready"], n + 1)
                    wait(dve, s["hid_ready"], n - 1 if j >= 2 else (MM * (c - 1) + NM - 1 + j if c > 0 else 0))
                    v.tensor_tensor(m.gated[:, g % 2, :], m.relu[:, n % 2, :], psW[g % 2][:, :], ALU.mult).then_inc(s["gated"], 1)
                    if j == 0 and c > 0:
                        residual(c - 1)
                    if j == 2 and c > 0:
                        apply(c - 1)
                    if c + 1 < NC:
                        if j == 3:
                            route_groups(c + 1)
                        if j == 5:
                            route_experts(c + 1)
                        if j == 6:
                            route_weights(c + 1)
            residual(NC - 1)
            apply(NC - 1)



MAGIC = 12582912.0
QMAX = 32767.0
SIG = 65536.0
NJ = 3


def quantised(nc, m, w, prefix):
    with ExitStack() as ctx:
        s = m.stages.semaphores(prefix,
                       "step xT_psum col_psum col_ready row_ready all_psum scaled x_shifted x_ready gu_psum gu_copied"
                       " g_shifted g_int sig_ready sig_int u_shifted q_shifted o_shifted o_ready y_psum r_done"
                       " var_ready ln_done rstd_ready")
        def sb(name, shape, dt=F32):
            return ctx.enter_context(nc.sbuf_tensor(prefix + name, shape, dt))

        m.xq = sb("xq", [P, NC, CH])
        m.G, m.U = sb("G", [P, NC, NJ, CH]), sb("U", [P, NC, NJ, CH])
        m.S = sb("S", [P, 2, NJ, CH])
        psM = m.bank[7]
        block = ctx.enter_context(nc.Block())

        @block.gpsimd
        def _(pool):
            m.stages.zero_spent(pool)
        NP = NJ * NC

        @block.tensor
        def _(pe):
            def spread_max(k):
                pe.wait_ge(s["col_ready"], k + 1)
                nc.tensor.transpose(psM[0:1, 0:P], m.q_col[:, 0:1], m.ident).then_inc(s["col_psum"], 1)
                pe.wait_ge(s["row_ready"], k + 1)
                nc.tensor.matmul(psM[:, P:P + 1], m.ones_row[0:1, :], m.q_one[0:1, 0:1], start=True,
                                 stop=True).then_inc(s["all_psum"], 1)

            for c in range(NC):
                for t in range(CT):
                    mm = nc.tensor.transpose(m.bank[c][:, t * P:(t + 1) * P], m.X[:, CT * c + t, :], m.ident)
                mm.then_inc(s["xT_psum"], 1)
            spread_max(0)
            for which, wt in enumerate((w.gate, w.up)):
                for j in range(NJ):
                    for c in range(NC):
                        n = NP * which + NC * j + c
                        if n < NC:
                            pe.wait_ge(s["x_ready"], n + 1)
                        wait(pe, s["gu_copied"], n - 2)
                        nc.tensor.matmul(m.bank[4 + n % 3][:, :], wt[:, j, :], m.xq[:, c, :], start=True,
                                         stop=True).then_inc(s["gu_psum"], 1)
            for k in range(1, 5):
                spread_max(k)
            for c in range(NC):
                pe.wait_ge(s["o_ready"], c + 1)
                for t in range(CT):
                    for j in range(NJ):
                        mm = nc.tensor.matmul(m.bank[c][:, t * D:(t + 1) * D], m.G[:, c, j, t * P:(t + 1) * P], w.down[:, j, :],
                                              start=(j == 0), stop=(j == NJ - 1))
                mm.then_inc(s["y_psum"], 1)

        @block.scalar
        def _(act):
            def shift(out, in_, scale):
                return nc.scalar.activation(out, in_, ACT.Identity, bias=m.magic[:, 0:1], scale=scale)

            act.wait_ge(s["scaled"], 1)
            for c in range(NC):
                act.wait_ge(s["xT_psum"], c + 1)
                shift(m.xq[:, c, :], m.bank[c][:, :], m.q_k[:, 0:1]).then_inc(s["x_shifted"], 1)
            for n in range(2 * NP):
                act.wait_ge(s["gu_psum"], n + 1)
                dst = (m.G if n < NP else m.U)[:, n % NC, n % NP // NC, :]
                nc.scalar.activation(dst, m.bank[4 + n % 3][:, :], ACT.Copy).then_inc(s["gu_copied"], 1)
            act.wait_ge(s["scaled"], 2)
            for c in range(NC):
                shift(m.G[:, c, :, :], m.G[:, c, :, :], m.q_k[:, 1:2]).then_inc(s["g_shifted"], 1)
            for c in range(NC):
                act.wait_ge(s["g_int"], c + 1)
                wait(act, s["sig_int"], c - 1)
                nc.scalar.activation(m.S[:, c % 2, :, :], m.G[:, c, :, :], ACT.Sigmoid, scale=m.q_s[:, 1:2]).then_inc(s["sig_ready"], 1)
            act.wait_ge(s["scaled"], 3)
            for c in range(NC):
                shift(m.U[:, c, :, :], m.U[:, c, :, :], m.q_k[:, 2:3]).then_inc(s["u_shifted"], 1)
            act.wait_ge(s["scaled"], 4)
            for c in range(NC):
                shift(m.G[:, c, :, :], m.G[:, c, :, :], m.q_k[:, 3:4]).then_inc(s["q_shifted"], 1)
            act.wait_ge(s["scaled"], 5)
            for c in range(NC):
                shift(m.G[:, c, :, :], m.G[:, c, :, :], m.q_k[:, 4:5]).then_inc(s["o_shifted"], 1)
            act.preload_act_table_set("natural_log_exp_and_others")
            for c in range(NC):
                act.wait_ge(s["var_ready"], c + 1)
                nc.scalar.activation(m.lnvar4[:, :], m.meanvar4[:, :, 1], ACT.Ln, bias=m.eps[:, 0:1]).then_inc(s["ln_done"], 1)
                act.wait_ge(s["ln_done"], c + 1)
                nc.scalar.activation(m.rstd4[:, :], m.lnvar4[:, :], ACT.Exp, scale=-0.5).then_inc(s["rstd_ready"], 1)

        @block.vector
        def _(dve):
            v = nc.vector
            link = Chain(dve, s["step"]).link

            def scale(k, parts, unit):
                v.tensor_reduce(m.q_col[:, 0:1], parts, AX.X, ALU.max).then_inc(s["col_ready"], 1)
                dve.wait_ge(s["col_psum"], k + 1)
                v.tensor_reduce(m.q_one[0:1, 0:1], psM[0:1, 0:P], AX.X, ALU.max).then_inc(s["row_ready"], 1)
                dve.wait_ge(s["all_psum"], k + 1)
                if unit is None:
                    link(v.tensor_scalar(m.q_s[:, k:k + 1], psM[:, P:P + 1], 1.0 / QMAX, 1e-12, ALU.mult, ALU.max))
                    v.reciprocal(m.q_k[:, k:k + 1], m.q_s[:, k:k + 1]).then_inc(s["scaled"], 1)
                else:
                    link(v.tensor_scalar(m.q_t[:, 0:1], psM[:, P:P + 1], unit, 1.0 / QMAX, ALU.mult, ALU.mult))
                    link(v.tensor_scalar(m.q_s[:, k:k + 1], m.q_t[:, 0:1], 1e-12, None, ALU.max))
                    link(v.reciprocal(m.q_t[:, 0:1], m.q_s[:, k:k + 1]))
                    v.tensor_tensor(m.q_k[:, k:k + 1], m.q_t[:, 0:1], unit, ALU.mult).then_inc(s["scaled"], 1)

            def absmax(out, in_):
                return v.tensor_reduce(out, in_, AX.XY if len(in_.shape) > 2 else AX.X, ALU.max, apply_absolute_value=True)

            link(absmax(m.q_parts[:, 0:1], m.X[:, :, :]))
            scale(0, m.q_parts[:, 0:1], None)
            for c in range(NC):
                dve.wait_ge(s["x_shifted"], c + 1)
                v.tensor_scalar(m.xq[:, c, :], m.xq[:, c, :], MAGIC, None, ALU.subtract).then_inc(s["x_ready"], 1)
            for which in range(2):
                for n in range(NP * which, NP * (which + 1)):
                    dve.wait_ge(s["gu_copied"], n + 1)
                    op = absmax(m.q_parts[:, n:n + 1], (m.G if n < NP else m.U)[:, n % NC, n % NP // NC, :])
                link(op)
                if which == 0:
                    scale(1, m.q_parts[:, 0:NP], m.q_s[:, 0:1])
            for c in range(NC):
                dve.wait_ge(s["g_shifted"], c + 1)
                v.tensor_scalar(m.G[:, c, :, :], m.G[:, c, :, :], MAGIC, None, ALU.subtract).then_inc(s["g_int"], 1)
            scale(2, m.q_parts[:, NP:2 * NP], m.q_s[:, 0:1])
            for c in range(NC):
                dve.wait_ge(s["sig_ready"], c + 1)
                link(v.tensor_scalar(m.S[:, c % 2, :, :], m.S[:, c % 2, :, :], SIG, SIG - 1, ALU.mult, ALU.min))
                link(v.tensor_scalar(m.S[:, c % 2, :, :], m.S[:, c % 2, :, :], MAGIC, MAGIC, ALU.add, ALU.subtract))
                v.tensor_tensor(m.G[:, c, :, :], m.S[:, c % 2, :, :], m.G[:, c, :, :], ALU.mult).then_inc(s["sig_int"], 1)
                dve.wait_ge(s["sig_int"], c + 1)
                op = absmax(m.q_parts[:, c:c + 1], m.G[:, c, :, :])
            link(op)
            link(v.tensor_scalar(m.q_u[:, 0:1], m.q_s[:, 1:2], 1.0 / SIG, None, ALU.mult))
            scale(3, m.q_parts[:, 0:NC], m.q_u[:, 0:1])
            for c in range(NC):
                dve.wait_ge(s["u_shifted"], c + 1)
                op = v.tensor_scalar(m.U[:, c, :, :], m.U[:, c, :, :], MAGIC, None, ALU.subtract)
            link(op)
            for c in range(NC):
                dve.wait_ge(s["q_shifted"], c + 1)
                link(v.scalar_tensor_tensor(out=m.G[:, c, :, :], in0=m.G[:, c, :, :], scalar=MAGIC, in1=m.U[:, c, :, :],
                                            op0=ALU.subtract, op1=ALU.mult))
                op = absmax(m.q_parts[:, c:c + 1], m.G[:, c, :, :])
            link(op)
            link(v.tensor_tensor(m.q_u[:, 1:2], m.q_s[:, 3:4], m.q_s[:, 2:3], ALU.mult))
            scale(4, m.q_parts[:, 0:NC], m.q_u[:, 1:2])
            for c in range(NC):
                dve.wait_ge(s["o_shifted"], c + 1)
                v.tensor_scalar(m.G[:, c, :, :], m.G[:, c, :, :], MAGIC, None, ALU.subtract).then_inc(s["o_ready"], 1)
            for c in range(NC):
                dve.wait_ge(s["y_psum"], c + 1)
                link(v.scalar_tensor_tensor(out=m.r4[:, :, :].rearrange("p t d -> p (t d)"), in0=m.bank[c][:, :],
                                            scalar=m.q_s[:, 4:5], in1=m.X[:, CT * c:CT * (c + 1), :].rearrange("p t d -> p (t d)"),
                                            op0=ALU.mult, op1=ALU.add))
                for t in range(CT):
                    op = v.bn_stats(m.bn24[:, t, :], m.r4[:, t, :])
                link(op)
                for t in range(CT):
                    op = v.bn_aggr(m.meanvar4[:, t, :], m.bn24[:, t, :])
                op.then_inc(s["var_ready"], 1)
                dve.wait_ge(s["rstd_ready"], c + 1)
                for t in range(CT):
                    op = v.tensor_scalar(m.X[:, CT * c + t, :], m.r4[:, t, :], m.meanvar4[:, t, 0:1], m.rstd4[:, t:t + 1],
                                         ALU.subtract, ALU.mult)
                link(op)



HEAD_COLS = [("ident", P), ("mask_ac", 4), ("mask_ca", 4), ("mask_i", NI), ("causal", T), ("w0_q", D), ("w0_k", D), ("w0_v", D),
             ("w0_bias", D), ("cos", T), ("sin", T), ("rotT", D),
             ("x0_q", D), ("x0_k", D), ("x0_v", D), ("x0_qf", D), ("x0_kf", D)]
BODY_COLS = [("x1_q", D), ("x1_k", D), ("x1_v", D), ("x1_qf", D), ("x1_kf", D), ("x1_bq", 1), ("x1_bk", 1), ("x1_bv", 1),
             ("x1_of", D), ("x1_bo", D),
             ("l_dq", LC), ("l_df", LC + LR), ("l_uq", LH * (LC + 1)), ("l_uk", LH * (LC + 1)), ("l_uv", LH * LC),
             ("l_buv", LH), ("l_o", LH * D), ("l_bo", D),
             ("e_router", NE), ("e_bias", NE), ("e_ahead", NG * NG), ("e_w1", NE * 64), ("e_w2", NM * D), ("e_s1", D), ("e_s2", D),
             ("e_spread", NM * P), ("q_w", 9 * D)]
ROW64_COLS = [("w0_o", 2 * D), ("x0_o", 2 * D), ("x1_o", 2 * D), ("l_qr", LH * LR),
              ("l_bq", 1), ("l_bf", 1), ("l_bl", LC)]


def columns(cols):
    at, out = 0, {}
    for name, n in cols:
        out[name] = (at, n)
        at += n
    return out, at


def decoder(nc, x, ctxT, mask, head, body, row64, out):
    with ExitStack() as ctx:
        m = Names()

        def sb(name, shape, dt=F32):
            return ctx.enter_context(nc.sbuf_tensor(name, shape, dt))

        m.bank = [ctx.enter_context(nc.psum_tensor(f"bank{i}", [P, 512], F32)) for i in range(8)]
        m.ctxT_dram = ctxT
        m.stages = Stages(nc)
        m.X = sb("X", [P, NT, D])
        head_at, head_n = columns(HEAD_COLS)
        body_at, body_n = columns(BODY_COLS)
        row64_at, row64_n = columns(ROW64_COLS)
        head_sb = sb("head_sb", [P, head_n])
        body_sb = sb("body_sb", [P, body_n])
        row64_sb = sb("row64_sb", [T, row64_n])

        def h(name):
            at, n = head_at[name]
            return head_sb[:, at:at + n]

        def bd(name):
            at, n = body_at[name]
            return body_sb[:, at:at + n]

        def r64(name):
            at, n = row64_at[name]
            return row64_sb[:, at:at + n]

        def out_rows(name):
            return r64(name).rearrange("p (c o) -> p c o", c=2)

        m.ident, m.mask_ac, m.mask_ca, m.mask_i, m.causal = h("ident"), h("mask_ac"), h("mask_ca"), h("mask_i"), h("causal")
        m.cos, m.sin = h("cos"), h("sin")
        m.mask_u8 = sb("mask_u8", [1, NSEQ * T], U8)
        m.mask_row = sb("mask_row", [1, NSEQ * T], BF16)
        m.ones_bf = sb("ones_bf", [1, P], BF16)
        m.one = sb("one", [P, 1])
        m.eps = sb("eps", [P, 1])
        m.zero_bias = sb("zero_bias", [P, D])
        m.xs = sb("xs", [P, 2, P])
        m.xb = sb("xb", [P, 2, P])
        m.xT = sb("xT", [P, 2, SB, 2, T])
        m.kvT = sb("kvT", [P, 2, SB, 2, T])
        m.qk = sb("qk", [P, 2, 2, P])
        m.vals = sb("vals", [P, 2, SB, NI, 2, 2, HD + 1])
        m.rowmax = sb("rowmax", [P, SB, 8])
        m.den = sb("den", [P, 16])
        m.rden = sb("rden", [P, 16])
        m.o = sb("o", [P, 2, SB, T])
        m.oT = sb("oT", [P, 2, P])
        m.r = sb("r", [P, D])
        m.bn6 = sb("bn6", [P, 6])
        m.meanvar = sb("meanvar", [P, 2])
        m.lnvar = sb("lnvar", [P, 1])
        m.rstd = sb("rstd", [P, 1])
        m.f = sb("f", [LF, 2, P])
        m.cq = sb("cq", [LC + 1, 2, P])
        m.g = sb("g", [LF, 2, SB, LH, T])
        m.lvals = sb("lvals", [P, 2, SB, 2, LC + 1])
        m.lprob = sb("lprob", [P, 2, SB, 2, P])
        m.lprobT = sb("lprobT", [P, 512])
        m.lo = sb("lo", [P, 2, SB, P])
        m.ones_row = sb("ones_row", [1, P])
        m.l_score = sb("l_score", [LC + 1, LH, LF])
        m.l_out = sb("l_out", [P, 2, D])
        m.l_bias = sb("l_bias", [P, D])
        m.x1_bias = sb("x1_bias", [P, D])
        m.ident_bf = sb("ident_bf", [P, P], BF16)
        m.spread = sb("spread", [CW, NM, P], BF16)
        m.xTc = sb("xTc", [P, 2, CH])
        m.route_e, m.route_s, m.score16, m.choice, m.masked = (sb(n, [P, CT * NE]) for n in ("route_e", "route_s", "score16", "choice", "masked"))
        m.pair_hi, m.pair_lo = sb("pair_hi", [P, CT * NE // 2]), sb("pair_lo", [P, CT * NE // 2])
        m.top1, m.second_a, m.second_b, m.group_score, m.rank = (sb(n, [P, CT * NG]) for n in ("top1", "second_a", "second_b", "group_score", "rank"))
        m.above, m.level = sb("above", [P, CT * NG * NG]), sb("level", [P, CT * NG * NG])
        m.top8 = sb("top8", [P, CT, 8])
        m.picked, m.fits, m.cw = (sb(n, [P, CT, NE]) for n in ("picked", "fits", "cw"))
        m.count = sb("count", [P, 3, CT, NE // 2 + NE])
        m.room, m.total = sb("room", [P, CT]), sb("total", [P, CT])
        m.cw3 = sb("cw3", [P, CT, CW], BF16)
        m.cwT = sb("cwT", [CW, 2, CH], BF16)
        m.relu, m.gated, m.hid = (sb(n, [P, 2, CH]) for n in ("relu", "gated", "hid"))
        m.r4, m.bn24, m.meanvar4 = sb("r4", [P, CT, D]), sb("bn24", [P, CT, 6]), sb("meanvar4", [P, CT, 2])
        m.lnvar4, m.rstd4 = sb("lnvar4", [P, CT]), sb("rstd4", [P, CT])
        m.magic = sb("magic", [P, 1])
        m.q_col, m.q_one, m.q_t, m.q_u = sb("q_col", [P, 1]), sb("q_one", [1, 1]), sb("q_t", [P, 1]), sb("q_u", [P, 2])
        m.q_s, m.q_k, m.q_parts = sb("q_s", [P, 5]), sb("q_k", [P, 5]), sb("q_parts", [P, 2 * NJ * NC])
        m.qw = sb("qw", [P, 9 * 4, 32])
        m.qwT = sb("qwT", [P, 9, D])
        m.qw_s, m.qw_i = sb("qw_s", [P, 36]), sb("qw_i", [P, 36])
        m.rot_w = sb("rot_w", [P, 4, D])
        m.rot_b = sb("rot_b", [P, 2])

        with ExitStack() as c2:
            s = m.stages.semaphores("i_", "x head body row64 mask memset rot_psum done vz weights qw_done qwT_psum")
            block = c2.enter_context(nc.Block())

            @block.sync
            def _(sp):
                sp.dma_start(head_sb[:, :], head).then_inc(s["head"], 16)
                sp.dma_start(body_sb[:, :], body).then_inc(s["body"], 16)
                sp.dma_start(row64_sb[:, :], row64).then_inc(s["row64"], 16)
                sp.wait_ge(s["row64"], 16)

            @block.scalar
            def _(act):
                act.dma_start(m.X[:, :, :], x.rearrange("(t p) c -> p t c", p=P)).then_inc(s["x"], 16)
                act.dma_start(m.mask_u8[:, :], mask).then_inc(s["mask"], 16)
                act.wait_ge(s["x"], 16)

            @block.gpsimd
            def _(pool):
                pool.memset(m.ones_bf[:, :], 1.0)
                pool.memset(m.one[:, :], 1.0)
                pool.memset(m.eps[:, :], EPS)
                pool.memset(m.zero_bias[:, :], 0.0)
                pool.memset(m.magic[:, :], MAGIC)
                pool.memset(m.cw3[:, :, :], 0.0)
                pool.memset(m.count[:, :, :, :], 0.0)
                pool.memset(m.ones_row[:, :], 1.0)
                pool.memset(m.lvals[:, :, :, :, :], 0.0)
                pool.memset(m.vals[:, :, :, :, :, :, :], 0.0).then_inc(s["vz"], 1)
                pool.wait_ge(s["vz"], 1)
                for a in range(2):
                    for par in range(2):
                        pool.memset(m.vals[a * T:a * T + T, par, :, :, a, :, HD], 1.0)
                        op = pool.memset(m.lvals[a * T:a * T + T, par, :, a, LC], 1.0)
                op.then_inc(s["memset"], 1)

            @block.tensor
            def _(pe):
                pe.wait_ge(s["head"], 16)
                pe.wait_ge(s["body"], 16)
                for n, wf in enumerate((h("x0_qf"), h("x0_kf"), bd("x1_qf"), bd("x1_kf"))):
                    nc.tensor.matmul(m.bank[0][:, n * D:(n + 1) * D], wf, h("rotT"), start=True, stop=True)
                for n, b in enumerate((bd("x1_bq"), bd("x1_bk"))):
                    nc.tensor.matmul(m.bank[1][:, n:n + 1], h("rotT"), b, start=True, stop=True)
                uq = bd("l_uq").rearrange("p (h l) -> p h l", h=LH)
                uk = bd("l_uk").rearrange("p (h l) -> p h l", h=LH)
                uv = bd("l_uv").rearrange("p (h l) -> p h l", h=LH)
                wo = bd("l_o").rearrange("p (h o) -> p h o", h=LH)
                for hh in range(LH):
                    nc.tensor.matmul(m.bank[2][0:LC + 1, hh * (LC + 1):(hh + 1) * (LC + 1)], uq[:, hh, :], uk[:, hh, :],
                                     start=True, stop=True)
                for hh in range(LH):
                    row, c = LC * (hh // 2), hh % 2
                    nc.tensor.matmul(m.bank[3][row:row + LC, c * D:(c + 1) * D], uv[:, hh, :], wo[:, hh, :],
                                     start=True, stop=True)
                for hh in range(LH):
                    nc.tensor.matmul(m.bank[4][:, 0:D], bd("l_buv")[:, hh:hh + 1].broadcast_to([P, P]), wo[:, hh, :],
                                     start=(hh == 0), stop=(hh == LH - 1))
                mm = nc.tensor.matmul(m.bank[4][:, D:2 * D], bd("x1_bv").broadcast_to([P, P]), bd("x1_of"),
                                      start=True, stop=True)
                mm.then_inc(s["rot_psum"], 1)
                pe.wait_ge(s["qw_done"], 1)
                for n in range(9):
                    mm = nc.tensor.transpose(m.bank[5 + n // 4][:, n % 4 * P:(n % 4 + 1) * P],
                                             m.qw[:, 4 * n:4 * n + 4, :], m.ident)
                mm.then_inc(s["qwT_psum"], 1)

            @block.vector
            def _(dve):
                nc.vector.memset(m.cq[LC:LC + 1, :, :], 1.0)
                nc.vector.memset(m.f[LC + LR:LF, :, :], 1.0)
                dve.wait_ge(s["rot_psum"], 1)
                link = Chain(dve, s["weights"]).link
                dve.wait_ge(s["body"], 16)
                raw = bd("q_w").rearrange("p (x k) -> p x k", k=32)
                by_block = lambda a: a.unsqueeze(2).broadcast_to([P, 36, 32])
                link(nc.vector.tensor_reduce(m.qw_i[:, :], raw, AX.X, ALU.max, apply_absolute_value=True))
                link(nc.vector.tensor_scalar(m.qw_s[:, :], m.qw_i[:, :], 1.0 / 7.0, 1e-12, ALU.mult, ALU.max))
                link(nc.vector.reciprocal(m.qw_i[:, :], m.qw_s[:, :]))
                link(nc.vector.tensor_tensor(m.qw[:, :, :], raw, by_block(m.qw_i[:, :]), ALU.mult))
                link(nc.vector.tensor_scalar(m.qw[:, :, :], m.qw[:, :, :], MAGIC, MAGIC, ALU.add, ALU.subtract))
                nc.vector.tensor_tensor(m.qw[:, :, :], m.qw[:, :, :], by_block(m.qw_s[:, :]), ALU.mult).then_inc(s["qw_done"], 1)
                nc.vector.tensor_copy(m.ident_bf[:, :], m.ident)
                nc.vector.tensor_copy(m.spread[:, :, :].rearrange("p j q -> p (j q)"), bd("e_spread")[0:CW, :])
                nc.vector.tensor_copy(m.rot_w[:, :, :].rearrange("p n d -> p (n d)"), m.bank[0][:, :])
                nc.vector.tensor_copy(m.rot_b[:, :], m.bank[1][:, 0:2])
                ps = m.bank[2][0:LC + 1, 0:LH * (LC + 1)].rearrange("p (h l) -> p h l", h=LH)
                dve.wait_ge(s["row64"], 16)
                nc.vector.tensor_copy(m.l_score[:, :, 0:LC], ps[:, :, 0:LC])
                nc.vector.tensor_copy(m.l_score[:, :, LC + LR:LF], ps[:, :, LC:LC + 1])
                nc.vector.tensor_copy(m.l_score[:, :, LC:LC + LR], r64("l_qr")[0:LC + 1, :].rearrange("p (h l) -> p h l", h=LH))
                nc.vector.tensor_copy(m.l_out[:, :, :].rearrange("p c o -> p (c o)"), m.bank[3][:, 0:2 * D])
                nc.vector.tensor_tensor(m.l_bias[:, :], m.bank[4][:, 0:D], bd("l_bo"), ALU.add)
                nc.vector.tensor_tensor(m.x1_bias[:, :], m.bank[4][:, D:2 * D], bd("x1_bo"), ALU.add)
                dve.wait_ge(s["qwT_psum"], 1)
                for n in range(9):
                    nc.vector.tensor_copy(m.qwT[:, n, :], m.bank[5 + n // 4][:, n % 4 * P:(n % 4 + 1) * P])
                dve.wait_ge(s["mask"], 16)
                nc.vector.tensor_scalar(m.mask_row[:, :], m.mask_u8[:, :], 1.0, BIG, ALU.subtract, ALU.mult).then_inc(s["done"], 1)

        w = Names()
        w.wq, w.wk, w.wv, w.wo, w.bias_tile, w.mask_row = h("w0_q"), h("w0_k"), h("w0_v"), out_rows("w0_o"), h("w0_bias"), None
        small_attention(nc, m, w, "causal", "a0_")
        w = Names()
        w.wq, w.wk, w.wv, w.wo, w.bias_tile, w.mask_row = h("x0_q"), h("x0_k"), h("x0_v"), out_rows("x0_o"), m.zero_bias[:, :], m.mask_row
        w.wqr, w.wkr = m.rot_w[:, 0, :], m.rot_w[:, 1, :]
        w.bq = w.bqr = w.bk = w.bkr = 0.0
        small_attention(nc, m, w, "cross", "x0_")

        w = Names()
        w.router, w.bias16, w.ahead = bd("e_router"), bd("e_bias"), bd("e_ahead")
        w.w1, w.w2, w.shared1, w.shared2 = bd("e_w1"), bd("e_w2"), bd("e_s1"), bd("e_s2")
        experts(nc, m, w, "e_")
        w = Names()
        w.dq, w.df, w.b_q, w.b_f, w.b_latent = bd("l_dq"), bd("l_df"), r64("l_bq")[0:LC, :], r64("l_bf"), r64("l_bl")[0:1, :]
        w.score, w.out, w.bias_tile = m.l_score, m.l_out, m.l_bias[:, :]
        latent_attention(nc, m, w, "l1_")
        w = Names()
        w.wq, w.wk, w.wv, w.wo, w.bias_tile, w.mask_row = bd("x1_q"), bd("x1_k"), bd("x1_v"), out_rows("x1_o"), m.x1_bias[:, :], None
        w.wqr, w.wkr = m.rot_w[:, 2, :], m.rot_w[:, 3, :]
        w.bq, w.bk, w.bqr, w.bkr = bd("x1_bq"), bd("x1_bk"), m.rot_b[:, 0:1], m.rot_b[:, 1:2]
        small_attention(nc, m, w, "cross", "x1_")
        w = Names()
        w.gate, w.up, w.down = m.qwT[:, 0:3, :], m.qwT[:, 3:6, :], m.qwT[:, 6:9, :]
        quantised(nc, m, w, "q_")

        with ExitStack() as c2:
            s = m.stages.semaphores("o_", "out")
            block = c2.enter_context(nc.Block())

            @block.sync
            def _(sp):
                sp.dma_start(out.rearrange("(t p) c -> p t c", p=P), m.X[:, :, :]).then_inc(s["out"], 16)
                sp.wait_ge(s["out"], 16)


def host_constants():
    import numpy as np
    c = {"ident": np.eye(P, dtype=np.float32)}
    p = np.arange(P)
    c["mask_ac"] = (p[:, None] // HD % 4 == np.arange(4)).astype(np.float32)
    c["mask_ca"] = np.ascontiguousarray(c["mask_ac"][:, [0, 2, 1, 3]])
    c["mask_i"] = (p[:, None] // (4 * HD) == np.arange(NI)).astype(np.float32)
    c["causal"] = np.where(p[:, None] % T <= np.arange(T), 0.0, -1e30).astype(np.float32)
    gj = np.arange(NG * NG)
    c["e_ahead"] = np.broadcast_to((gj % NG < gj // NG).astype(np.float32), (P, NG * NG))
    c["e_spread"] = (p[:, None] % 32 == np.arange(NM * P) // 64).astype(np.float32)
    d = p % HD
    inv = (1.0 / 10000.0 ** (np.arange(0, HD, 2, dtype=np.float32) / np.float32(HD))).astype(np.float32)
    ang = (np.arange(T, dtype=np.float32)[None, :] * inv[d % 4][:, None]).astype(np.float32)
    c["cos"], c["sin"] = np.cos(ang), np.sin(ang)
    rot = np.zeros((P, P), np.float32)
    for f in range(P):
        if f % HD < 4:
            rot[f, f + 4] = -1.0
        else:
            rot[f, f - 4] = 1.0
    c["rotT"] = np.ascontiguousarray(rot.T)
    return c


def kernel(**inputs):
    import numpy as np
    import concourse.bacc as bacc
    from concourse.bass_utils import run_bass_kernel_spmd

    g = {k: np.asarray(v) for k, v in inputs.items()}
    parts = host_constants()

    def small_out(wT):
        return wT.reshape(NI, 2, 2, HD, D).transpose(0, 1, 3, 2, 4).reshape(T, 2 * D)

    qkv = g["L0_attn_w_qkv"]
    parts["w0_q"], parts["w0_k"], parts["w0_v"] = qkv[:D].T, qkv[D:2 * D].T, qkv[2 * D:].T
    parts["w0_bias"] = np.broadcast_to(g["L0_attn_b_proj"], (P, D))
    parts["w0_o"] = small_out(g["L0_attn_w_proj"].T)
    parts["x0_q"], parts["x0_qf"] = g["L0_xattn_Wq"], g["L0_xattn_Wq"].T
    parts["x0_k"], parts["x0_v"] = g["L0_xattn_Wkv"][:, :D], g["L0_xattn_Wkv"][:, D:]
    parts["x0_kf"] = parts["x0_k"].T
    parts["x0_o"] = small_out(g["L0_xattn_Wout"])
    for n in "qk":
        wt = g["L1_xattn_W" + n]
        parts["x1_" + n], parts["x1_" + n + "f"] = wt.T, wt
        parts["x1_b" + n] = g["L1_xattn_b" + n].reshape(D, 1)
    parts["x1_v"] = g["L1_xattn_Wv"].T
    parts["e_router"] = g["L0_ffn_Wg"].T
    parts["e_bias"] = np.broadcast_to(g["L0_ffn_bias_corr"], (P, NE))
    parts["e_w1"] = g["L0_ffn_W1"].reshape(NE * 64, D).T
    parts["e_w2"] = g["L0_ffn_W2"].transpose(0, 2, 1).reshape(NM, P, D).transpose(1, 0, 2).reshape(P, NM * D)
    parts["e_s1"], parts["e_s2"] = g["L0_ffn_Ws1"].T, g["L0_ffn_Ws2"].T

    def side_by_side(wt):
        return wt.reshape(-1, P, wt.shape[1]).transpose(1, 0, 2).reshape(P, -1)

    parts["q_w"] = np.concatenate([side_by_side(g["L1_ffn_w_gate"]), side_by_side(g["L1_ffn_w_up"]), g["L1_ffn_w_down"]], axis=1)
    parts["x1_bv"] = g["L1_xattn_bv"].reshape(D, 1)
    parts["x1_of"] = g["L1_xattn_Wo"].T
    parts["x1_bo"] = np.broadcast_to(g["L1_xattn_bo"], (P, D))

    def up(n):
        both = np.concatenate([g["L1_attn_W_" + n], g["L1_attn_b_" + n][None]], axis=0)
        return both.reshape(LC + 1, LH, D).transpose(2, 1, 0).reshape(D, LH * (LC + 1))

    def rows64(v):
        return np.concatenate([v, np.zeros((T - v.shape[0], v.shape[1]), np.float32)], axis=0)

    parts["l_dq"] = g["L1_attn_W_DQ"]
    parts["l_df"] = np.concatenate([g["L1_attn_W_DKV"], g["L1_attn_W_KR"]], axis=1)
    parts["l_uq"], parts["l_uk"] = up("UQ"), up("UK")
    parts["l_uv"] = g["L1_attn_W_UV"].reshape(LC, LH, D).transpose(2, 1, 0).reshape(D, LH * LC)
    parts["l_buv"] = g["L1_attn_b_UV"].reshape(LH, D).T
    parts["l_o"] = g["L1_attn_W_O"].reshape(LH, D, D).transpose(1, 0, 2).reshape(D, LH * D)
    parts["l_bo"] = np.broadcast_to(g["L1_attn_b_O"], (P, D))
    parts["l_qr"] = rows64(np.concatenate([g["L1_attn_W_QR"], g["L1_attn_b_QR"][None]], axis=0))
    parts["l_bq"] = rows64(g["L1_attn_b_DQ"][:, None])
    parts["l_bf"] = np.concatenate([g["L1_attn_b_DKV"], g["L1_attn_b_KR"]])[:, None]
    parts["l_bl"] = rows64(g["L1_attn_b_DKV"][None])
    parts["x1_o"] = small_out(g["L1_xattn_Wo"].T)

    def pack(cols):
        return np.concatenate([parts[n] for n, _ in cols], axis=1)

    arrays = {
        "x": g["x"].reshape(NSEQ * T, D),
        "ctxT": g["ctx_1024"].reshape(NSEQ * T, D).T.reshape(D, NSEQ, T),
        "mask": g["mask_BxS2_bf1"].reshape(1, NSEQ * T).view(np.uint8),
        "head": pack(HEAD_COLS), "body": pack(BODY_COLS), "row64": pack(ROW64_COLS),
    }
    arrays = {f"in_{k}": np.ascontiguousarray(v) for k, v in arrays.items()}
    nc = bacc.Bacc("TRN2", target_bir_lowering=False, num_devices=1)
    args = [nc.dram_tensor(k, v.shape, mybir.dt.from_np(v.dtype), kind="ExternalInput").ap() for k, v in arrays.items()]
    out = nc.dram_tensor("out", (NSEQ * T, D), F32, kind="ExternalOutput").ap()
    decoder(nc, *args, out)
    r = run_bass_kernel_spmd(nc, [arrays], core_ids=[0])
    return r.results[0]["out"].reshape(NSEQ, T, D)
```

```python
from contextlib import ExitStack

import concourse.bass as bass
from concourse import mybir

F32 = mybir.dt.float32
BF16 = mybir.dt.bfloat16
U8 = mybir.dt.uint8
ALU = mybir.AluOpType
ACT = mybir.ActivationFunctionType
AX = mybir.AxisListType

P = 128
D = 128
T = 64
NSEQ = 32
NT = NSEQ * T // P
SB = P // T
HD = 8
NI = 4
EPS = 1e-5
SMALL_SCALE = HD ** -0.5
BIG = 3.3895313892515355e38

PHASES = 5
PEEL = PHASES + 1
SLOTS = NT + PHASES - 1
PAIRS = (NT - PEEL) // 2


def run_slots(eng, slot):
    for s in range(PEEL):
        slot(s, s % 2)
    with eng.Fori(0, PAIRS) as i:
        for j in range(2):
            slot(i * 2 + (PEEL + j), (PEEL + j) % 2)
    for s in range(PEEL + 2 * PAIRS, SLOTS):
        slot(s, s % 2)


def has(s, phase):
    return not isinstance(s, int) or 0 <= s - phase < NT


def wait(eng, sem, value):
    if not isinstance(value, int) or value > 0:
        eng.wait_ge(sem, value)


class Turn:

    def __init__(self, at, cur):
        self.at, self.cur = at, cur

    def __call__(self, step, phase):
        if has(self.at, phase):
            step(self.at - phase, (self.cur + phase) % 2)


class Names:
    pass


class Stages:

    def __init__(self, nc):
        self.nc, self.last, self.spent = nc, [], []

    def semaphores(self, prefix, names):
        for h in self.spent:
            self.nc.release_semaphore(h)
        self.spent = self.last
        self.last = [self.nc.alloc_semaphore(prefix + n) for n in names.split()]
        return dict(zip(names.split(), self.last))

    def zero_spent(self, pool):
        nums = sorted(h.num for h in self.spent)
        while nums:
            run = 1
            while run < len(nums) and nums[run] == nums[0] + run:
                run += 1
            pool.sem_clear(range(nums[0], nums[0] + run))
            nums = nums[run:]



class TailNorm:

    def __init__(self, nc, m, s, bias_tile, y):
        self.nc, self.m, self.s, self.bias_tile, self.y = nc, m, s, bias_tile, y

    def add_bias(self, pool, t, par):
        wait(pool, self.s["r_done"], t - 1)
        self.nc.gpsimd.tensor_tensor(self.m.xb[:, par, :], self.m.X[:, t, :], self.bias_tile, ALU.add).then_inc(self.s["xb_ready"], 1)

    def residual(self, dve, t, par):
        s, m = self.s, self.m
        if self.bias_tile is not None:
            wait(dve, s["xb_ready"], t + 1)
        wait(dve, s["y_psum"], t + 1)
        wait(dve, s["x_new"], t)
        x = m.X[:, t, :] if self.bias_tile is None else m.xb[:, par, :]
        self.nc.vector.tensor_tensor(m.r[:, :], self.y, x, ALU.add).then_inc(s["r_done"], 1)

    def statistics(self, dve, t, par):
        dve.wait_ge(self.s["r_done"], t + 1)
        self.nc.vector.bn_stats(self.m.bn6[:, :], self.m.r[:, :]).then_inc(self.s["bn6_done"], 1)

    def variance(self, dve, t, par):
        dve.wait_ge(self.s["bn6_done"], 1)
        dve.wait_ge(self.s["bn6_done"], t + 1)
        self.nc.vector.bn_aggr(self.m.meanvar[:, :], self.m.bn6[:, :]).then_inc(self.s["var_ready"], 1)

    def log_variance(self, act, t, par):
        act.wait_ge(self.s["var_ready"], t + 1)
        wait(act, self.s["rstd_ready"], t)
        self.nc.scalar.activation(self.m.lnvar[:, :], self.m.meanvar[:, 1:2], ACT.Ln,
                                  bias=self.m.eps[:, 0:1]).then_inc(self.s["lnvar_done"], 1)

    def rstd(self, act, t, par):
        act.wait_ge(self.s["lnvar_done"], t + 1)
        wait(act, self.s["x_new"], t)
        self.nc.scalar.activation(self.m.rstd[:, :], self.m.lnvar[:, :], ACT.Exp, scale=-0.5).then_inc(self.s["rstd_ready"], 1)

    def apply(self, dve, t, par):
        m = self.m
        dve.wait_ge(self.s["rstd_ready"], t + 1)
        self.nc.vector.tensor_scalar(m.X[:, t, :], m.r[:, :], m.meanvar[:, 0:1], m.rstd[:, 0:1],
                                     ALU.subtract, ALU.mult).then_inc(self.s["x_new"], 1)


def stage_tiles(sp, m, s, with_context):
    def tile(t, par):
        wait(sp, s["xT_psum"], t - 1)
        sp.dma_start(m.xs[:, par, :], m.X[:, t, :]).then_inc(s["xs_load0"] if par == 0 else s["xs_load1"], 16)
        if with_context:
            wait(sp, s["v_psum"], t - 1)
            for a in range(2):
                sp.dma_start(m.kvT[:, par, :, a, :], m.ctxT_dram[:, bass.ds(t * SB, SB), :]).then_inc(s["kv_load0"] if par == 0 else s["kv_load1"], 16)
    for t in range(4):
        tile(t, t % 2)
    with sp.Fori(2, NT // 2) as i:
        tile(i * 2, 0)
        tile(i * 2 + 1, 1)



def small_attention(nc, m, w, kind, prefix):
    causal = kind == "causal"
    with ExitStack() as ctx:
        s = m.stages.semaphores(prefix,
                       "xs_load0 xs_load1 kv_load0 kv_load1 xb_ready xT_psum xT_ready qk_psum qk_ready v_psum rope_parts"
                       " qk_sum stat_ready mov_ready v_ready s_psum0 s_psum1 max_done0 max_done1 shifted0 shifted1"
                       " clamped0 clamped1 exp_done0 exp_done1 ln_done0 ln_done1 soft_done0 soft_done1"
                       " prob_ready0 prob_ready1 pT_psum0 pT_psum1 pT_ready0 pT_ready1 o_psum0 o_psum1 den_done rden_done"
                       " o_ready oT_psum oT_ready y_psum r_done bn6_done var_ready lnvar_done rstd_ready x_new")
        def sb(name, shape, dt=F32):
            return ctx.enter_context(nc.sbuf_tensor(prefix + name, shape, dt))

        m.rope = sb("rope", [P, 2, 2, 2, P])
        m.stat = sb("stat", [P, 2, SB, 4, T])
        m.mov = sb("mov", [P, 2, SB, NI, T])
        m.prob = sb("prob", [P, 2, SB, NI, 2, T])
        m.probT = sb("probT", [P, SB, NI, P])
        m.soft = sb("soft", [P, SB, 512])
        m.score = sb("score", [P, SB, 512])
        psS = [m.bank[0], m.bank[1]]
        psT = [m.bank[2], m.bank[3]]
        psQK, psXV, psO, psOY = m.bank[4], m.bank[5], m.bank[6], m.bank[7]
        psY = psOY[:, 256:384]
        tail = TailNorm(nc, m, s, w.bias_tile, psY)
        masked = not causal and w.mask_row is not None
        block = ctx.enter_context(nc.Block())

        @block.sync
        def _(sp):
            stage_tiles(sp, m, s, with_context=not causal)
            if causal:
                for name in ("mid", "mask", "body", "row64"):
                    sp.wait_ge(m.load[name], 16)

        @block.gpsimd
        def _(pool):
            m.stages.zero_spent(pool)

            def rope_sum(t, par):
                pool.wait_ge(s["rope_parts"], t + 1)
                wait(pool, s["mov_ready"], t - 1)
                nc.gpsimd.tensor_tensor(m.qk[:, par, :, :], m.rope[:, par, :, 0, :], m.rope[:, par, :, 1, :],
                                        ALU.add).then_inc(s["qk_sum"], 1)

            def mask_operand(t, par, out, which, mask, done):
                if causal:
                    pool.wait_ge(s["qk_ready"], t + 1)
                else:
                    pool.wait_ge(s["qk_sum"], t + 1)
                wait(pool, s["s_psum1"], t - 1)
                nc.gpsimd.tensor_tensor(
                    out[:, par, :, :, :],
                    m.qk[:, par, which, :].rearrange("p (b k) -> p b k", b=SB).unsqueeze(2).broadcast_to([P, SB, 4, T]),
                    mask.unsqueeze(1).unsqueeze(3).broadcast_to([P, SB, 4, T]), ALU.mult).then_inc(s[done], 1)

            def stationary(t, par):
                mask_operand(t, par, m.stat, 1 if causal else 0, m.mask_ca if causal else m.mask_ac, "stat_ready")

            def moving(t, par):
                mask_operand(t, par, m.mov, 0 if causal else 1, m.mask_i, "mov_ready")

            def square1(t, par):
                pool.wait_ge(s["soft_done1"], t + 1)
                wait(pool, s["o_psum1"], t - 1)
                soft = m.soft[:, 1, :].rearrange("p (c i q) -> p c i q", c=2, i=NI)
                nc.gpsimd.tensor_tensor(m.prob[:, par, 1, :, :, :].rearrange("p i c q -> p c i q"), soft, soft,
                                        ALU.mult).then_inc(s["prob_ready1"], 1)

            def add_bias(t, par):
                tail.add_bias(pool, t, par)

            def slot(at, cur):
                run = Turn(at, cur)
                if causal:
                    run(moving, 1), run(add_bias, 2), run(square1, 2), run(stationary, 0)
                else:
                    run(rope_sum, 0), run(stationary, 0), run(moving, 0)
                    if w.bias_tile is not None:
                        run(add_bias, 1)
            run_slots(pool, slot)
            if causal:
                pool.wait_ge(m.load["mask"], 16)
                nc.gpsimd.tensor_scalar(m.mask_row[:, :], m.mask_u8[:, :], 1.0, BIG, ALU.subtract, ALU.mult)

        @block.tensor
        def _(pe):
            def turn(t, par):
                pe.wait_ge(s["xs_load0"] if par == 0 else s["xs_load1"], 8 * (t - par) + 16)
                wait(pe, s["v_ready"], t)
                nc.tensor.transpose(psXV[:, 0:P], m.xs[:, par, :], m.ident).then_inc(s["xT_psum"], 1)

            def project(t, par):
                pe.wait_ge(s["xT_ready"], t + 1)
                xT = m.xT[:, par, :, 0, :]
                if causal:
                    wait(pe, s["qk_ready"], t)
                    parts = ((w.wq, xT), (w.wk, xT))
                else:
                    wait(pe, s["rope_parts"], t)
                    pe.wait_ge(s["kv_load0"] if par == 0 else s["kv_load1"], 16 * (t - par) + 32)
                    cT = m.kvT[:, par, :, 0, :]
                    parts = ((w.wq, xT), (w.wqr, xT), (w.wk, cT), (w.wkr, cT))
                for n, (wt, xT) in enumerate(parts):
                    mm = nc.tensor.matmul(psQK[:, n * P:(n + 1) * P], wt, xT, start=True, stop=True)
                mm.then_inc(s["qk_psum"], 1)

            def values(t, par):
                pe.wait_ge(s["xT_ready"], t + 1)
                if not causal:
                    pe.wait_ge(s["kv_load0"] if par == 0 else s["kv_load1"], 16 * (t - par) + 32)
                kvT = m.xT if causal else m.kvT
                for b in range(SB):
                    mm = nc.tensor.matmul(psXV[:, 256 + b * P:256 + (b + 1) * P], kvT[:, par, b, :, :], w.wv, start=True, stop=True)
                mm.then_inc(s["v_psum"], 1)

            def scores(t, par, b):
                pe.wait_ge(s["stat_ready"], t + 1)
                pe.wait_ge(s["mov_ready"], t + 1)
                wait(pe, s[f"shifted{b}"], t)
                if masked:
                    nc.tensor.matmul(psS[b][:, :], m.ones_bf[0:1, :],
                                     w.mask_row[0:1, bass.ds(t * P + b * T, T)].unsqueeze(1).broadcast_to([1, 8, T]),
                                     start=True, stop=False, skip_group_check=True)
                for half in range(2):
                    mm = nc.tensor.matmul(psS[b][:, 256 * half:256 * half + 256], m.stat[:, par, b, 2 * half:2 * half + 2, :],
                                          m.mov[:, par, b, :, :], start=not masked, stop=True, skip_group_check=masked)
                mm.then_inc(s[f"s_psum{b}"], 1)

            def scores0(t, par):
                scores(t, par, 0)

            def scores1(t, par):
                scores(t, par, 1)

            def turn_probs(t, par, b):
                wait(pe, s[f"pT_ready{b}"], t)
                pe.wait_ge(s[f"exp_done{b}"], t + 1)
                for i in range(NI):
                    mm = nc.tensor.transpose(psT[b][:, i * P:(i + 1) * P], m.prob[:, par, b, i, :, :], m.ident)
                mm.then_inc(s[f"pT_psum{b}"], 1)

            def turn_probs0(t, par):
                turn_probs(t, par, 0)

            def turn_probs1(t, par):
                turn_probs(t, par, 1)

            def outputs(t, par, b):
                wait(pe, s["o_ready"], t)
                pe.wait_ge(s["v_ready"], t + 1)
                pe.wait_ge(s[f"prob_ready{b}" if causal else f"pT_ready{b}"], t + 1)
                for i in range(NI):
                    lhsT = m.prob[:, par, b, i, :, :] if causal else m.probT[:, b, i, :]
                    at = 36 * (NI * b + i)
                    mm = nc.tensor.matmul(psO[:, at:at + 36], lhsT, m.vals[:, par, b, i, :, :, :], start=True, stop=True)
                mm.then_inc(s[f"o_psum{b}"], 1)

            def outputs0(t, par):
                outputs(t, par, 0)

            def outputs1(t, par):
                outputs(t, par, 1)

            def turn_outputs(t, par):
                wait(pe, s["r_done"], t)
                pe.wait_ge(s["o_ready"], t + 1)
                nc.tensor.transpose(psOY[:, 0:P], m.o[:, par, :, :], m.ident).then_inc(s["oT_psum"], 1)

            def project_outputs(t, par):
                pe.wait_ge(s["oT_ready"], t + 1)
                nc.tensor.matmul(psY, m.oT[:, 0, :], w.wo, start=True, stop=True).then_inc(s["y_psum"], 1)

            def slot(at, cur):
                run = Turn(at, cur)
                if causal:
                    run(turn, 0), run(scores1, 1), run(project_outputs, 3), run(project, 0), run(outputs0, 2)
                    run(outputs1, 2), run(values, 0), run(scores0, 0), run(turn_outputs, 2)
                else:
                    run(turn, 0), run(scores0, 1), run(outputs1, 2), run(project, 0), run(scores1, 1), run(turn_probs0, 1)
                    run(values, 0), run(turn_outputs, 2), run(outputs0, 1), run(project_outputs, 2), run(turn_probs1, 1)
            run_slots(pe, slot)

        @block.scalar
        def _(act):
            act.preload_act_table_set("natural_log_exp_and_others")

            def copy_turned(t, par):
                act.wait_ge(s["xT_psum"], t + 1)
                wait(act, s["qk_psum"], t - 1)
                wait(act, s["v_psum"], t - 1)
                nc.scalar.activation(m.xT[:, par, :, :, :],
                                     psXV[:, 0:P].rearrange("p (b k) -> p b k", b=SB).unsqueeze(2).broadcast_to([P, SB, 2, T]),
                                     ACT.Copy).then_inc(s["xT_ready"], 1)

            def copy_qk(t, par):
                act.wait_ge(s["qk_psum"], t + 1)
                wait(act, s["mov_ready"], t - 1)
                nc.scalar.activation(m.qk[:, par, :, :], psQK[:, 0:256].rearrange("p (x t) -> p x t", x=2),
                                     ACT.Copy).then_inc(s["qk_ready"], 1)

            def copy_values(t, par):
                act.wait_ge(s["v_psum"], t + 1)
                wait(act, s["o_psum1"], t - 1)
                for a in range(2):
                    half = slice(a * T, a * T + T)
                    op = nc.scalar.activation(
                        m.vals[half, par, :, :, a, :, 0:HD].rearrange("p b i c d -> p (b i) c d"),
                        psXV[half, 256:512].rearrange("p (bi a c d) -> p bi a c d", a=2, c=2, d=HD)[:, :, a, :, :],
                        ACT.Copy)
                op.then_inc(s["v_ready"], 1)

            def exponential(t, par, b):
                sc = m.prob[:, par, b, :, :, :].rearrange("p i a k -> p (i a k)")
                if causal:
                    act.wait_ge(s[f"clamped{b}"], t + 1)
                    nc.scalar.activation(m.soft[:, b, :], m.soft[:, b, :], ACT.Exp).then_inc(s[f"exp_done{b}"], 1)
                else:
                    act.wait_ge(s[f"shifted{b}"], t + 1)
                    nc.scalar.activation(sc, sc, ACT.Exp, scale=SMALL_SCALE).then_inc(s[f"exp_done{b}"], 1)

            def exponential0(t, par):
                exponential(t, par, 0)

            def exponential1(t, par):
                exponential(t, par, 1)

            def log_one_plus(t, par, b):
                act.wait_ge(s[f"exp_done{b}"], t + 1)
                nc.scalar.activation(m.soft[:, b, :], m.soft[:, b, :], ACT.Ln, bias=m.one[:, 0:1]).then_inc(s[f"ln_done{b}"], 1)

            def log_one_plus0(t, par):
                log_one_plus(t, par, 0)

            def log_one_plus1(t, par):
                log_one_plus(t, par, 1)

            def square0(t, par):
                act.wait_ge(s["soft_done0"], t + 1)
                wait(act, s["o_psum0"], t - 1)
                nc.scalar.activation(m.prob[:, par, 0, :, :, :].rearrange("p i c q -> p c i q"),
                                     m.soft[:, 0, :].rearrange("p (c i q) -> p c i q", c=2, i=NI), ACT.Square).then_inc(s["prob_ready0"], 1)

            def copy_probs(t, par, b):
                act.wait_ge(s[f"pT_psum{b}"], t + 1)
                wait(act, s[f"o_psum{b}"], t)
                nc.scalar.activation(m.probT[:, b, :, :].rearrange("p i q -> p (i q)"), psT[b][:, :],
                                     ACT.Copy).then_inc(s[f"pT_ready{b}"], 1)

            def copy_probs0(t, par):
                copy_probs(t, par, 0)

            def copy_probs1(t, par):
                copy_probs(t, par, 1)

            def copy_outputs(t, par):
                act.wait_ge(s["oT_psum"], t + 1)
                wait(act, s["y_psum"], t)
                for b in range(SB):
                    for c in range(2):
                        op = nc.scalar.activation(m.oT[c * T:(c + 1) * T, 0, b * T:(b + 1) * T],
                                                  psOY[b * T:(b + 1) * T, c * T:(c + 1) * T], ACT.Copy)
                op.then_inc(s["oT_ready"], 1)

            def log_variance(t, par):
                tail.log_variance(act, t, par)

            def rstd(t, par):
                tail.rstd(act, t, par)

            def slot(at, cur):
                run = Turn(at, cur)
                if causal:
                    run(copy_turned, 0), run(copy_qk, 0), run(exponential0, 1), run(log_one_plus0, 1), run(exponential1, 1)
                    run(log_variance, 3), run(log_one_plus1, 1), run(copy_values, 0), run(rstd, 3), run(square0, 1)
                    run(copy_outputs, 2)
                else:
                    run(rstd, 4), run(exponential1, 2), run(copy_values, 1), run(copy_probs1, 2), run(copy_turned, 0)
                    run(exponential0, 1), run(copy_probs0, 1), run(log_variance, 3), run(copy_outputs, 2)
            run_slots(act, slot)

        @block.vector
        def _(dve):
            def scale_and_mask(t, par, b):
                dve.wait_ge(s[f"s_psum{b}"], t + 1)
                wait(dve, s[f"soft_done{b}"], t)
                nc.vector.scalar_tensor_tensor(
                    out=m.score[:, b, :].rearrange("p (x k) -> p x k", k=T), in0=psS[b][:, :].rearrange("p (x k) -> p x k", k=T),
                    scalar=SMALL_SCALE, in1=m.causal.unsqueeze(1).broadcast_to([P, 8, T]),
                    op0=ALU.mult, op1=ALU.add).then_inc(s[f"shifted{b}"], 1)

            def clamp(t, par, b):
                dve.wait_ge(s[f"shifted{b}"], t + 1)
                wait(dve, s[f"prob_ready{b}"], t)
                nc.vector.tensor_scalar(m.soft[:, b, :], m.score[:, b, :], 40.0, None, ALU.min).then_inc(s[f"clamped{b}"], 1)

            def softplus(t, par, b):
                dve.wait_ge(s[f"ln_done{b}"], t + 1)
                nc.vector.tensor_tensor(m.soft[:, b, :], m.soft[:, b, :], m.score[:, b, :], ALU.max).then_inc(s[f"soft_done{b}"], 1)

            def maximum(t, par, b):
                dve.wait_ge(s[f"s_psum{b}"], t + 1)
                wait(dve, s[f"shifted{b}"], t)
                nc.vector.tensor_reduce(m.rowmax[:, b, :], psS[b][:, :].rearrange("p (x k) -> p x k", k=T), AX.X,
                                        ALU.max).then_inc(s[f"max_done{b}"], 1)

            def less_maximum(t, par, b):
                dve.wait_ge(s[f"max_done{b}"], t + 1)
                wait(dve, s[f"pT_psum{b}"], t - 1)
                nc.vector.tensor_tensor(m.prob[:, par, b, :, :, :].rearrange("p i a k -> p a i k"),
                                        psS[b][:, :].rearrange("p (a i k) -> p a i k", a=2, i=NI),
                                        m.rowmax[:, b, :].rearrange("p (a i) -> p a i", a=2).unsqueeze(3)
                                        .broadcast_to([P, 2, NI, T]),
                                        ALU.subtract).then_inc(s[f"shifted{b}"], 1)

            def scale_and_mask0(t, par):
                scale_and_mask(t, par, 0)

            def scale_and_mask1(t, par):
                scale_and_mask(t, par, 1)

            def clamp0(t, par):
                clamp(t, par, 0)

            def clamp1(t, par):
                clamp(t, par, 1)

            def softplus0(t, par):
                softplus(t, par, 0)

            def softplus1(t, par):
                softplus(t, par, 1)

            def maximum0(t, par):
                maximum(t, par, 0)

            def maximum1(t, par):
                maximum(t, par, 1)

            def less_maximum0(t, par):
                less_maximum(t, par, 0)

            def less_maximum1(t, par):
                less_maximum(t, par, 1)

            def rotate(t, par):
                dve.wait_ge(s["qk_psum"], t + 1)
                wait(dve, s["qk_sum"], t - 1)
                for n, (bias, table) in enumerate(((w.bq, m.cos), (w.bqr, m.sin), (w.bk, m.cos), (w.bkr, m.sin))):
                    op = nc.vector.scalar_tensor_tensor(
                        out=m.rope[:, par, n // 2, n % 2, :].rearrange("p (b t) -> p b t", b=SB),
                        in0=psQK[:, n * P:(n + 1) * P].rearrange("p (b t) -> p b t", b=SB),
                        scalar=bias, in1=table.unsqueeze(1).broadcast_to([P, SB, T]), op0=ALU.add, op1=ALU.mult)
                op.then_inc(s["rope_parts"], 1)

            o = psO[:, 0:288].rearrange("p (bia c e) -> p bia c e", c=2, e=HD + 1)
            halves = (slice(0, T), slice(T, P))

            def denominators(t, par):
                for b in range(SB):
                    dve.wait_ge(s[f"o_psum{b}"], t + 1)
                wait(dve, s["rden_done"], t)
                for c in range(2):
                    op = nc.vector.tensor_scalar(m.den[halves[c], :], o[halves[c], :, c, HD], 1e-9, None, ALU.add)
                op.then_inc(s["den_done"], 1)

            def reciprocals(t, par):
                wait(dve, s["o_ready"], t)
                if causal:
                    dve.wait_ge(s["den_done"], t + 1)
                    nc.vector.reciprocal(m.rden[:, :], m.den[:, :]).then_inc(s["rden_done"], 1)
                else:
                    for b in range(SB):
                        dve.wait_ge(s[f"o_psum{b}"], t + 1)
                    for c in range(2):
                        op = nc.vector.reciprocal(m.rden[halves[c], :], o[halves[c], :, c, HD])
                    op.then_inc(s["rden_done"], 1)

            def normalise(t, par):
                dve.wait_ge(s["rden_done"], t + 1)
                wait(dve, s["oT_psum"], t - 1)
                for c in range(2):
                    op = nc.vector.tensor_tensor(
                        m.o[halves[c], par, :, :].rearrange("p b (ia d) -> p (b ia) d", d=HD), o[halves[c], :, c, 0:HD],
                        m.rden[halves[c], :].unsqueeze(2).broadcast_to([T, 16, HD]), ALU.mult)
                op.then_inc(s["o_ready"], 1)

            def residual(t, par):
                tail.residual(dve, t, par)

            def statistics(t, par):
                tail.statistics(dve, t, par)

            def variance(t, par):
                tail.variance(dve, t, par)

            def apply(t, par):
                tail.apply(dve, t, par)

            def slot(at, cur):
                run = Turn(at, cur)
                if causal:
                    run(softplus1, 1), run(apply, 3), run(scale_and_mask0, 0), run(clamp0, 0), run(residual, 2)
                    run(scale_and_mask1, 0), run(statistics, 2), run(variance, 2), run(clamp1, 0)
                    run(denominators, 1), run(reciprocals, 1), run(normalise, 1), run(softplus0, 0)
                else:
                    run(maximum0, 1), run(less_maximum0, 1), run(reciprocals, 2), run(rotate, 0), run(normalise, 2)
                    run(variance, 3), run(maximum1, 1), run(less_maximum1, 1), run(apply, 3), run(residual, 2)
                    run(statistics, 2)
            run_slots(dve, slot)



LH, LC, LR = 8, 32, 32
LF = LC + LR + 1
LATENT_SCALE = (D + LR) ** -0.5


def latent_attention(nc, m, w, prefix):
    with ExitStack() as ctx:
        s = m.stages.semaphores(prefix,
                       "blocks xs_load0 xs_load1 xb_ready xT_psum xT_ready low_psum q_ready f_ready v_ready g_psum0 g_psum1"
                       " g_ready0 g_ready1 s_psum max_done shifted exp_done pT_psum pT_ready o_psum rden_done o_ready"
                       " oT_psum oT_ready y_psum r_done bn6_done var_ready lnvar_done rstd_ready x_new")
        psS = [m.bank[0], m.bank[1]]
        psG = [m.bank[2], m.bank[3]]
        psT, psXV, psO, psOY = m.bank[4], m.bank[5], m.bank[6], m.bank[7]
        psY = psOY[:, 256:384]
        tail = TailNorm(nc, m, s, w.bias_tile, psY)
        block = ctx.enter_context(nc.Block())

        @block.sync
        def _(sp):
            stage_tiles(sp, m, s, with_context=False)

        @block.gpsimd
        def _(pool):
            m.stages.zero_spent(pool)

            def add_bias(t, par):
                tail.add_bias(pool, t, par)

            def slot(at, cur):
                run = Turn(at, cur)
                run(add_bias, 1)
            run_slots(pool, slot)

        @block.tensor
        def _(pe):
            def turn(t, par):
                pe.wait_ge(s["xs_load0"] if par == 0 else s["xs_load1"], 8 * (t - par) + 16)
                wait(pe, s["q_ready"], t)
                wait(pe, s["f_ready"], t)
                wait(pe, s["v_ready"], t)
                nc.tensor.transpose(psXV[:, 0:P], m.xs[:, par, :], m.ident).then_inc(s["xT_psum"], 1)

            def low_rank(t, par):
                pe.wait_ge(s["xT_ready"], t + 1)
                xT = m.xT[:, par, :, 0, :]
                nc.tensor.matmul(psXV[0:LC, 128:256], w.dq, xT, start=True, stop=True)
                nc.tensor.matmul(psXV[0:LC + LR, 256:384], w.df, xT, start=True, stop=True)
                for b in range(SB):
                    mm = nc.tensor.matmul(psXV[:, 384 + b * LC:384 + (b + 1) * LC], m.xT[:, par, b, :, :], w.df[:, 0:LC],
                                          start=True, stop=True)
                mm.then_inc(s["low_psum"], 1)

            def queries(t, par, half):
                pe.wait_ge(s["q_ready"], t + 1)
                wait(pe, s[f"g_ready{half}"], t)
                for h in range(4):
                    mm = nc.tensor.matmul(psG[half][:, h * P:(h + 1) * P], w.score[:, 4 * half + h, :],
                                          m.cq[:, par, :], start=True, stop=True)
                mm.then_inc(s[f"g_psum{half}"], 1)

            def queries0(t, par):
                queries(t, par, 0)

            def queries1(t, par):
                queries(t, par, 1)

            def scores(t, par):
                pe.wait_ge(s["g_ready0"], t + 1)
                pe.wait_ge(s["g_ready1"], t + 1)
                pe.wait_ge(s["f_ready"], t + 1)
                wait(pe, s["shifted"], t - 1)
                for b in range(SB):
                    for ia in range(4):
                        mm = nc.tensor.matmul(psS[par][:, (4 * b + ia) * T:(4 * b + ia + 1) * T],
                                              m.g[:, par, b, 2 * ia:2 * ia + 2, :], m.f[:, par, b * T:(b + 1) * T],
                                              start=True, stop=True)
                mm.then_inc(s["s_psum"], 1)

            def turn_probs(t, par):
                wait(pe, s["pT_ready"], t)
                pe.wait_ge(s["exp_done"], t + 1)
                for b in range(SB):
                    for i in range(2):
                        mm = nc.tensor.transpose(psT[:, (2 * b + i) * P:(2 * b + i + 1) * P],
                                                 m.lprob[:, par, b, i, :], m.ident)
                mm.then_inc(s["pT_psum"], 1)

            def outputs(t, par):
                wait(pe, s["o_ready"], t)
                pe.wait_ge(s["pT_ready"], t + 1)
                pe.wait_ge(s["v_ready"], t + 1)
                for b in range(SB):
                    for i in range(2):
                        n = 2 * b + i
                        mm = nc.tensor.matmul(psO[:, n * 66:(n + 1) * 66], m.lprobT[:, n * P:(n + 1) * P],
                                              m.lvals[:, par, b, :, :], start=True, stop=True)
                mm.then_inc(s["o_psum"], 1)

            def turn_outputs(t, par):
                wait(pe, s["r_done"], t)
                pe.wait_ge(s["o_ready"], t + 1)
                for b in range(SB):
                    mm = nc.tensor.transpose(psOY[:, b * P:(b + 1) * P], m.lo[:, par, b, :], m.ident)
                mm.then_inc(s["oT_psum"], 1)

            def project_outputs(t, par):
                pe.wait_ge(s["oT_ready"], t + 1)
                for c in range(2):
                    mm = nc.tensor.matmul(psY, m.oT[:, c, :], w.out[:, c, :], start=(c == 0), stop=(c == 1))
                mm.then_inc(s["y_psum"], 1)

            def slot(at, cur):
                run = Turn(at, cur)
                run(turn, 0), run(outputs, 2), run(scores, 1), run(turn_outputs, 2), run(low_rank, 0)
                run(project_outputs, 2), run(queries1, 0), run(turn_probs, 1), run(queries0, 0)
            run_slots(pe, slot)

        @block.scalar
        def _(act):
            act.preload_act_table_set("natural_log_exp_and_others")

            def copy_turned(t, par):
                act.wait_ge(s["xT_psum"], t + 1)
                wait(act, s["low_psum"], t - 1)
                nc.scalar.activation(m.xT[:, par, :, :, :],
                                     psXV[:, 0:P].rearrange("p (b k) -> p b k", b=SB).unsqueeze(2).broadcast_to([P, SB, 2, T]),
                                     ACT.Copy).then_inc(s["xT_ready"], 1)

            def copy_cq(t, par):
                act.wait_ge(s["low_psum"], t + 1)
                wait(act, s["g_psum0"], t - 1)
                wait(act, s["g_psum1"], t - 1)
                nc.scalar.activation(m.cq[0:LC, par, :], psXV[0:LC, 128:256], ACT.Identity,
                                     bias=w.b_q).then_inc(s["q_ready"], 1)

            def copy_features(t, par):
                act.wait_ge(s["low_psum"], t + 1)
                wait(act, s["s_psum"], t - 1)
                nc.scalar.activation(m.f[0:LC + LR, par, :], psXV[0:LC + LR, 256:384], ACT.Identity,
                                     bias=w.b_f).then_inc(s["f_ready"], 1)

            def copy_latents(t, par):
                act.wait_ge(s["low_psum"], t + 1)
                wait(act, s["o_psum"], t - 1)
                for a in range(2):
                    half = slice(a * T, a * T + T)
                    op = nc.scalar.activation(m.lvals[half, par, :, a, 0:LC],
                                              psXV[half, 384:448].rearrange("p (b l) -> p b l", b=SB), ACT.Copy)
                op.then_inc(s["v_ready"], 1)

            def copy_queries(t, par, half):
                act.wait_ge(s[f"g_psum{half}"], t + 1)
                wait(act, s["s_psum"], t - 1)
                nc.scalar.activation(m.g[:, par, :, 4 * half:4 * half + 4, :].rearrange("p b h q -> p h b q"),
                                     psG[half][:, :].rearrange("p (h b q) -> p h b q", h=4, b=SB),
                                     ACT.Copy).then_inc(s[f"g_ready{half}"], 1)

            def copy_queries0(t, par):
                copy_queries(t, par, 0)

            def copy_queries1(t, par):
                copy_queries(t, par, 1)

            def exponential(t, par):
                act.wait_ge(s["shifted"], t + 1)
                sc = m.lprob[:, par, :, :, :].rearrange("p b i k -> p (b i k)")
                nc.scalar.activation(sc, sc, ACT.Exp, scale=LATENT_SCALE).then_inc(s["exp_done"], 1)

            def copy_outputs(t, par):
                act.wait_ge(s["oT_psum"], t + 1)
                wait(act, s["y_psum"], t)
                nc.scalar.activation(m.oT[:, :, :].rearrange("p c (b q) -> p c b q", b=SB),
                                     psOY[:, 0:256].rearrange("p (b c q) -> p c b q", b=SB, c=2),
                                     ACT.Copy).then_inc(s["oT_ready"], 1)

            def log_variance(t, par):
                tail.log_variance(act, t, par)

            def rstd(t, par):
                tail.rstd(act, t, par)

            def slot(at, cur):
                run = Turn(at, cur)
                run(copy_turned, 0), run(log_variance, 3), run(copy_outputs, 2), run(rstd, 3), run(copy_cq, 0)
                run(exponential, 1), run(copy_queries1, 0), run(copy_features, 0), run(copy_latents, 0), run(copy_queries0, 0)
            run_slots(act, slot)

        @block.vector
        def _(dve):
            link = Chain(dve, s["blocks"]).link
            by_block = lambda a: a.unsqueeze(2).broadcast_to([P, 36, 32])
            raw = w.q_w.rearrange("p (x k) -> p x k", k=32)
            link(nc.vector.tensor_reduce(m.qw_i[:, :], raw, AX.X, ALU.max, apply_absolute_value=True))
            link(nc.vector.tensor_scalar(m.qw_s[:, :], m.qw_i[:, :], 1.0 / 7.0, 1e-12, ALU.mult, ALU.max))
            link(nc.vector.reciprocal(m.qw_i[:, :], m.qw_s[:, :]))
            link(nc.vector.tensor_tensor(m.qw[:, :, :], raw, by_block(m.qw_i[:, :]), ALU.mult))
            link(nc.vector.tensor_scalar(m.qw[:, :, :], m.qw[:, :, :], MAGIC, MAGIC, ALU.add, ALU.subtract))
            nc.vector.tensor_tensor(m.qw[:, :, :], m.qw[:, :, :], by_block(m.qw_s[:, :]), ALU.mult)

            def maximum(t, par):
                dve.wait_ge(s["s_psum"], t + 1)
                wait(dve, s["shifted"], t)
                nc.vector.tensor_reduce(m.rowmax[:, 0, :], psS[par][:, :].rearrange("p (x k) -> p x k", k=T), AX.X,
                                        ALU.max).then_inc(s["max_done"], 1)

            def less_maximum(t, par):
                dve.wait_ge(s["max_done"], t + 1)
                wait(dve, s["pT_psum"], t - 1)
                nc.vector.tensor_tensor(m.lprob[:, par, :, :, :].rearrange("p b i (a k) -> p (b i a) k", k=T),
                                        psS[par][:, :].rearrange("p (x k) -> p x k", k=T),
                                        m.rowmax[:, 0, :].unsqueeze(2).broadcast_to([P, 8, T]),
                                        ALU.subtract).then_inc(s["shifted"], 1)

            def copy_probs(t, par):
                dve.wait_ge(s["pT_psum"], t + 1)
                wait(dve, s["o_psum"], t)
                nc.vector.tensor_copy(m.lprobT[:, :], psT[:, :]).then_inc(s["pT_ready"], 1)

            o = psO[:, 0:264].rearrange("p (x e) -> p x e", e=LC + 1)

            def reciprocals(t, par):
                dve.wait_ge(s["o_psum"], t + 1)
                wait(dve, s["o_ready"], t)
                nc.vector.reciprocal(m.rden[:, 0:8], o[:, :, LC]).then_inc(s["rden_done"], 1)

            def normalise(t, par):
                dve.wait_ge(s["rden_done"], t + 1)
                wait(dve, s["oT_psum"], t - 1)
                nc.vector.tensor_tensor(m.lo[:, par, :, :].rearrange("p b (x l) -> p (b x) l", l=LC), o[:, :, 0:LC],
                                        m.rden[:, 0:8].unsqueeze(2).broadcast_to([P, 8, LC]),
                                        ALU.mult).then_inc(s["o_ready"], 1)

            def residual(t, par):
                tail.residual(dve, t, par)

            def statistics(t, par):
                tail.statistics(dve, t, par)

            def variance(t, par):
                tail.variance(dve, t, par)

            def apply(t, par):
                tail.apply(dve, t, par)

            def slot(at, cur):
                run = Turn(at, cur)
                run(less_maximum, 1), run(apply, 3), run(residual, 2), run(statistics, 2)
                run(copy_probs, 1), run(reciprocals, 1), run(variance, 2), run(normalise, 1), run(maximum, 0)
            run_slots(dve, slot)



NE, NG, TOPG, TOPK = 16, 4, 2, 4
NM = NE // 2
CH = 512
NC = NSEQ * T // CH
CT = CH // P
CW = 128


class Chain:

    def __init__(self, eng, sem):
        self.eng, self.sem, self.n = eng, sem, 0

    def link(self, op):
        op.then_inc(self.sem, 1)
        self.n += 1
        self.eng.wait_ge(self.sem, self.n)


def experts(nc, m, w, prefix):
    with ExitStack() as ctx:
        s = m.stages.semaphores(prefix,
                       "constants made_psum made_copied bias_psum bias_copied xT_psum xT_ready logit_psum exp_ready route cw_ready cwT_psum cwT_ready z_psum gate_psum relu_ready"
                       " gated hid_ready y_psum r_done var_ready ln_done rstd_ready x_new")
        psX, psL, psC = m.bank[0], m.bank[1], m.bank[2]
        psZ, psW, psY = [m.bank[3], m.bank[4]], [m.bank[5], m.bank[6]], m.bank[7]
        block = ctx.enter_context(nc.Block())
        MM = NM + 1

        @block.tensor
        def _(pe):
            def turn(c):
                wait(pe, s["xT_ready"], c)
                for t in range(CT):
                    mm = nc.tensor.transpose(psX[:, t * P:(t + 1) * P], m.X[:, CT * c + t, :], m.ident)
                mm.then_inc(s["xT_psum"], 1)

            def logits(c):
                pe.wait_ge(s["xT_ready"], c + 1)
                for t in range(CT):
                    mm = nc.tensor.matmul(psL[:, t * NE:(t + 1) * NE], m.xTc[:, c % 2, t * P:(t + 1) * P], w.router,
                                          start=True, stop=True)
                mm.then_inc(s["logit_psum"], 1)

            def turn_weights(c):
                pe.wait_ge(s["cw_ready"], c + 1)
                pe.wait_ge(s["constants"], 1)
                wait(pe, s["cwT_ready"], c)
                ps = psC[:, :].bitcast(BF16)
                for t in range(CT):
                    mm = nc.tensor.transpose(ps[0:CW, t * P:(t + 1) * P], m.cw3[:, t, :], m.ident_bf[:, :])
                mm.then_inc(s["cwT_psum"], 1)

            def hidden(c, j):
                n = MM * c + j
                wait(pe, s["relu_ready"], n - 1)
                w1 = w.w1[:, j * P:(j + 1) * P] if j < NM else w.shared1
                nc.tensor.matmul(psZ[n % 2][:, :], w1, m.xTc[:, c % 2, :], start=True, stop=True).then_inc(s["z_psum"], 1)
                if j < NM:
                    g = NM * c + j
                    if j == 0:
                        pe.wait_ge(s["cwT_ready"], c + 1)
                    wait(pe, s["gated"], g - 1)
                    nc.tensor.matmul(psW[g % 2][:, :], m.spread[:, j, :], m.cwT[:, c % 2, :],
                                     start=True, stop=True).then_inc(s["gate_psum"], 1)

            def down(c, j):
                n = MM * c + j
                pe.wait_ge(s["hid_ready"], n + 1)
                if j == 0:
                    wait(pe, s["r_done"], c)
                w2 = w.w2[:, j * D:(j + 1) * D] if j < NM else w.shared2
                for t in range(CT):
                    mm = nc.tensor.matmul(psY[:, t * D:(t + 1) * D], m.hid[:, n % 2, t * P:(t + 1) * P], w2,
                                          start=(j == 0 and t == 0), stop=(j == MM - 1), skip_group_check=True)
                mm.then_inc(s["y_psum"], 1)

            def prepare():
                b_score, b_out, b_bias = m.bank[3], m.bank[4], m.bank[5]
                for hh in range(LH):
                    nc.tensor.matmul(b_score[0:LC + 1, hh * (LC + 1):(hh + 1) * (LC + 1)], w.uq[:, hh, :], w.uk[:, hh, :],
                                     start=True, stop=True)
                for hh in range(LH):
                    row, c = LC * (hh // 2), hh % 2
                    mm = nc.tensor.matmul(b_out[row:row + LC, c * D:(c + 1) * D], w.uv[:, hh, :], w.up_o[:, hh, :],
                                          start=True, stop=True)
                mm.then_inc(s["made_psum"], 1)
                to_all = m.ones_row[0:1, :]
                nc.tensor.matmul(b_bias[:, D:2 * D], w.x1_bv.broadcast_to([P, P]), w.x1_o, start=True, stop=False)
                nc.tensor.matmul(b_bias[:, D:2 * D], to_all, w.x1_bo, start=False, stop=True)
                for hh in range(LH):
                    nc.tensor.matmul(b_bias[:, 0:D], w.buv[:, hh:hh + 1].broadcast_to([P, P]), w.up_o[:, hh, :],
                                     start=(hh == 0), stop=False)
                nc.tensor.matmul(b_bias[:, 0:D], to_all, w.l_bo, start=False, stop=False)
                pe.wait_ge(s["made_copied"], 1)
                for c in range(2):
                    mm = nc.tensor.matmul(b_bias[:, 0:D], w.b_latent.broadcast_to([P, P]), m.l_out[:, c, :],
                                          start=False, stop=(c == 1))
                mm.then_inc(s["bias_psum"], 1)

            turn(0)
            logits(0)
            prepare()
            turn_weights(0)
            pe.wait_ge(s["bias_copied"], 1)
            for c in range(NC):
                for j in range(MM + 2):
                    if j < MM:
                        hidden(c, j)
                    if j >= 2:
                        down(c, j - 2)
                    if c + 1 < NC:
                        if j == 0:
                            turn(c + 1)
                        if j == 1:
                            logits(c + 1)
                        if j == MM:
                            turn_weights(c + 1)

        @block.scalar
        def _(act):
            act.preload_act_table_set("natural_log_exp_and_others")

            def copy_turned(c):
                act.wait_ge(s["xT_psum"], c + 1)
                wait(act, s["z_psum"], MM * (c - 1))
                nc.scalar.activation(m.xTc[:, c % 2, :], psX[:, :], ACT.Copy).then_inc(s["xT_ready"], 1)

            def exponentials(c):
                act.wait_ge(s["logit_psum"], c + 1)
                wait(act, s["cw_ready"], c)
                nc.scalar.activation(m.route_e[:, :], psL[:, 0:CT * NE], ACT.Exp, scale=-1.0).then_inc(s["exp_ready"], 1)

            def copy_weights(c):
                act.wait_ge(s["cwT_psum"], c + 1)
                wait(act, s["gate_psum"], NM * (c - 1))
                nc.scalar.activation(m.cwT[0:CW, c % 2, :], psC[:, :].bitcast(BF16)[0:CW, 0:CH], ACT.Copy).then_inc(s["cwT_ready"], 1)

            def rstd(c):
                act.wait_ge(s["var_ready"], c + 1)
                nc.scalar.activation(m.lnvar4[:, :], m.meanvar4[:, :, 1], ACT.Ln, bias=m.eps[:, 0:1]).then_inc(s["ln_done"], 1)
                act.wait_ge(s["ln_done"], c + 1)
                nc.scalar.activation(m.rstd4[:, :], m.lnvar4[:, :], ACT.Exp, scale=-0.5).then_inc(s["rstd_ready"], 1)

            copy_turned(0)
            exponentials(0)
            nc.scalar.activation(m.ident_bf[:, :], m.ident, ACT.Copy)
            nc.scalar.activation(m.spread[:, :, :].rearrange("p j q -> p (j q)"), w.spread, ACT.Copy).then_inc(s["constants"], 1)
            act.wait_ge(s["made_psum"], 1)
            nc.scalar.activation(m.l_out[:, :, :].rearrange("p c o -> p (c o)"), m.bank[4][:, 0:2 * D], ACT.Copy).then_inc(s["made_copied"], 1)
            made = m.bank[3][0:LC + 1, 0:LH * (LC + 1)].rearrange("p (h l) -> p h l", h=LH)
            nc.scalar.activation(m.l_score[0:LC + 1, :, 0:LC], made[:, :, 0:LC], ACT.Copy)
            nc.scalar.activation(m.l_score[0:LC + 1, :, LC + LR:LF], made[:, :, LC:LC + 1], ACT.Copy)
            nc.scalar.activation(m.l_score[0:LC + 1, :, LC:LC + LR], w.qr.rearrange("p (h l) -> p h l", h=LH), ACT.Copy)
            act.wait_ge(s["bias_psum"], 1)
            nc.scalar.activation(m.made_bias[:, :], m.bank[5][:, 0:2 * D], ACT.Copy).then_inc(s["bias_copied"], 1)
            copy_weights(0)
            for c in range(NC):
                for j in range(MM):
                    n = MM * c + j
                    act.wait_ge(s["z_psum"], n + 1)
                    wait(act, s["hid_ready"], n - 1)
                    nc.scalar.activation(m.relu[:, n % 2, :], psZ[n % 2][:, :], ACT.Relu).then_inc(s["relu_ready"], 1)
                    if j == 1 and c > 0:
                        rstd(c - 1)
                    if c + 1 < NC:
                        if j == 1:
                            copy_turned(c + 1)
                        if j == 2:
                            exponentials(c + 1)
                if c + 1 < NC:
                    copy_weights(c + 1)
            rstd(NC - 1)

        @block.gpsimd
        def _(pool):
            m.stages.zero_spent(pool)

            for c in range(NC):
                for j in range(MM):
                    n = MM * c + j
                    wait(pool, s["y_psum"], n - 1)
                    if j < NM:
                        g = NM * c + j
                        pool.wait_ge(s["gated"], g + 1)
                        a = m.gated[:, g % 2, :]
                    else:
                        pool.wait_ge(s["relu_ready"], n + 1)
                        a = m.relu[:, n % 2, :]
                    nc.gpsimd.tensor_tensor(m.hid[:, n % 2, :], a, m.relu[:, n % 2, :], ALU.mult).then_inc(s["hid_ready"], 1)

        @block.vector
        def _(dve):
            steps = Chain(dve, s["route"])
            link = steps.link
            v = nc.vector
            ch = m.choice[:, :]
            groups = "p (x e) -> p x e"

            def route_groups(c):
                dve.wait_ge(s["exp_ready"], c + 1)
                link(v.tensor_scalar(m.route_s[:, :], m.route_e[:, :], 1.0, None, ALU.add))
                link(v.reciprocal(m.score16[:, :], m.route_s[:, :]))
                link(v.tensor_tensor(ch.rearrange("p (t e) -> p t e", e=NE), m.score16[:, :].rearrange("p (t e) -> p t e", e=NE),
                                     w.bias16.unsqueeze(1).broadcast_to([P, CT, NE]), ALU.add))
                pair = ch.rearrange("p (x z) -> p x z", z=2)
                v.tensor_tensor(m.pair_hi[:, :], pair[:, :, 0], pair[:, :, 1], ALU.max)
                link(v.tensor_tensor(m.pair_lo[:, :], pair[:, :, 0], pair[:, :, 1], ALU.min))
                hi = m.pair_hi[:, :].rearrange("p (x z) -> p x z", z=2)
                lo = m.pair_lo[:, :].rearrange("p (x z) -> p x z", z=2)
                v.tensor_tensor(m.top1[:, :], hi[:, :, 0], hi[:, :, 1], ALU.max)
                v.tensor_tensor(m.second_a[:, :], hi[:, :, 0], hi[:, :, 1], ALU.min)
                link(v.tensor_tensor(m.second_b[:, :], lo[:, :, 0], lo[:, :, 1], ALU.max))
                link(v.tensor_tensor(m.second_a[:, :], m.second_a[:, :], m.second_b[:, :], ALU.max))
                link(v.tensor_tensor(m.group_score[:, :], m.top1[:, :], m.second_a[:, :], ALU.add))
                gs = m.group_score[:, :].rearrange("p (t g) -> p t g", g=NG)
                theirs = gs.unsqueeze(2).broadcast_to([P, CT, NG, NG])
                own = gs.unsqueeze(3).broadcast_to([P, CT, NG, NG])
                v.tensor_tensor(m.above[:, :].rearrange("p (t g j) -> p t g j", g=NG, j=NG), theirs, own, ALU.is_gt)
                link(v.tensor_tensor(m.level[:, :].rearrange("p (t g j) -> p t g j", g=NG, j=NG), theirs, own, ALU.is_equal))
                link(v.tensor_tensor(m.level[:, :].rearrange("p (t gj) -> p t gj", t=CT), m.level[:, :].rearrange("p (t gj) -> p t gj", t=CT),
                                     w.ahead.unsqueeze(1).broadcast_to([P, CT, NG * NG]), ALU.mult))
                link(v.tensor_tensor(m.above[:, :], m.above[:, :], m.level[:, :], ALU.add))
                link(v.tensor_reduce(m.rank[:, :], m.above[:, :].rearrange("p (x j) -> p x j", j=NG), AX.X, ALU.add))
                link(v.tensor_scalar(m.rank[:, :], m.rank[:, :], TOPG - 0.5, None, ALU.is_lt))
                link(v.tensor_tensor(m.masked[:, :].rearrange("p (x e) -> p x e", e=NE // NG),
                                     ch.rearrange("p (x e) -> p x e", e=NE // NG),
                                     m.rank[:, :].unsqueeze(2).broadcast_to([P, CT * NG, NE // NG]), ALU.mult))

            def route_experts(c):
                masked = m.masked[:, :].rearrange("p (t e) -> p t e", e=NE)
                for t in range(CT):
                    op = v.max(m.top8[:, t, :], masked[:, t, :])
                link(op)
                fourth = m.top8[:, :, TOPK - 1:TOPK].broadcast_to([P, CT, NE])
                v.tensor_tensor(m.picked[:, :, :], masked, fourth, ALU.is_gt)
                link(v.tensor_tensor(m.count[:, 0, :, NE // 2:], masked, fourth, ALU.is_equal))
                link(v.tensor_reduce(m.room[:, :], m.picked[:, :, :], AX.X, ALU.add))
                link(v.tensor_scalar(m.room[:, :], m.room[:, :], -1.0, float(TOPK), ALU.mult, ALU.add))
                src = 0
                for shift in (1, 2, 4, 8):
                    dst = 1 if src != 1 else 2
                    link(v.tensor_tensor(m.count[:, dst, :, NE // 2:], m.count[:, src, :, NE // 2:],
                                         m.count[:, src, :, NE // 2 - shift:NE // 2 - shift + NE], ALU.add))
                    src = dst
                link(v.tensor_tensor(m.fits[:, :, :], m.count[:, src, :, NE // 2:],
                                     m.room[:, :].unsqueeze(2).broadcast_to([P, CT, NE]), ALU.is_le))
                link(v.tensor_tensor(m.fits[:, :, :], m.fits[:, :, :], m.count[:, 0, :, NE // 2:], ALU.mult))
                link(v.tensor_tensor(m.picked[:, :, :], m.picked[:, :, :], m.fits[:, :, :], ALU.add))

            def route_weights(c):
                sc = m.score16[:, :].rearrange("p (t e) -> p t e", e=NE)
                link(v.tensor_tensor(m.picked[:, :, :], m.picked[:, :, :], sc, ALU.mult))
                link(v.tensor_reduce(m.total[:, :], m.picked[:, :, :], AX.X, ALU.add))
                link(v.tensor_scalar(m.total[:, :], m.total[:, :], 1e-20, None, ALU.add))
                link(v.reciprocal(m.total[:, :], m.total[:, :]))
                link(v.scalar_tensor_tensor(out=m.cw[:, :, :], in0=m.picked[:, :, :], scalar=2.5,
                                            in1=m.total[:, :].unsqueeze(2).broadcast_to([P, CT, NE]),
                                            op0=ALU.mult, op1=ALU.mult))
                wait(dve, s["cwT_psum"], c)
                link(v.tensor_copy(m.cw3[:, :, 0:NE], m.cw[:, :, :]))
                link(v.tensor_tensor(m.cw[:, :, :], m.cw[:, :, :], m.cw3[:, :, 0:NE], ALU.subtract))
                link(v.tensor_copy(m.cw3[:, :, 32:32 + NE], m.cw[:, :, :]))
                v.tensor_tensor(m.cw3[:, :, 64:64 + NE], m.cw[:, :, :], m.cw3[:, :, 32:32 + NE],
                                ALU.subtract).then_inc(s["cw_ready"], 1)

            def residual(c):
                dve.wait_ge(s["y_psum"], MM * (c + 1))
                wait(dve, s["x_new"], c)
                v.tensor_tensor(m.r4[:, :, :].rearrange("p t d -> p (t d)"), psY[:, :],
                                m.X[:, CT * c:CT * (c + 1), :].rearrange("p t d -> p (t d)"), ALU.add).then_inc(s["r_done"], 1)
                dve.wait_ge(s["r_done"], c + 1)
                for t in range(CT):
                    op = v.bn_stats(m.bn24[:, t, :], m.r4[:, t, :])
                link(op)
                for t in range(CT):
                    op = v.bn_aggr(m.meanvar4[:, t, :], m.bn24[:, t, :])
                op.then_inc(s["var_ready"], 1)

            def apply(c):
                dve.wait_ge(s["rstd_ready"], c + 1)
                for t in range(CT):
                    op = v.tensor_scalar(m.X[:, CT * c + t, :], m.r4[:, t, :], m.meanvar4[:, t, 0:1], m.rstd4[:, t:t + 1],
                                         ALU.subtract, ALU.mult)
                op.then_inc(s["x_new"], 1)

            route_groups(0)
            route_experts(0)
            route_weights(0)
            for c in range(NC):
                for j in range(NM):
                    g, n = NM * c + j, MM * c + j
                    dve.wait_ge(s["gate_psum"], g + 1)
                    dve.wait_ge(s["relu_ready"], n + 1)
                    wait(dve, s["hid_ready"], n - 1 if j >= 2 else (MM * (c - 1) + NM - 1 + j if c > 0 else 0))
                    v.tensor_tensor(m.gated[:, g % 2, :], m.relu[:, n % 2, :], psW[g % 2][:, :], ALU.mult).then_inc(s["gated"], 1)
                    if j == 0 and c > 0:
                        residual(c - 1)
                    if j == 2 and c > 0:
                        apply(c - 1)
                    if c + 1 < NC:
                        if j == 3:
                            route_groups(c + 1)
                        if j == 5:
                            route_experts(c + 1)
                        if j == 6:
                            route_weights(c + 1)
            residual(NC - 1)
            apply(NC - 1)



MAGIC = 12582912.0
QMAX = 32767.0
SIG = 65536.0
NJ = 3


def quantised(nc, m, w, prefix):
    with ExitStack() as ctx:
        s = m.stages.semaphores(prefix,
                       "step wT_psum wT_ready xT_psum col_psum col_ready row_ready all_psum scaled x_shifted x_ready gu_psum gu_copied"
                       " g_shifted g_int sig_ready sig_int u_shifted q_shifted o_shifted o_ready y_psum r_done"
                       " var_ready ln_done rstd_ready")
        def sb(name, shape, dt=F32):
            return ctx.enter_context(nc.sbuf_tensor(prefix + name, shape, dt))

        m.xq = sb("xq", [P, NC, CH])
        m.G, m.U = sb("G", [P, NC, NJ, CH]), sb("U", [P, NC, NJ, CH])
        m.S = sb("S", [P, 2, NJ, CH])
        psM = m.bank[7]
        block = ctx.enter_context(nc.Block())

        @block.gpsimd
        def _(pool):
            m.stages.zero_spent(pool)
        NP = NJ * NC

        @block.tensor
        def _(pe):
            def spread_max(k):
                pe.wait_ge(s["col_ready"], k + 1)
                nc.tensor.transpose(psM[0:1, 0:P], m.q_col[:, 0:1], m.ident).then_inc(s["col_psum"], 1)
                pe.wait_ge(s["row_ready"], k + 1)
                nc.tensor.matmul(psM[:, P:P + 1], m.ones_row[0:1, :], m.q_one[0:1, 0:1], start=True,
                                 stop=True).then_inc(s["all_psum"], 1)

            for c in range(NC):
                for t in range(CT):
                    mm = nc.tensor.transpose(m.bank[c][:, t * P:(t + 1) * P], m.X[:, CT * c + t, :], m.ident)
                mm.then_inc(s["xT_psum"], 1)
            for n in range(3 * NJ):
                mm = nc.tensor.transpose(m.bank[4 + n // 3][:, n % 3 * P:(n % 3 + 1) * P], m.qw[:, 4 * n:4 * n + 4, :], m.ident)
            mm.then_inc(s["wT_psum"], 1)
            spread_max(0)
            for which, wt in enumerate((w.gate, w.up)):
                for j in range(NJ):
                    for c in range(NC):
                        n = NP * which + NC * j + c
                        if n < NC:
                            pe.wait_ge(s["x_ready"], n + 1)
                            pe.wait_ge(s["wT_ready"], 3)
                        wait(pe, s["gu_copied"], n - 2)
                        nc.tensor.matmul(m.bank[4 + n % 3][:, :], wt[:, j, :], m.xq[:, c, :], start=True,
                                         stop=True).then_inc(s["gu_psum"], 1)
            for k in range(1, 5):
                spread_max(k)
            for c in range(NC):
                pe.wait_ge(s["o_ready"], c + 1)
                for t in range(CT):
                    for j in range(NJ):
                        mm = nc.tensor.matmul(m.bank[c][:, t * D:(t + 1) * D], m.G[:, c, j, t * P:(t + 1) * P], w.down[:, j, :],
                                              start=(j == 0), stop=(j == NJ - 1))
                mm.then_inc(s["y_psum"], 1)

        @block.scalar
        def _(act):
            def shift(out, in_, scale):
                return nc.scalar.activation(out, in_, ACT.Identity, bias=m.magic[:, 0:1], scale=scale)

            act.wait_ge(s["wT_psum"], 1)
            for n in range(3):
                nc.scalar.activation(m.qwT[:, 3 * n:3 * n + 3, :].rearrange("p n o -> p (n o)"), m.bank[4 + n][:, 0:3 * P],
                                     ACT.Copy).then_inc(s["wT_ready"], 1)
            act.wait_ge(s["scaled"], 1)
            for c in range(NC):
                act.wait_ge(s["xT_psum"], c + 1)
                shift(m.xq[:, c, :], m.bank[c][:, :], m.q_k[:, 0:1]).then_inc(s["x_shifted"], 1)
            for n in range(2 * NP):
                act.wait_ge(s["gu_psum"], n + 1)
                dst = (m.G if n < NP else m.U)[:, n % NC, n % NP // NC, :]
                nc.scalar.activation(dst, m.bank[4 + n % 3][:, :], ACT.Copy).then_inc(s["gu_copied"], 1)
            act.wait_ge(s["scaled"], 2)
            for c in range(NC):
                shift(m.G[:, c, :, :], m.G[:, c, :, :], m.q_k[:, 1:2]).then_inc(s["g_shifted"], 1)
            for c in range(NC):
                act.wait_ge(s["g_int"], c + 1)
                wait(act, s["sig_int"], c - 1)
                nc.scalar.activation(m.S[:, c % 2, :, :], m.G[:, c, :, :], ACT.Sigmoid, scale=m.q_s[:, 1:2]).then_inc(s["sig_ready"], 1)
            act.wait_ge(s["scaled"], 3)
            for c in range(NC):
                shift(m.U[:, c, :, :], m.U[:, c, :, :], m.q_k[:, 2:3]).then_inc(s["u_shifted"], 1)
            act.wait_ge(s["scaled"], 4)
            for c in range(NC):
                shift(m.G[:, c, :, :], m.G[:, c, :, :], m.q_k[:, 3:4]).then_inc(s["q_shifted"], 1)
            act.wait_ge(s["scaled"], 5)
            for c in range(NC):
                shift(m.G[:, c, :, :], m.G[:, c, :, :], m.q_k[:, 4:5]).then_inc(s["o_shifted"], 1)
            act.preload_act_table_set("natural_log_exp_and_others")
            for c in range(NC):
                act.wait_ge(s["var_ready"], c + 1)
                nc.scalar.activation(m.lnvar4[:, :], m.meanvar4[:, :, 1], ACT.Ln, bias=m.eps[:, 0:1]).then_inc(s["ln_done"], 1)
                act.wait_ge(s["ln_done"], c + 1)
                nc.scalar.activation(m.rstd4[:, :], m.lnvar4[:, :], ACT.Exp, scale=-0.5).then_inc(s["rstd_ready"], 1)

        @block.vector
        def _(dve):
            v = nc.vector
            link = Chain(dve, s["step"]).link

            def scale(k, parts, unit):
                v.tensor_reduce(m.q_col[:, 0:1], parts, AX.X, ALU.max).then_inc(s["col_ready"], 1)
                dve.wait_ge(s["col_psum"], k + 1)
                v.tensor_reduce(m.q_one[0:1, 0:1], psM[0:1, 0:P], AX.X, ALU.max).then_inc(s["row_ready"], 1)
                dve.wait_ge(s["all_psum"], k + 1)
                if unit is None:
                    link(v.tensor_scalar(m.q_s[:, k:k + 1], psM[:, P:P + 1], 1.0 / QMAX, 1e-12, ALU.mult, ALU.max))
                    v.reciprocal(m.q_k[:, k:k + 1], m.q_s[:, k:k + 1]).then_inc(s["scaled"], 1)
                else:
                    link(v.tensor_scalar(m.q_t[:, 0:1], psM[:, P:P + 1], unit, 1.0 / QMAX, ALU.mult, ALU.mult))
                    link(v.tensor_scalar(m.q_s[:, k:k + 1], m.q_t[:, 0:1], 1e-12, None, ALU.max))
                    link(v.reciprocal(m.q_t[:, 0:1], m.q_s[:, k:k + 1]))
                    v.tensor_tensor(m.q_k[:, k:k + 1], m.q_t[:, 0:1], unit, ALU.mult).then_inc(s["scaled"], 1)

            def absmax(out, in_):
                return v.tensor_reduce(out, in_, AX.XY if len(in_.shape) > 2 else AX.X, ALU.max, apply_absolute_value=True)

            link(absmax(m.q_parts[:, 0:1], m.X[:, :, :]))
            scale(0, m.q_parts[:, 0:1], None)
            for c in range(NC):
                dve.wait_ge(s["x_shifted"], c + 1)
                v.tensor_scalar(m.xq[:, c, :], m.xq[:, c, :], MAGIC, None, ALU.subtract).then_inc(s["x_ready"], 1)
            for which in range(2):
                for n in range(NP * which, NP * (which + 1)):
                    dve.wait_ge(s["gu_copied"], n + 1)
                    op = absmax(m.q_parts[:, n:n + 1], (m.G if n < NP else m.U)[:, n % NC, n % NP // NC, :])
                link(op)
                if which == 0:
                    scale(1, m.q_parts[:, 0:NP], m.q_s[:, 0:1])
            for c in range(NC):
                dve.wait_ge(s["g_shifted"], c + 1)
                v.tensor_scalar(m.G[:, c, :, :], m.G[:, c, :, :], MAGIC, None, ALU.subtract).then_inc(s["g_int"], 1)
            scale(2, m.q_parts[:, NP:2 * NP], m.q_s[:, 0:1])
            for c in range(NC):
                dve.wait_ge(s["sig_ready"], c + 1)
                link(v.tensor_scalar(m.S[:, c % 2, :, :], m.S[:, c % 2, :, :], SIG, SIG - 1, ALU.mult, ALU.min))
                link(v.tensor_scalar(m.S[:, c % 2, :, :], m.S[:, c % 2, :, :], MAGIC, MAGIC, ALU.add, ALU.subtract))
                v.tensor_tensor(m.G[:, c, :, :], m.S[:, c % 2, :, :], m.G[:, c, :, :], ALU.mult).then_inc(s["sig_int"], 1)
                dve.wait_ge(s["sig_int"], c + 1)
                op = absmax(m.q_parts[:, c:c + 1], m.G[:, c, :, :])
            link(op)
            link(v.tensor_scalar(m.q_u[:, 0:1], m.q_s[:, 1:2], 1.0 / SIG, None, ALU.mult))
            scale(3, m.q_parts[:, 0:NC], m.q_u[:, 0:1])
            for c in range(NC):
                dve.wait_ge(s["u_shifted"], c + 1)
                op = v.tensor_scalar(m.U[:, c, :, :], m.U[:, c, :, :], MAGIC, None, ALU.subtract)
            link(op)
            for c in range(NC):
                dve.wait_ge(s["q_shifted"], c + 1)
                link(v.scalar_tensor_tensor(out=m.G[:, c, :, :], in0=m.G[:, c, :, :], scalar=MAGIC, in1=m.U[:, c, :, :],
                                            op0=ALU.subtract, op1=ALU.mult))
                op = absmax(m.q_parts[:, c:c + 1], m.G[:, c, :, :])
            link(op)
            link(v.tensor_tensor(m.q_u[:, 1:2], m.q_s[:, 3:4], m.q_s[:, 2:3], ALU.mult))
            scale(4, m.q_parts[:, 0:NC], m.q_u[:, 1:2])
            for c in range(NC):
                dve.wait_ge(s["o_shifted"], c + 1)
                v.tensor_scalar(m.G[:, c, :, :], m.G[:, c, :, :], MAGIC, None, ALU.subtract).then_inc(s["o_ready"], 1)
            for c in range(NC):
                dve.wait_ge(s["y_psum"], c + 1)
                link(v.scalar_tensor_tensor(out=m.r4[:, :, :].rearrange("p t d -> p (t d)"), in0=m.bank[c][:, :],
                                            scalar=m.q_s[:, 4:5], in1=m.X[:, CT * c:CT * (c + 1), :].rearrange("p t d -> p (t d)"),
                                            op0=ALU.mult, op1=ALU.add))
                for t in range(CT):
                    op = v.bn_stats(m.bn24[:, t, :], m.r4[:, t, :])
                link(op)
                for t in range(CT):
                    op = v.bn_aggr(m.meanvar4[:, t, :], m.bn24[:, t, :])
                op.then_inc(s["var_ready"], 1)
                dve.wait_ge(s["rstd_ready"], c + 1)
                for t in range(CT):
                    op = v.tensor_scalar(m.X[:, CT * c + t, :], m.r4[:, t, :], m.meanvar4[:, t, 0:1], m.rstd4[:, t:t + 1],
                                         ALU.subtract, ALU.mult)
                link(op)



HEAD_COLS = [("ident", P), ("mask_ac", 4), ("mask_ca", 4), ("mask_i", NI), ("causal", T), ("w0_q", D), ("w0_k", D), ("w0_v", D), ("w0_o", D),
             ("w0_bias", D)]
MID_COLS = [("cos", T), ("sin", T), ("x0_q", D), ("x0_qr", D), ("x0_k", D), ("x0_kr", D), ("x0_v", D), ("x0_o", D)]
BODY_COLS = [("x1_q", D), ("x1_k", D), ("x1_v", D), ("x1_o", D), ("x1_qr", D), ("x1_kr", D),
             ("x1_bq", 1), ("x1_bk", 1), ("x1_bqr", 1), ("x1_bkr", 1), ("x1_bv", 1),
             ("x1_of", D), ("x1_bo", D),
             ("l_dq", LC), ("l_df", LC + LR), ("l_uq", LH * (LC + 1)), ("l_uk", LH * (LC + 1)), ("l_uv", LH * LC),
             ("l_buv", LH), ("l_o", LH * D), ("l_bo", D), ("l_bl", 1),
             ("e_router", NE), ("e_bias", NE), ("e_ahead", NG * NG), ("e_w1", NE * 64), ("e_w2", NM * D), ("e_s1", D), ("e_s2", D),
             ("e_spread", NM * P), ("q_w", 9 * D)]
ROW64_COLS = [("l_qr", LH * LR),
              ("l_bq", 1), ("l_bf", 1)]


def columns(cols):
    at, out = 0, {}
    for name, n in cols:
        out[name] = (at, n)
        at += n
    return out, at


def decoder(nc, x, ctxT, mask, head, mid, body, row64, out):
    with ExitStack() as ctx:
        m = Names()

        def sb(name, shape, dt=F32):
            return ctx.enter_context(nc.sbuf_tensor(name, shape, dt))

        m.bank = [ctx.enter_context(nc.psum_tensor(f"bank{i}", [P, 512], F32)) for i in range(8)]
        m.ctxT_dram = ctxT
        m.stages = Stages(nc)
        m.X = sb("X", [P, NT, D])
        head_at, head_n = columns(HEAD_COLS)
        mid_at, mid_n = columns(MID_COLS)
        body_at, body_n = columns(BODY_COLS)
        row64_at, row64_n = columns(ROW64_COLS)
        head_sb = sb("head_sb", [P, head_n])
        mid_sb = sb("mid_sb", [P, mid_n])
        body_sb = sb("body_sb", [P, body_n])
        row64_sb = sb("row64_sb", [T, row64_n])

        def h(name):
            at, n = head_at[name]
            return head_sb[:, at:at + n]

        def mi(name):
            at, n = mid_at[name]
            return mid_sb[:, at:at + n]

        def bd(name):
            at, n = body_at[name]
            return body_sb[:, at:at + n]

        def r64(name):
            at, n = row64_at[name]
            return row64_sb[:, at:at + n]

        m.ident, m.mask_ac, m.mask_ca, m.mask_i, m.causal = h("ident"), h("mask_ac"), h("mask_ca"), h("mask_i"), h("causal")
        m.cos, m.sin = mi("cos"), mi("sin")
        m.mask_u8 = sb("mask_u8", [1, NSEQ * T], U8)
        m.mask_row = sb("mask_row", [1, NSEQ * T], BF16)
        m.ones_bf = sb("ones_bf", [1, P], BF16)
        m.one = sb("one", [P, 1])
        m.eps = sb("eps", [P, 1])
        m.xs = sb("xs", [P, 2, P])
        m.xb = sb("xb", [P, 2, P])
        m.xT = sb("xT", [P, 2, SB, 2, T])
        m.kvT = sb("kvT", [P, 2, SB, 2, T])
        m.qk = sb("qk", [P, 2, 2, P])
        m.vals = sb("vals", [P, 2, SB, NI, 2, 2, HD + 1])
        m.rowmax = sb("rowmax", [P, SB, 8])
        m.den = sb("den", [P, 16])
        m.rden = sb("rden", [P, 16])
        m.o = sb("o", [P, 2, SB, T])
        m.oT = sb("oT", [P, 2, P])
        m.r = sb("r", [P, D])
        m.bn6 = sb("bn6", [P, 6])
        m.meanvar = sb("meanvar", [P, 2])
        m.lnvar = sb("lnvar", [P, 1])
        m.rstd = sb("rstd", [P, 1])
        m.f = sb("f", [P, 2, P])
        m.cq = sb("cq", [P, 2, P])
        m.g = sb("g", [P, 2, SB, LH, T])
        m.lvals = sb("lvals", [P, 2, SB, 2, LC + 1])
        m.lprob = sb("lprob", [P, 2, SB, 2, P])
        m.lprobT = sb("lprobT", [P, 512])
        m.lo = sb("lo", [P, 2, SB, P])
        m.ones_row = sb("ones_row", [1, P])
        m.l_score = sb("l_score", [P, LH, P])
        m.l_out = sb("l_out", [P, 2, D])
        m.made_bias = sb("made_bias", [P, 2 * D])
        m.ident_bf = sb("ident_bf", [P, P], BF16)
        m.spread = sb("spread", [P, NM, P], BF16)
        m.xTc = sb("xTc", [P, 2, CH])
        m.route_e, m.route_s, m.score16, m.choice, m.masked = (sb(n, [P, CT * NE]) for n in ("route_e", "route_s", "score16", "choice", "masked"))
        m.pair_hi, m.pair_lo = sb("pair_hi", [P, CT * NE // 2]), sb("pair_lo", [P, CT * NE // 2])
        m.top1, m.second_a, m.second_b, m.group_score, m.rank = (sb(n, [P, CT * NG]) for n in ("top1", "second_a", "second_b", "group_score", "rank"))
        m.above, m.level = sb("above", [P, CT * NG * NG]), sb("level", [P, CT * NG * NG])
        m.top8 = sb("top8", [P, CT, 8])
        m.picked, m.fits, m.cw = (sb(n, [P, CT, NE]) for n in ("picked", "fits", "cw"))
        m.count = sb("count", [P, 3, CT, NE // 2 + NE])
        m.room, m.total = sb("room", [P, CT]), sb("total", [P, CT])
        m.cw3 = sb("cw3", [P, CT, CW], BF16)
        m.cwT = sb("cwT", [CW, 2, CH], BF16)
        m.relu, m.gated, m.hid = (sb(n, [P, 2, CH]) for n in ("relu", "gated", "hid"))
        m.r4, m.bn24, m.meanvar4 = sb("r4", [P, CT, D]), sb("bn24", [P, CT, 6]), sb("meanvar4", [P, CT, 2])
        m.lnvar4, m.rstd4 = sb("lnvar4", [P, CT]), sb("rstd4", [P, CT])
        m.magic = sb("magic", [P, 1])
        m.q_col, m.q_one, m.q_t, m.q_u = sb("q_col", [P, 1]), sb("q_one", [1, 1]), sb("q_t", [P, 1]), sb("q_u", [P, 2])
        m.q_s, m.q_k, m.q_parts = sb("q_s", [P, 5]), sb("q_k", [P, 5]), sb("q_parts", [P, 2 * NJ * NC])
        m.qw = sb("qw", [P, 9 * 4, 32])
        m.qwT = sb("qwT", [P, 9, D])
        m.qw_s, m.qw_i = sb("qw_s", [P, 36]), sb("qw_i", [P, 36])

        m.load = {n: ctx.enter_context(nc.semaphore("load_" + n)) for n in ("head", "x", "mid", "mask", "body", "row64")}
        with ExitStack() as c2:
            s = m.stages.semaphores("i_", "zeros memset")
            block = c2.enter_context(nc.Block())

            @block.sync
            def _(sp):
                sp.dma_start(head_sb[:, :], head).then_inc(m.load["head"], 16)
                sp.dma_start(m.X[:, :, :], x.rearrange("(t p) c -> p t c", p=P)).then_inc(m.load["x"], 16)
                sp.dma_start(mid_sb[:, :], mid).then_inc(m.load["mid"], 16)
                sp.dma_start(m.mask_u8[:, :], mask).then_inc(m.load["mask"], 16)
                sp.dma_start(body_sb[:, :], body).then_inc(m.load["body"], 16)
                sp.dma_start(row64_sb[:, :], row64).then_inc(m.load["row64"], 16)
                sp.wait_ge(m.load["head"], 16)
                sp.wait_ge(m.load["x"], 16)

            @block.gpsimd
            def _(pool):
                pool.memset(m.ones_bf[:, :], 1.0)
                pool.memset(m.one[:, :], 1.0)
                pool.memset(m.eps[:, :], EPS)
                pool.memset(m.magic[:, :], MAGIC)
                pool.memset(m.ones_row[:, :], 1.0)
                pool.memset(m.cw3[:, :, :], 0.0)
                pool.memset(m.count[:, :, :, :], 0.0)
                pool.memset(m.lvals[:, :, :, :, :], 0.0)
                pool.memset(m.vals[:, :, :, :, :, :, :], 0.0).then_inc(s["zeros"], 1)
                pool.wait_ge(s["zeros"], 1)
                for a in range(2):
                    for par in range(2):
                        pool.memset(m.vals[a * T:a * T + T, par, :, :, a, :, HD], 1.0)
                        pool.memset(m.lvals[a * T:a * T + T, par, :, a, LC], 1.0)

            @block.vector
            def _(dve):
                nc.vector.memset(m.l_score[:, :, :], 0.0)
                nc.vector.memset(m.cq[:, :, :], 0.0)
                nc.vector.memset(m.f[LC + LR:, :, :], 0.0).then_inc(s["memset"], 1)
                dve.wait_ge(s["memset"], 1)
                nc.vector.memset(m.cq[LC:LC + 1, :, :], 1.0)
                nc.vector.memset(m.f[LC + LR:LF, :, :], 1.0)

        w = Names()
        w.wq, w.wk, w.wv, w.wo, w.bias_tile, w.mask_row = h("w0_q"), h("w0_k"), h("w0_v"), h("w0_o"), h("w0_bias"), None
        small_attention(nc, m, w, "causal", "a0_")
        w = Names()
        w.wq, w.wk, w.wv, w.wo, w.bias_tile, w.mask_row = mi("x0_q"), mi("x0_k"), mi("x0_v"), mi("x0_o"), None, m.mask_row
        w.wqr, w.wkr = mi("x0_qr"), mi("x0_kr")
        w.bq = w.bqr = w.bk = w.bkr = 0.0
        small_attention(nc, m, w, "cross", "x0_")

        w = Names()
        w.router, w.bias16, w.ahead = bd("e_router"), bd("e_bias"), bd("e_ahead")
        w.w1, w.w2, w.shared1, w.shared2 = bd("e_w1"), bd("e_w2"), bd("e_s1"), bd("e_s2")
        w.uq, w.uk, w.uv = (bd(n).rearrange("p (h l) -> p h l", h=LH) for n in ("l_uq", "l_uk", "l_uv"))
        w.up_o, w.buv, w.b_latent, w.l_bo = bd("l_o").rearrange("p (h o) -> p h o", h=LH), bd("l_buv"), bd("l_bl"), bd("l_bo")[0:1, :]
        w.x1_bv, w.x1_o, w.x1_bo, w.qr, w.spread = bd("x1_bv"), bd("x1_of"), bd("x1_bo")[0:1, :], r64("l_qr")[0:LC + 1, :], bd("e_spread")
        experts(nc, m, w, "e_")
        w = Names()
        w.dq, w.df, w.b_q, w.b_f = bd("l_dq"), bd("l_df"), r64("l_bq")[0:LC, :], r64("l_bf")
        w.q_w = bd("q_w")
        w.score, w.out, w.bias_tile = m.l_score, m.l_out, m.made_bias[:, 0:D]
        latent_attention(nc, m, w, "l1_")
        w = Names()
        w.wq, w.wk, w.wv, w.wo, w.bias_tile, w.mask_row = bd("x1_q"), bd("x1_k"), bd("x1_v"), bd("x1_o"), m.made_bias[:, D:2 * D], None
        w.wqr, w.wkr = bd("x1_qr"), bd("x1_kr")
        w.bq, w.bk, w.bqr, w.bkr = bd("x1_bq"), bd("x1_bk"), bd("x1_bqr"), bd("x1_bkr")
        small_attention(nc, m, w, "cross", "x1_")
        w = Names()
        w.gate, w.up, w.down = m.qwT[:, 0:3, :], m.qwT[:, 3:6, :], m.qwT[:, 6:9, :]
        quantised(nc, m, w, "q_")

        with ExitStack() as c2:
            s = m.stages.semaphores("o_", "out")
            block = c2.enter_context(nc.Block())

            @block.sync
            def _(sp):
                sp.dma_start(out.rearrange("(t p) c -> p t c", p=P), m.X[:, :, :]).then_inc(s["out"], 16)
                sp.wait_ge(s["out"], 16)


def host_constants():
    import numpy as np
    c = {"ident": np.eye(P, dtype=np.float32)}
    p = np.arange(P)
    c["mask_ac"] = (p[:, None] // HD % 4 == np.arange(4)).astype(np.float32)
    c["mask_ca"] = np.ascontiguousarray(c["mask_ac"][:, [0, 2, 1, 3]])
    c["mask_i"] = (p[:, None] // (4 * HD) == np.arange(NI)).astype(np.float32)
    c["causal"] = np.where(p[:, None] % T <= np.arange(T), 0.0, -1e30).astype(np.float32)
    gj = np.arange(NG * NG)
    c["e_ahead"] = np.broadcast_to((gj % NG < gj // NG).astype(np.float32), (P, NG * NG))
    c["e_spread"] = (p[:, None] % 32 == np.arange(NM * P) // 64).astype(np.float32)
    d = p % HD
    inv = (1.0 / 10000.0 ** (np.arange(0, HD, 2, dtype=np.float32) / np.float32(HD))).astype(np.float32)
    ang = (np.arange(T, dtype=np.float32)[None, :] * inv[d % 4][:, None]).astype(np.float32)
    c["cos"] = np.cos(ang)
    c["sin"] = np.sin(ang) * np.where(d < HD // 2, -1, 1).astype(np.float32)[:, None]
    return c


def kernel(**inputs):
    import numpy as np
    import concourse.bacc as bacc
    from concourse.bass_utils import run_bass_kernel_spmd

    g = {k: np.asarray(v) for k, v in inputs.items()}
    parts = host_constants()

    def small_out(wT):
        return wT.reshape(NI, 2, 2, HD, D).transpose(2, 0, 1, 3, 4).reshape(P, D)

    qkv = g["L0_attn_w_qkv"]
    parts["w0_q"], parts["w0_k"], parts["w0_v"] = qkv[:D].T, qkv[D:2 * D].T, qkv[2 * D:].T
    parts["w0_bias"] = np.broadcast_to(g["L0_attn_b_proj"], (P, D))
    parts["w0_o"] = small_out(g["L0_attn_w_proj"].T)
    parts["x0_q"], parts["x0_k"], parts["x0_v"] = g["L0_xattn_Wq"], g["L0_xattn_Wkv"][:, :D], g["L0_xattn_Wkv"][:, D:]
    swapped = (np.arange(D) // HD) * HD + (np.arange(D) + HD // 2) % HD
    parts["x0_qr"], parts["x0_kr"] = parts["x0_q"][:, swapped], parts["x0_k"][:, swapped]
    parts["x0_o"] = small_out(g["L0_xattn_Wout"])
    for n in "qk":
        wt = g["L1_xattn_W" + n]
        parts["x1_" + n], parts["x1_" + n + "r"] = wt.T, wt.T[:, swapped]
        parts["x1_b" + n] = g["L1_xattn_b" + n].reshape(D, 1)
        parts["x1_b" + n + "r"] = parts["x1_b" + n][swapped]
    parts["x1_v"] = g["L1_xattn_Wv"].T
    parts["e_router"] = g["L0_ffn_Wg"].T
    parts["e_bias"] = np.broadcast_to(g["L0_ffn_bias_corr"], (P, NE))
    parts["e_w1"] = g["L0_ffn_W1"].reshape(NE * 64, D).T
    parts["e_w2"] = g["L0_ffn_W2"].transpose(0, 2, 1).reshape(NM, P, D).transpose(1, 0, 2).reshape(P, NM * D)
    parts["e_s1"], parts["e_s2"] = g["L0_ffn_Ws1"].T, g["L0_ffn_Ws2"].T

    def side_by_side(wt):
        return wt.reshape(-1, P, wt.shape[1]).transpose(1, 0, 2).reshape(P, -1)

    parts["q_w"] = np.concatenate([side_by_side(g["L1_ffn_w_gate"]), side_by_side(g["L1_ffn_w_up"]), g["L1_ffn_w_down"]], axis=1)
    parts["x1_bv"] = g["L1_xattn_bv"].reshape(D, 1)
    parts["x1_of"] = g["L1_xattn_Wo"].T
    parts["x1_bo"] = np.broadcast_to(g["L1_xattn_bo"], (P, D))

    def up(n):
        both = np.concatenate([g["L1_attn_W_" + n], g["L1_attn_b_" + n][None]], axis=0)
        return both.reshape(LC + 1, LH, D).transpose(2, 1, 0).reshape(D, LH * (LC + 1))

    def rows64(v):
        return np.concatenate([v, np.zeros((T - v.shape[0], v.shape[1]), np.float32)], axis=0)

    parts["l_dq"] = g["L1_attn_W_DQ"]
    parts["l_df"] = np.concatenate([g["L1_attn_W_DKV"], g["L1_attn_W_KR"]], axis=1)
    parts["l_uq"], parts["l_uk"] = up("UQ"), up("UK")
    parts["l_uv"] = g["L1_attn_W_UV"].reshape(LC, LH, D).transpose(2, 1, 0).reshape(D, LH * LC)
    parts["l_buv"] = g["L1_attn_b_UV"].reshape(LH, D).T
    parts["l_o"] = g["L1_attn_W_O"].reshape(LH, D, D).transpose(1, 0, 2).reshape(D, LH * D)
    parts["l_bo"] = np.broadcast_to(g["L1_attn_b_O"], (P, D))
    parts["l_qr"] = rows64(np.concatenate([g["L1_attn_W_QR"], g["L1_attn_b_QR"][None]], axis=0))
    parts["l_bq"] = rows64(g["L1_attn_b_DQ"][:, None])
    parts["l_bf"] = np.concatenate([g["L1_attn_b_DKV"], g["L1_attn_b_KR"]])[:, None]
    parts["l_bl"] = np.tile(g["L1_attn_b_DKV"], P // LC)[:, None]
    parts["x1_o"] = small_out(g["L1_xattn_Wo"].T)

    def pack(cols):
        return np.concatenate([parts[n] for n, _ in cols], axis=1)

    arrays = {
        "x": g["x"].reshape(NSEQ * T, D),
        "ctxT": g["ctx_1024"].reshape(NSEQ * T, D).T.reshape(D, NSEQ, T),
        "mask": g["mask_BxS2_bf1"].reshape(1, NSEQ * T).view(np.uint8),
        "head": pack(HEAD_COLS), "mid": pack(MID_COLS), "body": pack(BODY_COLS), "row64": pack(ROW64_COLS),
    }
    arrays = {f"in_{k}": np.ascontiguousarray(v) for k, v in arrays.items()}
    nc = bacc.Bacc("TRN2", target_bir_lowering=False, num_devices=1)
    args = [nc.dram_tensor(k, v.shape, mybir.dt.from_np(v.dtype), kind="ExternalInput").ap() for k, v in arrays.items()]
    out = nc.dram_tensor("out", (NSEQ * T, D), F32, kind="ExternalOutput").ap()
    decoder(nc, *args, out)
    r = run_bass_kernel_spmd(nc, [arrays], core_ids=[0])
    return r.results[0]["out"].reshape(NSEQ, T, D)
```

```python
from contextlib import ExitStack

import concourse.bass as bass
from concourse import mybir

F32 = mybir.dt.float32
BF16 = mybir.dt.bfloat16
U8 = mybir.dt.uint8
ALU = mybir.AluOpType
ACT = mybir.ActivationFunctionType
AX = mybir.AxisListType

P = 128
D = 128
T = 64
NSEQ = 32
NT = NSEQ * T // P
SB = P // T
HD = 8
NI = 4
EPS = 1e-5
SMALL_SCALE = HD ** -0.5
BIG = 3.3895313892515355e38

PHASES = 5
PEEL = PHASES + 1
SLOTS = NT + PHASES - 1
PAIRS = (NT - PEEL) // 2


def run_slots(eng, first, second, lead):
    for s in range(PEEL):
        first(s, s % 2)
    with eng.Fori(0, PAIRS) as i:
        for j in range(2):
            first(i * 2 + (PEEL + j), (PEEL + j) % 2)
    for s in range(PEEL + lead):
        first(NT + s, s % 2)
        if s >= lead:
            second(s - lead, (s - lead) % 2)
    with eng.Fori(0, PAIRS) as i:
        for j in range(2):
            second(i * 2 + (PEEL + j), (PEEL + j) % 2)
    for s in range(NT, SLOTS):
        second(s, s % 2)


def has(s, phase):
    return not isinstance(s, int) or 0 <= s - phase < NT


def wait(eng, mark, value):
    start = mark.start if isinstance(mark, Mark) else 0
    sem = mark.sem if isinstance(mark, Mark) else mark
    if not isinstance(value, int) or value + start > 0:
        eng.wait_ge(sem, value + start)


def wait_before(eng, before, step, t):
    if isinstance(t, int) and t < 2:
        for sem, value in before.get(step, ()):
            eng.wait_ge(sem, value(t))


class Turn:

    def __init__(self, at, cur):
        self.at, self.cur = at, cur

    def __call__(self, step, phase):
        if has(self.at, phase):
            step(self.at - phase, (self.cur + phase) % 2)


class Names:
    pass


class Stage:

    def __init__(self, pool, pe, act, dve, with_context):
        self.pool, self.pe, self.act, self.dve, self.with_context = pool, pe, act, dve, with_context


class Stages:

    def __init__(self, nc):
        self.nc, self.last, self.spent = nc, [], []

    def semaphores(self, prefix, names):
        for h in self.spent:
            self.nc.release_semaphore(h)
        self.spent = self.last
        self.last = [self.nc.alloc_semaphore(prefix + n) for n in names.split()]
        return dict(zip(names.split(), self.last))

    def zero_spent(self, pool):
        nums = sorted(h.num for h in self.spent)
        while nums:
            run = 1
            while run < len(nums) and nums[run] == nums[0] + run:
                run += 1
            pool.sem_clear(range(nums[0], nums[0] + run))
            nums = nums[run:]



class TailNorm:

    def __init__(self, nc, m, s, bias_tile, y):
        self.nc, self.m, self.s, self.bias_tile, self.y = nc, m, s, bias_tile, y

    def add_bias(self, pool, t, par):
        wait(pool, self.s["xT_psum"], t + 1)
        wait(pool, self.s["r_done"], t - 1)
        self.nc.gpsimd.tensor_tensor(self.m.xb[:, par, :], self.m.X[:, t, :], self.bias_tile, ALU.add).then_inc(self.s["xb_ready"].sem, 1)

    def residual(self, dve, t, par):
        s, m = self.s, self.m
        if self.bias_tile is not None:
            wait(dve, s["xb_ready"], t + 1)
        wait(dve, s["y_psum"], t + 1)
        wait(dve, s["x_new"], t)
        x = m.X[:, t, :] if self.bias_tile is None else m.xb[:, par, :]
        self.nc.vector.tensor_tensor(m.r[:, :], self.y, x, ALU.add).then_inc(s["r_done"].sem, 1)

    def statistics(self, dve, t, par):
        wait(dve, self.s["r_done"], t + 1)
        self.nc.vector.bn_stats(self.m.bn6[:, :], self.m.r[:, :]).then_inc(self.s["bn6_done"].sem, 1)

    def variance(self, dve, t, par):
        dve.wait_ge(self.s["bn6_done"].sem, 1)
        wait(dve, self.s["bn6_done"], t + 1)
        self.nc.vector.bn_aggr(self.m.meanvar[:, :], self.m.bn6[:, :]).then_inc(self.s["var_ready"].sem, 1)

    def log_variance(self, act, t, par):
        wait(act, self.s["var_ready"], t + 1)
        wait(act, self.s["rstd_ready"], t)
        self.nc.scalar.activation(self.m.lnvar[:, :], self.m.meanvar[:, 1:2], ACT.Ln,
                                  bias=self.m.eps[:, 0:1]).then_inc(self.s["lnvar_done"].sem, 1)

    def rstd(self, act, t, par):
        wait(act, self.s["lnvar_done"], t + 1)
        wait(act, self.s["x_new"], t)
        self.nc.scalar.activation(self.m.rstd[:, :], self.m.lnvar[:, :], ACT.Exp, scale=-0.5).then_inc(self.s["rstd_ready"].sem, 1)

    def apply(self, dve, t, par):
        m = self.m
        wait(dve, self.s["rstd_ready"], t + 1)
        self.nc.vector.tensor_scalar(m.X[:, t, :], m.r[:, :], m.meanvar[:, 0:1], m.rstd[:, 0:1],
                                     ALU.subtract, ALU.mult).then_inc(self.s["x_new"].sem, 1)


def stage_tiles(sp, m, s, with_context, second, loads):
    def tile(t, par):
        if not isinstance(t, int) or t >= 2:
            wait(sp, s["xT_psum"], t - 1)
            if second and isinstance(t, int):
                wait(sp, s["x_new"], t + 1 - NT)
            sp.dma_start(m.xs[:, par, :], m.X[:, t, :]).then_inc(s[f"xs_load{par}"].sem, 16)
        if with_context:
            wait(sp, s["v_psum"], t - 1)
            for a in range(2):
                sp.dma_start(m.kvT[:, par, :, a, :], m.ctxT_dram[:, bass.ds(t * SB, SB), :]).then_inc(s[f"kv_load{par}"].sem, 16)
    peeled = 8 if loads else 6 if second else 4
    for t in range(peeled):
        for load in loads.get(t, ()):
            load(sp)
        tile(t, t % 2)
    if second:
        wait(sp, s["x_new"], 0)
    with sp.Fori(peeled // 2, NT // 2) as i:
        tile(i * 2, 0)
        tile(i * 2 + 1, 1)


def placed_tile(pe, m, s, t, par):
    if isinstance(t, int) and t < 2:
        wait(pe, s["x_new"], t + 1 - NT)
        return m.X[:, t, :]
    wait(pe, s[f"xs_load{par}"], 8 * (t - par))
    return m.xs[:, par, :]



def small_attention(nc, m, w, kind, s, before):
    causal = kind == "causal"
    psS = [m.bank[0], m.bank[1]]
    psT = [m.bank[2], m.bank[3]]
    psQK, psXV, psO, psOY = m.bank[4], m.bank[5], m.bank[6], m.bank[7]
    psY = psOY[:, 256:384]
    tail = TailNorm(nc, m, s, w.bias_tile, psY)
    masked = not causal and w.mask_row is not None


    def on_pool(pool):

        def rope_sum(t, par):
            wait(pool, s["rope_parts"], t + 1)
            wait(pool, s["mov_ready"], t - 1)
            nc.gpsimd.tensor_tensor(m.qk[:, par, :, :], m.rope[:, par, :, 0, :], m.rope[:, par, :, 1, :],
                                    ALU.add).then_inc(s["qk_sum"].sem, 1)

        def mask_operand(t, par, out, which, mask, done):
            if causal:
                wait(pool, s["qk_ready"], t + 1)
            else:
                wait(pool, s["qk_sum"], t + 1)
            wait(pool, s["s_psum1"], t - 1)
            nc.gpsimd.tensor_tensor(
                out[:, par, :, :, :],
                m.qk[:, par, which, :].rearrange("p (b k) -> p b k", b=SB).unsqueeze(2).broadcast_to([P, SB, 4, T]),
                mask.unsqueeze(1).unsqueeze(3).broadcast_to([P, SB, 4, T]), ALU.mult).then_inc(s[done].sem, 1)

        def stationary(t, par):
            mask_operand(t, par, m.stat, 1 if causal else 0, m.mask_ca if causal else m.mask_ac, "stat_ready")

        def moving(t, par):
            mask_operand(t, par, m.mov, 0 if causal else 1, m.mask_i, "mov_ready")

        def square1(t, par):
            wait(pool, s["soft_done1"], t + 1)
            wait(pool, s["o_psum1"], t - 1)
            soft = m.soft[:, 1, :].rearrange("p (c i q) -> p c i q", c=2, i=NI)
            nc.gpsimd.tensor_tensor(m.prob[:, par, 1, :, :, :].rearrange("p i c q -> p c i q"), soft, soft,
                                    ALU.mult).then_inc(s["prob_ready1"].sem, 1)

        def add_bias(t, par):
            tail.add_bias(pool, t, par)

        def slot(at, cur):
            run = Turn(at, cur)
            if causal:
                run(moving, 1), run(add_bias, 2), run(square1, 2), run(stationary, 0)
            else:
                run(rope_sum, 0), run(stationary, 0), run(moving, 0)
                if w.bias_tile is not None:
                    run(add_bias, 1)
        return slot

    def on_pe(pe):
        def turn(t, par):
            x = placed_tile(pe, m, s, t, par)
            wait(pe, s["v_ready"], t)
            wait_before(pe, before, "turn", t)
            nc.tensor.transpose(psXV[:, 0:P], x, m.ident).then_inc(s["xT_psum"].sem, 1)

        def project(t, par):
            wait_before(pe, before, "project", t)
            wait(pe, s["xT_ready"], t + 1)
            xT = m.xT[:, par, :, 0, :]
            if causal:
                wait(pe, s["qk_ready"], t)
                parts = ((w.wq, xT), (w.wk, xT))
            else:
                wait(pe, s["rope_parts"], t)
                wait(pe, s[f"kv_load{par}"], 16 * (t - par) + 32)
                cT = m.kvT[:, par, :, 0, :]
                parts = ((w.wq, xT), (w.wqr, xT), (w.wk, cT), (w.wkr, cT))
            for n, (wt, xT) in enumerate(parts):
                mm = nc.tensor.matmul(psQK[:, n * P:(n + 1) * P], wt, xT, start=True, stop=True)
            mm.then_inc(s["qk_psum"].sem, 1)

        def values(t, par):
            wait(pe, s["xT_ready"], t + 1)
            if not causal:
                wait(pe, s[f"kv_load{par}"], 16 * (t - par) + 32)
            kvT = m.xT if causal else m.kvT
            for b in range(SB):
                mm = nc.tensor.matmul(psXV[:, 256 + b * P:256 + (b + 1) * P], kvT[:, par, b, :, :], w.wv, start=True, stop=True)
            mm.then_inc(s["v_psum"].sem, 1)

        def scores(t, par, b):
            wait_before(pe, before, "scores", t)
            wait(pe, s["stat_ready"], t + 1)
            wait(pe, s["mov_ready"], t + 1)
            wait(pe, s[f"shifted{b}"], t)
            if masked:
                nc.tensor.matmul(psS[b][:, :], m.ones_bf[0:1, :],
                                 w.mask_row[0:1, bass.ds(t * P + b * T, T)].unsqueeze(1).broadcast_to([1, 8, T]),
                                 start=True, stop=False, skip_group_check=True)
            for half in range(2):
                mm = nc.tensor.matmul(psS[b][:, 256 * half:256 * half + 256], m.stat[:, par, b, 2 * half:2 * half + 2, :],
                                      m.mov[:, par, b, :, :], start=not masked, stop=True, skip_group_check=masked)
            mm.then_inc(s[f"s_psum{b}"].sem, 1)

        def scores0(t, par):
            scores(t, par, 0)

        def scores1(t, par):
            scores(t, par, 1)

        def turn_probs(t, par, b):
            wait_before(pe, before, "turn_probs", t)
            wait(pe, s[f"pT_ready{b}"], t)
            wait(pe, s[f"exp_done{b}"], t + 1)
            for i in range(NI):
                mm = nc.tensor.transpose(psT[b][:, i * P:(i + 1) * P], m.prob[:, par, b, i, :, :], m.ident)
            mm.then_inc(s[f"pT_psum{b}"].sem, 1)

        def turn_probs0(t, par):
            turn_probs(t, par, 0)

        def turn_probs1(t, par):
            turn_probs(t, par, 1)

        def outputs(t, par, b):
            wait(pe, s["o_ready"], t)
            wait(pe, s["v_ready"], t + 1)
            wait(pe, s[f"prob_ready{b}" if causal else f"pT_ready{b}"], t + 1)
            for i in range(NI):
                lhsT = m.prob[:, par, b, i, :, :] if causal else m.probT[:, b, i, :]
                at = 36 * (NI * b + i)
                mm = nc.tensor.matmul(psO[:, at:at + 36], lhsT, m.vals[:, par, b, i, :, :, :], start=True, stop=True)
            mm.then_inc(s[f"o_psum{b}"].sem, 1)

        def outputs0(t, par):
            outputs(t, par, 0)

        def outputs1(t, par):
            outputs(t, par, 1)

        def turn_outputs(t, par):
            wait(pe, s["r_done"], t)
            wait(pe, s["o_ready"], t + 1)
            nc.tensor.transpose(psOY[:, 0:P], m.o[:, par, :, :], m.ident).then_inc(s["oT_psum"].sem, 1)

        def project_outputs(t, par):
            wait(pe, s["oT_ready"], t + 1)
            nc.tensor.matmul(psY, m.oT[:, 0, :], w.wo, start=True, stop=True).then_inc(s["y_psum"].sem, 1)

        def slot(at, cur):
            run = Turn(at, cur)
            if causal:
                run(turn, 0), run(scores1, 1), run(project_outputs, 3), run(project, 0), run(outputs0, 2)
                run(outputs1, 2), run(values, 0), run(scores0, 0), run(turn_outputs, 2)
            else:
                run(turn, 0), run(scores0, 1), run(outputs1, 2), run(project, 0), run(scores1, 1), run(turn_probs0, 1)
                run(values, 0), run(turn_outputs, 2), run(outputs0, 1), run(project_outputs, 2), run(turn_probs1, 1)
        return slot

    def on_act(act):

        def copy_turned(t, par):
            wait(act, s["xT_psum"], t + 1)
            wait(act, s["qk_psum"], t - 1)
            wait(act, s["v_psum"], t - 1)
            wait_before(act, before, "copy_turned", t)
            nc.scalar.activation(m.xT[:, par, :, :, :],
                                 psXV[:, 0:P].rearrange("p (b k) -> p b k", b=SB).unsqueeze(2).broadcast_to([P, SB, 2, T]),
                                 ACT.Copy).then_inc(s["xT_ready"].sem, 1)

        def copy_qk(t, par):
            wait(act, s["qk_psum"], t + 1)
            wait(act, s["mov_ready"], t - 1)
            nc.scalar.activation(m.qk[:, par, :, :], psQK[:, 0:256].rearrange("p (x t) -> p x t", x=2),
                                 ACT.Copy).then_inc(s["qk_ready"].sem, 1)

        def copy_values(t, par):
            wait(act, s["v_psum"], t + 1)
            wait(act, s["o_psum1"], t - 1)
            for a in range(2):
                half = slice(a * T, a * T + T)
                op = nc.scalar.activation(
                    m.vals[half, par, :, :, a, :, 0:HD].rearrange("p b i c d -> p (b i) c d"),
                    psXV[half, 256:512].rearrange("p (bi a c d) -> p bi a c d", a=2, c=2, d=HD)[:, :, a, :, :],
                    ACT.Copy)
            op.then_inc(s["v_ready"].sem, 1)

        def exponential(t, par, b):
            sc = m.prob[:, par, b, :, :, :].rearrange("p i a k -> p (i a k)")
            if causal:
                wait(act, s[f"clamped{b}"], t + 1)
                nc.scalar.activation(m.soft[:, b, :], m.soft[:, b, :], ACT.Exp).then_inc(s[f"exp_done{b}"].sem, 1)
            else:
                wait(act, s[f"shifted{b}"], t + 1)
                nc.scalar.activation(sc, sc, ACT.Exp, scale=SMALL_SCALE).then_inc(s[f"exp_done{b}"].sem, 1)

        def exponential0(t, par):
            exponential(t, par, 0)

        def exponential1(t, par):
            exponential(t, par, 1)

        def log_one_plus(t, par, b):
            wait(act, s[f"exp_done{b}"], t + 1)
            nc.scalar.activation(m.soft[:, b, :], m.soft[:, b, :], ACT.Ln, bias=m.one[:, 0:1]).then_inc(s[f"ln_done{b}"].sem, 1)

        def log_one_plus0(t, par):
            log_one_plus(t, par, 0)

        def log_one_plus1(t, par):
            log_one_plus(t, par, 1)

        def square0(t, par):
            wait(act, s["soft_done0"], t + 1)
            wait(act, s["o_psum0"], t - 1)
            nc.scalar.activation(m.prob[:, par, 0, :, :, :].rearrange("p i c q -> p c i q"),
                                 m.soft[:, 0, :].rearrange("p (c i q) -> p c i q", c=2, i=NI), ACT.Square).then_inc(s["prob_ready0"].sem, 1)

        def copy_probs(t, par, b):
            wait(act, s[f"pT_psum{b}"], t + 1)
            wait(act, s[f"o_psum{b}"], t)
            nc.scalar.activation(m.probT[:, b, :, :].rearrange("p i q -> p (i q)"), psT[b][:, :],
                                 ACT.Copy).then_inc(s[f"pT_ready{b}"].sem, 1)

        def copy_probs0(t, par):
            copy_probs(t, par, 0)

        def copy_probs1(t, par):
            copy_probs(t, par, 1)

        def copy_outputs(t, par):
            wait(act, s["oT_psum"], t + 1)
            wait(act, s["y_psum"], t)
            for b in range(SB):
                for c in range(2):
                    op = nc.scalar.activation(m.oT[c * T:(c + 1) * T, 0, b * T:(b + 1) * T],
                                              psOY[b * T:(b + 1) * T, c * T:(c + 1) * T], ACT.Copy)
            op.then_inc(s["oT_ready"].sem, 1)

        def log_variance(t, par):
            tail.log_variance(act, t, par)

        def rstd(t, par):
            tail.rstd(act, t, par)

        def slot(at, cur):
            run = Turn(at, cur)
            if causal:
                run(copy_turned, 0), run(copy_qk, 0), run(exponential0, 1), run(log_one_plus0, 1), run(exponential1, 1)
                run(log_variance, 3), run(log_one_plus1, 1), run(copy_values, 0), run(rstd, 3), run(square0, 1)
                run(copy_outputs, 2)
            else:
                run(rstd, 4), run(exponential1, 2), run(copy_values, 1), run(copy_probs1, 2), run(copy_turned, 0)
                run(exponential0, 1), run(copy_probs0, 1), run(log_variance, 3), run(copy_outputs, 2)
        return slot

    def on_dve(dve):
        def scale_and_mask(t, par, b):
            wait(dve, s[f"s_psum{b}"], t + 1)
            wait(dve, s[f"soft_done{b}"], t)
            nc.vector.scalar_tensor_tensor(
                out=m.score[:, b, :].rearrange("p (x k) -> p x k", k=T), in0=psS[b][:, :].rearrange("p (x k) -> p x k", k=T),
                scalar=SMALL_SCALE, in1=m.causal.unsqueeze(1).broadcast_to([P, 8, T]),
                op0=ALU.mult, op1=ALU.add).then_inc(s[f"shifted{b}"].sem, 1)

        def clamp(t, par, b):
            wait(dve, s[f"shifted{b}"], t + 1)
            wait(dve, s[f"prob_ready{b}"], t)
            nc.vector.tensor_scalar(m.soft[:, b, :], m.score[:, b, :], 40.0, None, ALU.min).then_inc(s[f"clamped{b}"].sem, 1)

        def softplus(t, par, b):
            wait(dve, s[f"ln_done{b}"], t + 1)
            nc.vector.tensor_tensor(m.soft[:, b, :], m.soft[:, b, :], m.score[:, b, :], ALU.max).then_inc(s[f"soft_done{b}"].sem, 1)

        def maximum(t, par, b):
            wait(dve, s[f"s_psum{b}"], t + 1)
            wait(dve, s[f"shifted{b}"], t)
            wait_before(dve, before, "maximum", t)
            nc.vector.tensor_reduce(m.rowmax[:, b, :], psS[b][:, :].rearrange("p (x k) -> p x k", k=T), AX.X,
                                    ALU.max).then_inc(s[f"max_done{b}"].sem, 1)

        def less_maximum(t, par, b):
            wait(dve, s[f"max_done{b}"], t + 1)
            wait_before(dve, before, f"less_maximum{b}", t)
            wait(dve, s[f"pT_psum{b}"], t - 1)
            nc.vector.tensor_tensor(m.prob[:, par, b, :, :, :].rearrange("p i a k -> p a i k"),
                                    psS[b][:, :].rearrange("p (a i k) -> p a i k", a=2, i=NI),
                                    m.rowmax[:, b, :].rearrange("p (a i) -> p a i", a=2).unsqueeze(3)
                                    .broadcast_to([P, 2, NI, T]),
                                    ALU.subtract).then_inc(s[f"shifted{b}"].sem, 1)

        def scale_and_mask0(t, par):
            scale_and_mask(t, par, 0)

        def scale_and_mask1(t, par):
            scale_and_mask(t, par, 1)

        def clamp0(t, par):
            clamp(t, par, 0)

        def clamp1(t, par):
            clamp(t, par, 1)

        def softplus0(t, par):
            softplus(t, par, 0)

        def softplus1(t, par):
            softplus(t, par, 1)

        def maximum0(t, par):
            maximum(t, par, 0)

        def maximum1(t, par):
            maximum(t, par, 1)

        def less_maximum0(t, par):
            less_maximum(t, par, 0)

        def less_maximum1(t, par):
            less_maximum(t, par, 1)

        def rotate(t, par):
            wait(dve, s["qk_psum"], t + 1)
            wait(dve, s["qk_sum"], t - 1)
            for n, (bias, table) in enumerate(((w.bq, m.cos), (w.bqr, m.sin), (w.bk, m.cos), (w.bkr, m.sin))):
                op = nc.vector.scalar_tensor_tensor(
                    out=m.rope[:, par, n // 2, n % 2, :].rearrange("p (b t) -> p b t", b=SB),
                    in0=psQK[:, n * P:(n + 1) * P].rearrange("p (b t) -> p b t", b=SB),
                    scalar=bias, in1=table.unsqueeze(1).broadcast_to([P, SB, T]), op0=ALU.add, op1=ALU.mult)
            op.then_inc(s["rope_parts"].sem, 1)

        o = psO[:, 0:288].rearrange("p (bia c e) -> p bia c e", c=2, e=HD + 1)
        halves = (slice(0, T), slice(T, P))

        def denominators(t, par):
            for b in range(SB):
                wait(dve, s[f"o_psum{b}"], t + 1)
            wait(dve, s["rden_done"], t)
            for c in range(2):
                op = nc.vector.tensor_scalar(m.den[halves[c], :], o[halves[c], :, c, HD], 1e-9, None, ALU.add)
            op.then_inc(s["den_done"].sem, 1)

        def reciprocals(t, par):
            wait(dve, s["o_ready"], t)
            if causal:
                wait(dve, s["den_done"], t + 1)
                nc.vector.reciprocal(m.rden[:, :], m.den[:, :]).then_inc(s["rden_done"].sem, 1)
            else:
                for b in range(SB):
                    wait(dve, s[f"o_psum{b}"], t + 1)
                for c in range(2):
                    op = nc.vector.reciprocal(m.rden[halves[c], :], o[halves[c], :, c, HD])
                op.then_inc(s["rden_done"].sem, 1)

        def normalise(t, par):
            wait(dve, s["rden_done"], t + 1)
            wait(dve, s["oT_psum"], t - 1)
            for c in range(2):
                op = nc.vector.tensor_tensor(
                    m.o[halves[c], par, :, :].rearrange("p b (ia d) -> p (b ia) d", d=HD), o[halves[c], :, c, 0:HD],
                    m.rden[halves[c], :].unsqueeze(2).broadcast_to([T, 16, HD]), ALU.mult)
            op.then_inc(s["o_ready"].sem, 1)

        def residual(t, par):
            tail.residual(dve, t, par)

        def statistics(t, par):
            tail.statistics(dve, t, par)

        def variance(t, par):
            tail.variance(dve, t, par)

        def apply(t, par):
            tail.apply(dve, t, par)

        def slot(at, cur):
            run = Turn(at, cur)
            if causal:
                run(softplus1, 1), run(apply, 3), run(scale_and_mask0, 0), run(clamp0, 0), run(residual, 2)
                run(scale_and_mask1, 0), run(statistics, 2), run(variance, 2), run(clamp1, 0)
                run(denominators, 1), run(reciprocals, 1), run(normalise, 1), run(softplus0, 0)
            else:
                run(maximum0, 1), run(less_maximum0, 1), run(reciprocals, 2), run(rotate, 0), run(normalise, 2)
                run(variance, 3), run(maximum1, 1), run(less_maximum1, 1), run(apply, 3), run(residual, 2)
                run(statistics, 2)
        return slot
    return Stage(pool=on_pool, pe=on_pe, act=on_act, dve=on_dve, with_context=not causal)



LH, LC, LR = 8, 32, 32
LF = LC + LR + 1
LATENT_SCALE = (D + LR) ** -0.5


def latent_attention(nc, m, w, s):
    psS = [m.bank[0], m.bank[1]]
    psG = [m.bank[2], m.bank[3]]
    psT, psXV, psO, psOY = m.bank[4], m.bank[5], m.bank[6], m.bank[7]
    psY = psOY[:, 256:384]
    tail = TailNorm(nc, m, s, w.bias_tile, psY)


    def on_pool(pool):

        def add_bias(t, par):
            tail.add_bias(pool, t, par)

        def slot(at, cur):
            run = Turn(at, cur)
            run(add_bias, 1)
        return slot

    def on_pe(pe):
        def turn(t, par):
            x = placed_tile(pe, m, s, t, par)
            wait(pe, s["q_ready"], t)
            wait(pe, s["f_ready"], t)
            wait(pe, s["v_ready"], t)
            nc.tensor.transpose(psXV[:, 0:P], x, m.ident).then_inc(s["xT_psum"].sem, 1)

        def low_rank(t, par):
            wait(pe, s["xT_ready"], t + 1)
            xT = m.xT[:, par, :, 0, :]
            nc.tensor.matmul(psXV[0:LC, 128:256], w.dq, xT, start=True, stop=True)
            nc.tensor.matmul(psXV[0:LC + LR, 256:384], w.df, xT, start=True, stop=True)
            for b in range(SB):
                mm = nc.tensor.matmul(psXV[:, 384 + b * LC:384 + (b + 1) * LC], m.xT[:, par, b, :, :], w.df[:, 0:LC],
                                      start=True, stop=True)
            mm.then_inc(s["low_psum"].sem, 1)

        def queries(t, par, half):
            wait(pe, s["q_ready"], t + 1)
            wait(pe, s[f"g_ready{half}"], t)
            for h in range(4):
                mm = nc.tensor.matmul(psG[half][:, h * P:(h + 1) * P], w.score[:, 4 * half + h, :],
                                      m.cq[:, par, :], start=True, stop=True)
            mm.then_inc(s[f"g_psum{half}"].sem, 1)

        def queries0(t, par):
            queries(t, par, 0)

        def queries1(t, par):
            queries(t, par, 1)

        def scores(t, par):
            wait(pe, s["g_ready0"], t + 1)
            wait(pe, s["g_ready1"], t + 1)
            wait(pe, s["f_ready"], t + 1)
            wait(pe, s["shifted"], t - 1)
            for b in range(SB):
                for ia in range(4):
                    mm = nc.tensor.matmul(psS[par][:, (4 * b + ia) * T:(4 * b + ia + 1) * T],
                                          m.g[:, par, b, 2 * ia:2 * ia + 2, :], m.f[:, par, b * T:(b + 1) * T],
                                          start=True, stop=True)
            mm.then_inc(s["s_psum"].sem, 1)

        def turn_probs(t, par):
            wait(pe, s["pT_ready"], t)
            wait(pe, s["exp_done"], t + 1)
            for b in range(SB):
                for i in range(2):
                    mm = nc.tensor.transpose(psT[:, (2 * b + i) * P:(2 * b + i + 1) * P],
                                             m.lprob[:, par, b, i, :], m.ident)
            mm.then_inc(s["pT_psum"].sem, 1)

        def outputs(t, par):
            wait(pe, s["o_ready"], t)
            wait(pe, s["pT_ready"], t + 1)
            wait(pe, s["v_ready"], t + 1)
            for b in range(SB):
                for i in range(2):
                    n = 2 * b + i
                    mm = nc.tensor.matmul(psO[:, n * 66:(n + 1) * 66], m.lprobT[:, n * P:(n + 1) * P],
                                          m.lvals[:, par, b, :, :], start=True, stop=True)
            mm.then_inc(s["o_psum"].sem, 1)

        def turn_outputs(t, par):
            wait(pe, s["r_done"], t)
            wait(pe, s["o_ready"], t + 1)
            for b in range(SB):
                mm = nc.tensor.transpose(psOY[:, b * P:(b + 1) * P], m.lo[:, par, b, :], m.ident)
            mm.then_inc(s["oT_psum"].sem, 1)

        def project_outputs(t, par):
            wait(pe, s["oT_ready"], t + 1)
            for c in range(2):
                mm = nc.tensor.matmul(psY, m.oT[:, c, :], w.out[:, c, :], start=(c == 0), stop=(c == 1))
            mm.then_inc(s["y_psum"].sem, 1)

        def slot(at, cur):
            run = Turn(at, cur)
            run(turn, 0), run(outputs, 2), run(scores, 1), run(turn_outputs, 2), run(low_rank, 0)
            run(project_outputs, 2), run(queries1, 0), run(turn_probs, 1), run(queries0, 0)
        return slot

    def on_act(act):

        def copy_turned(t, par):
            wait(act, s["xT_psum"], t + 1)
            wait(act, s["low_psum"], t - 1)
            nc.scalar.activation(m.xT[:, par, :, :, :],
                                 psXV[:, 0:P].rearrange("p (b k) -> p b k", b=SB).unsqueeze(2).broadcast_to([P, SB, 2, T]),
                                 ACT.Copy).then_inc(s["xT_ready"].sem, 1)

        def copy_cq(t, par):
            wait(act, s["low_psum"], t + 1)
            wait(act, s["g_psum0"], t - 1)
            wait(act, s["g_psum1"], t - 1)
            nc.scalar.activation(m.cq[0:LC, par, :], psXV[0:LC, 128:256], ACT.Identity,
                                 bias=w.b_q).then_inc(s["q_ready"].sem, 1)

        def copy_features(t, par):
            wait(act, s["low_psum"], t + 1)
            wait(act, s["s_psum"], t - 1)
            nc.scalar.activation(m.f[0:LC + LR, par, :], psXV[0:LC + LR, 256:384], ACT.Identity,
                                 bias=w.b_f).then_inc(s["f_ready"].sem, 1)

        def copy_latents(t, par):
            wait(act, s["low_psum"], t + 1)
            wait(act, s["o_psum"], t - 1)
            for a in range(2):
                half = slice(a * T, a * T + T)
                op = nc.scalar.activation(m.lvals[half, par, :, a, 0:LC],
                                          psXV[half, 384:448].rearrange("p (b l) -> p b l", b=SB), ACT.Copy)
            op.then_inc(s["v_ready"].sem, 1)

        def copy_queries(t, par, half):
            wait(act, s[f"g_psum{half}"], t + 1)
            wait(act, s["s_psum"], t - 1)
            nc.scalar.activation(m.g[:, par, :, 4 * half:4 * half + 4, :].rearrange("p b h q -> p h b q"),
                                 psG[half][:, :].rearrange("p (h b q) -> p h b q", h=4, b=SB),
                                 ACT.Copy).then_inc(s[f"g_ready{half}"].sem, 1)

        def copy_queries0(t, par):
            copy_queries(t, par, 0)

        def copy_queries1(t, par):
            copy_queries(t, par, 1)

        def exponential(t, par):
            wait(act, s["shifted"], t + 1)
            sc = m.lprob[:, par, :, :, :].rearrange("p b i k -> p (b i k)")
            nc.scalar.activation(sc, sc, ACT.Exp, scale=LATENT_SCALE).then_inc(s["exp_done"].sem, 1)

        def copy_outputs(t, par):
            wait(act, s["oT_psum"], t + 1)
            wait(act, s["y_psum"], t)
            nc.scalar.activation(m.oT[:, :, :].rearrange("p c (b q) -> p c b q", b=SB),
                                 psOY[:, 0:256].rearrange("p (b c q) -> p c b q", b=SB, c=2),
                                 ACT.Copy).then_inc(s["oT_ready"].sem, 1)

        def log_variance(t, par):
            tail.log_variance(act, t, par)

        def rstd(t, par):
            tail.rstd(act, t, par)

        def slot(at, cur):
            run = Turn(at, cur)
            run(copy_turned, 0), run(log_variance, 3), run(copy_outputs, 2), run(rstd, 3), run(copy_cq, 0)
            run(exponential, 1), run(copy_queries1, 0), run(copy_features, 0), run(copy_latents, 0), run(copy_queries0, 0)
        return slot

    def on_dve(dve):
        link = Chain(dve, s["blocks"].sem).link
        by_block = lambda a: a.unsqueeze(2).broadcast_to([P, 36, 32])
        raw = w.q_w.rearrange("p (x k) -> p x k", k=32)
        link(nc.vector.tensor_reduce(m.qw_i[:, :], raw, AX.X, ALU.max, apply_absolute_value=True))
        link(nc.vector.tensor_scalar(m.qw_s[:, :], m.qw_i[:, :], 1.0 / 7.0, 1e-12, ALU.mult, ALU.max))
        link(nc.vector.reciprocal(m.qw_i[:, :], m.qw_s[:, :]))
        link(nc.vector.tensor_tensor(m.qw[:, :, :], raw, by_block(m.qw_i[:, :]), ALU.mult))
        link(nc.vector.tensor_scalar(m.qw[:, :, :], m.qw[:, :, :], MAGIC, MAGIC, ALU.add, ALU.subtract))
        nc.vector.tensor_tensor(m.qw[:, :, :], m.qw[:, :, :], by_block(m.qw_s[:, :]), ALU.mult)

        def maximum(t, par):
            wait(dve, s["s_psum"], t + 1)
            wait(dve, s["shifted"], t)
            nc.vector.tensor_reduce(m.rowmax[:, 0, :], psS[par][:, :].rearrange("p (x k) -> p x k", k=T), AX.X,
                                    ALU.max).then_inc(s["max_done"].sem, 1)

        def less_maximum(t, par):
            wait(dve, s["max_done"], t + 1)
            wait(dve, s["pT_psum"], t - 1)
            nc.vector.tensor_tensor(m.lprob[:, par, :, :, :].rearrange("p b i (a k) -> p (b i a) k", k=T),
                                    psS[par][:, :].rearrange("p (x k) -> p x k", k=T),
                                    m.rowmax[:, 0, :].unsqueeze(2).broadcast_to([P, 8, T]),
                                    ALU.subtract).then_inc(s["shifted"].sem, 1)

        def copy_probs(t, par):
            wait(dve, s["pT_psum"], t + 1)
            wait(dve, s["o_psum"], t)
            nc.vector.tensor_copy(m.lprobT[:, :], psT[:, :]).then_inc(s["pT_ready"].sem, 1)

        o = psO[:, 0:264].rearrange("p (x e) -> p x e", e=LC + 1)

        def reciprocals(t, par):
            wait(dve, s["o_psum"], t + 1)
            wait(dve, s["o_ready"], t)
            nc.vector.reciprocal(m.rden[:, 0:8], o[:, :, LC]).then_inc(s["rden_done"].sem, 1)

        def normalise(t, par):
            wait(dve, s["rden_done"], t + 1)
            wait(dve, s["oT_psum"], t - 1)
            nc.vector.tensor_tensor(m.lo[:, par, :, :].rearrange("p b (x l) -> p (b x) l", l=LC), o[:, :, 0:LC],
                                    m.rden[:, 0:8].unsqueeze(2).broadcast_to([P, 8, LC]),
                                    ALU.mult).then_inc(s["o_ready"].sem, 1)

        def residual(t, par):
            tail.residual(dve, t, par)

        def statistics(t, par):
            tail.statistics(dve, t, par)

        def variance(t, par):
            tail.variance(dve, t, par)

        def apply(t, par):
            tail.apply(dve, t, par)

        def slot(at, cur):
            run = Turn(at, cur)
            run(less_maximum, 1), run(apply, 3), run(residual, 2), run(statistics, 2)
            run(copy_probs, 1), run(reciprocals, 1), run(variance, 2), run(normalise, 1), run(maximum, 0)
        return slot
    return Stage(pool=on_pool, pe=on_pe, act=on_act, dve=on_dve, with_context=False)


EACH = "xs_load0 xs_load1 xT_psum xT_ready v_ready o_ready oT_psum oT_ready y_psum r_done bn6_done var_ready lnvar_done rstd_ready x_new rden_done"
BY_SEQUENCE = "s_psum0 s_psum1 shifted0 shifted1 exp_done0 exp_done1 o_psum0 o_psum1 qk_psum v_psum stat_ready mov_ready"
SEMAPHORES = {
    "causal": f"{EACH} {BY_SEQUENCE} xb_ready qk_ready clamped0 clamped1 ln_done0 ln_done1 soft_done0 soft_done1"
              " prob_ready0 prob_ready1 den_done",
    "cross": f"{EACH} {BY_SEQUENCE} kv_load0 kv_load1 rope_parts qk_sum max_done0 max_done1 pT_psum0 pT_psum1 pT_ready0 pT_ready1",
    "biased cross": f"{EACH} {BY_SEQUENCE} xb_ready kv_load0 kv_load1 rope_parts qk_sum max_done0 max_done1 pT_psum0 pT_psum1"
                    " pT_ready0 pT_ready1",
    "latent": f"{EACH} xb_ready low_psum q_ready f_ready g_psum0 g_psum1 g_ready0 g_ready1 s_psum max_done shifted exp_done"
              " pT_psum pT_ready o_psum blocks",
}


class Mark:

    def __init__(self, sem, start):
        self.sem, self.start = sem, start


def marks(m, prefix, first, second):
    names = sorted(set(SEMAPHORES[first].split()) | set(SEMAPHORES[second].split()))
    sems = m.stages.semaphores(prefix, " ".join(names))
    of_first = {n: Mark(sems[n], 0) for n in SEMAPHORES[first].split()}
    tiles = {n: (NT - 2) * 8 if n.startswith("xs_load") else NT for n in of_first}
    of_second = {n: Mark(sems[n], tiles.get(n, 0)) for n in SEMAPHORES[second].split()}
    return of_first, of_second


def two_stages(nc, m, ctx, s, one, two, lead, loads):
    block = ctx.enter_context(nc.Block())

    @block.sync
    def _(sp):
        stage_tiles(sp, m, s[0], one.with_context, False, loads)
        stage_tiles(sp, m, s[1], two.with_context, True, {})
        sp.wait_ge(m.load["body"], 16 * (BODY_PARTS + 1))

    @block.gpsimd
    def _(pool):
        m.stages.zero_spent(pool)
        run_slots(pool, one.pool(pool), two.pool(pool), lead[0])

    @block.tensor
    def _(pe):
        run_slots(pe, one.pe(pe), two.pe(pe), lead[1])

    @block.scalar
    def _(act):
        act.preload_act_table_set("natural_log_exp_and_others")
        run_slots(act, one.act(act), two.act(act), lead[2])

    @block.vector
    def _(dve):
        run_slots(dve, one.dve(dve), two.dve(dve), lead[3])


def small_buffers(nc, m, ctx, prefix):
    def sb(name, shape, dt=F32):
        return ctx.enter_context(nc.sbuf_tensor(prefix + name, shape, dt))

    m.rope = sb("rope", [P, 2, 2, 2, P])
    m.stat = sb("stat", [P, 2, SB, 4, T])
    m.mov = sb("mov", [P, 2, SB, NI, T])
    m.prob = sb("prob", [P, 2, SB, NI, 2, T])
    m.probT = sb("probT", [P, SB, NI, P])
    m.soft = sb("soft", [P, SB, 512])
    m.score = sb("score", [P, SB, 512])


def causal_then_cross(nc, m, w1, w2, loads, prefix):
    with ExitStack() as ctx:
        small_buffers(nc, m, ctx, prefix)
        s1, s2 = marks(m, prefix, "causal", "cross")
        before = {
            "project": [(m.load["mid"], lambda t: 16),
                        (s1["qk_ready"].sem, lambda t: NT)],
            "less_maximum0": [(s1["o_psum0"].sem, lambda t: NT - 1 + t)],
            "less_maximum1": [(s1["o_psum1"].sem, lambda t: NT - 1 + t)],
        }
        two_stages(nc, m, ctx, (s1, s2), small_attention(nc, m, w1, "causal", s1, {}),
                   small_attention(nc, m, w2, "cross", s2, before), lead=(2, 1, 0, 0), loads=loads)


def latent_then_cross(nc, m, w1, w2, prefix):
    with ExitStack() as ctx:
        small_buffers(nc, m, ctx, prefix)
        s1, s2 = marks(m, prefix, "latent", "biased cross")
        before = {
            "turn": [(s1["q_ready"].sem, lambda t: NT), (s1["f_ready"].sem, lambda t: NT)],
            "project": [(s1["pT_ready"].sem, lambda t: NT)],
            "scores": [(s1["shifted"].sem, lambda t: NT)],
            "turn_probs": [(s1["g_ready0"].sem, lambda t: NT), (s1["g_ready1"].sem, lambda t: NT)],
            "copy_turned": [(s1["low_psum"].sem, lambda t: NT - 1 + t)],
            "maximum": [(s1["shifted"].sem, lambda t: NT)],
        }
        two_stages(nc, m, ctx, (s1, s2), latent_attention(nc, m, w1, s1),
                   small_attention(nc, m, w2, "cross", s2, before), lead=(0, 0, 0, 0), loads={})



NE, NG, TOPG, TOPK = 16, 4, 2, 4
NM = NE // 2
CH = 512
NC = NSEQ * T // CH
LAG = 3
DEEP = LAG + 1
CT = CH // P
CW = 128


class Chain:

    def __init__(self, eng, sem):
        self.eng, self.sem, self.n = eng, sem, 0

    def link(self, op):
        op.then_inc(self.sem, 1)
        self.n += 1
        self.eng.wait_ge(self.sem, self.n)


def experts(nc, m, w, prefix):
    with ExitStack() as ctx:
        s = m.stages.semaphores(prefix,
                       "zeros constants made_psum made_copied bias_psum bias_copied xT_psum xT_ready logit_psum exp_ready route cw_ready cwT_psum cwT_ready z_psum gate_psum relu_ready"
                       " gated hid_ready y_psum r_done var_ready ln_done rstd_ready x_new")
        def sb(name, shape, dt=F32):
            return ctx.enter_context(nc.sbuf_tensor(prefix + name, shape, dt))

        m.ident_bf = sb("ident_bf", [P, P], BF16)
        m.spread = sb("spread", [P, NM, P], BF16)
        m.xTc = sb("xTc", [P, NC, CH])
        m.route_e, m.route_s, m.score16, m.choice, m.masked, m.picked, m.fits, m.cw = (
            sb(n, [P, NT * NE]) for n in ("route_e", "route_s", "score16", "choice", "masked", "picked", "fits", "cw"))
        m.pair_hi, m.pair_lo = sb("pair_hi", [P, NT * NE // 2]), sb("pair_lo", [P, NT * NE // 2])
        m.top1, m.second_a, m.second_b, m.group_score, m.rank = (sb(n, [P, NT * NG]) for n in ("top1", "second_a", "second_b", "group_score", "rank"))
        m.above, m.level = sb("above", [P, NT * NG * NG]), sb("level", [P, NT * NG * NG])
        m.top8 = sb("top8", [P, NT, 8])
        m.count = sb("count", [P, 3, NT, NE // 2 + NE])
        m.room, m.total = sb("room", [P, NT]), sb("total", [P, NT])
        m.cw3 = sb("cw3", [P, NT, CW], BF16)
        m.cwT = sb("cwT", [CW, 2, CH], BF16)
        m.gated = sb("gated", [P, 2, CH])
        m.relu, m.hid = sb("relu", [P, DEEP, CH]), sb("hid", [P, DEEP, CH])
        psX, psL, psC = [m.bank[0], m.bank[6]], m.bank[1], m.bank[2]
        psZ, psW, psY = [m.bank[3], m.bank[4]], [m.bank[5], m.bank[6]], m.bank[7]
        block = ctx.enter_context(nc.Block())
        MM = NM + 1

        @block.tensor
        def _(pe):
            def turn(c):
                wait(pe, s["xT_ready"], c - 1)
                for t in range(CT):
                    mm = nc.tensor.transpose(psX[c % 2][:, t * P:(t + 1) * P], m.X[:, CT * c + t, :], m.ident)
                mm.then_inc(s["xT_psum"], 1)

            def logits(c):
                pe.wait_ge(s["xT_ready"], c + 1)
                for t in range(CT):
                    at = (CT * c + t) * NE
                    mm = nc.tensor.matmul(psL[:, at:at + NE], m.xTc[:, c, t * P:(t + 1) * P], w.router, start=True, stop=True)
                mm.then_inc(s["logit_psum"], 1)

            def turn_weights(c):
                pe.wait_ge(s["cw_ready"], min(c, 1) + 1)
                pe.wait_ge(s["constants"], 1)
                wait(pe, s["cwT_ready"], c)
                ps = psC[:, :].bitcast(BF16)
                for t in range(CT):
                    mm = nc.tensor.transpose(ps[0:CW, t * P:(t + 1) * P], m.cw3[:, CT * c + t, :], m.ident_bf[:, :])
                mm.then_inc(s["cwT_psum"], 1)

            def hidden(n):
                c, j = divmod(n, MM)
                wait(pe, s["relu_ready"], n - 1)
                w1 = w.w1[:, j * P:(j + 1) * P] if j < NM else w.shared1
                nc.tensor.matmul(psZ[n % 2][:, :], w1, m.xTc[:, c, :], start=True, stop=True).then_inc(s["z_psum"], 1)

            def spread_weights(n):
                c, j = divmod(n, MM)
                if j < NM:
                    g = NM * c + j
                    if j == 0:
                        pe.wait_ge(s["cwT_ready"], c + 1)
                    wait(pe, s["gated"], g - 1)
                    nc.tensor.matmul(psW[g % 2][:, :], m.spread[:, j, :], m.cwT[:, c % 2, :],
                                     start=True, stop=True).then_inc(s["gate_psum"], 1)

            def down(n):
                c, j = divmod(n, MM)
                pe.wait_ge(s["hid_ready"], n + 1)
                if j == 0:
                    wait(pe, s["r_done"], c)
                w2 = w.w2[:, j * D:(j + 1) * D] if j < NM else w.shared2
                for t in range(CT):
                    mm = nc.tensor.matmul(psY[:, t * D:(t + 1) * D], m.hid[:, n % DEEP, t * P:(t + 1) * P], w2,
                                          start=(j == 0 and t == 0), stop=(j == MM - 1), skip_group_check=True)
                mm.then_inc(s["y_psum"], 1)

            def prepare():
                b_score, b_out, b_bias = m.bank[3], m.bank[4], m.bank[5]
                for hh in range(LH):
                    nc.tensor.matmul(b_score[0:LC + 1, hh * (LC + 1):(hh + 1) * (LC + 1)], w.uq[:, hh, :], w.uk[:, hh, :],
                                     start=True, stop=True)
                for hh in range(LH):
                    row, c = LC * (hh // 2), hh % 2
                    mm = nc.tensor.matmul(b_out[row:row + LC, c * D:(c + 1) * D], w.uv[:, hh, :], w.up_o[:, hh, :],
                                          start=True, stop=True)
                mm.then_inc(s["made_psum"], 1)
                to_all = m.ones_row[0:1, :]
                nc.tensor.matmul(b_bias[:, D:2 * D], w.x1_bv.broadcast_to([P, P]), w.x1_o, start=True, stop=False)
                nc.tensor.matmul(b_bias[:, D:2 * D], to_all, w.x1_bo, start=False, stop=True)
                for hh in range(LH):
                    nc.tensor.matmul(b_bias[:, 0:D], w.buv[:, hh:hh + 1].broadcast_to([P, P]), w.up_o[:, hh, :],
                                     start=(hh == 0), stop=False)
                nc.tensor.matmul(b_bias[:, 0:D], to_all, w.l_bo, start=False, stop=False)
                pe.wait_ge(s["made_copied"], 1)
                for c in range(2):
                    mm = nc.tensor.matmul(b_bias[:, 0:D], w.b_latent.broadcast_to([P, P]), m.l_out[:, c, :],
                                          start=False, stop=(c == 1))
                mm.then_inc(s["bias_psum"], 1)

            turn(0)
            logits(0)
            turn(1)
            prepare()
            for c in range(2, NC):
                turn(c)
            pe.wait_ge(s["exp_ready"], 1)
            for c in range(1, NC):
                logits(c)
            turn_weights(0)
            pe.wait_ge(s["bias_copied"], 1)
            for n in range(MM * NC + LAG):
                c, j = divmod(n, MM)
                if c < NC:
                    hidden(n)
                if n >= LAG:
                    down(n - LAG)
                if c < NC:
                    spread_weights(n)
                if c + 1 < NC and j == MM - 1:
                    turn_weights(c + 1)

        @block.scalar
        def _(act):
            act.preload_act_table_set("natural_log_exp_and_others")

            def copy_turned(c):
                act.wait_ge(s["xT_psum"], c + 1)
                nc.scalar.activation(m.xTc[:, c, :], psX[c % 2][:, :], ACT.Copy).then_inc(s["xT_ready"], 1)

            def exponentials(batch):
                first, last = (0, CT) if batch == 0 else (CT, NT)
                act.wait_ge(s["logit_psum"], 1 if batch == 0 else NC)
                nc.scalar.activation(m.route_e[:, first * NE:last * NE], psL[:, first * NE:last * NE], ACT.Exp,
                                     scale=-1.0).then_inc(s["exp_ready"], 1)

            def copy_weights(c):
                act.wait_ge(s["cwT_psum"], c + 1)
                wait(act, s["gate_psum"], NM * (c - 1))
                nc.scalar.activation(m.cwT[0:CW, c % 2, :], psC[:, :].bitcast(BF16)[0:CW, 0:CH], ACT.Copy).then_inc(s["cwT_ready"], 1)

            def rstd(c):
                act.wait_ge(s["var_ready"], c + 1)
                nc.scalar.activation(m.lnvar4[:, 0, :], m.meanvar4[:, 0, :, 1], ACT.Ln, bias=m.eps[:, 0:1]).then_inc(s["ln_done"], 1)
                act.wait_ge(s["ln_done"], c + 1)
                nc.scalar.activation(m.rstd4[:, 0, :], m.lnvar4[:, 0, :], ACT.Exp, scale=-0.5).then_inc(s["rstd_ready"], 1)

            copy_turned(0)
            exponentials(0)
            copy_turned(1)
            nc.scalar.activation(m.ident_bf[:, :], m.ident, ACT.Copy)
            nc.scalar.activation(m.spread[:, :, :].rearrange("p j q -> p (j q)"), w.spread, ACT.Copy).then_inc(s["constants"], 1)
            act.wait_ge(s["made_psum"], 1)
            nc.scalar.activation(m.l_out[:, :, :].rearrange("p c o -> p (c o)"), m.bank[4][:, 0:2 * D], ACT.Copy).then_inc(s["made_copied"], 1)
            made = m.bank[3][0:LC + 1, 0:LH * (LC + 1)].rearrange("p (h l) -> p h l", h=LH)
            nc.scalar.activation(m.l_score[0:LC + 1, :, 0:LC], made[:, :, 0:LC], ACT.Copy)
            nc.scalar.activation(m.l_score[0:LC + 1, :, LC + LR:LF], made[:, :, LC:LC + 1], ACT.Copy)
            nc.scalar.activation(m.l_score[0:LC + 1, :, LC:LC + LR], w.qr.rearrange("p (h l) -> p h l", h=LH), ACT.Copy)
            act.wait_ge(s["bias_psum"], 1)
            nc.scalar.activation(m.made_bias[:, :], m.bank[5][:, 0:2 * D], ACT.Copy).then_inc(s["bias_copied"], 1)
            for c in range(2, NC):
                copy_turned(c)
            exponentials(1)
            copy_weights(0)
            for c in range(NC):
                for j in range(MM):
                    n = MM * c + j
                    act.wait_ge(s["z_psum"], n + 1)
                    wait(act, s["hid_ready"], n - DEEP + 1)
                    nc.scalar.activation(m.relu[:, n % DEEP, :], psZ[n % 2][:, :], ACT.Relu).then_inc(s["relu_ready"], 1)
                    if j == LAG + 1 and c > 0:
                        rstd(c - 1)
                if c + 1 < NC:
                    copy_weights(c + 1)
            rstd(NC - 1)

        @block.gpsimd
        def _(pool):
            m.stages.zero_spent(pool)
            pool.memset(m.cw3[:, :, :], 0.0)
            pool.memset(m.count[:, :, :, :], 0.0).then_inc(s["zeros"], 1)
            for c in range(NC):
                for j in range(MM):
                    n = MM * c + j
                    wait(pool, s["y_psum"], n - DEEP + 1)
                    if j < NM:
                        g = NM * c + j
                        pool.wait_ge(s["gated"], g + 1)
                        a = m.gated[:, g % 2, :]
                    else:
                        pool.wait_ge(s["relu_ready"], n + 1)
                        a = m.relu[:, n % DEEP, :]
                    nc.gpsimd.tensor_tensor(m.hid[:, n % DEEP, :], a, m.relu[:, n % DEEP, :], ALU.mult).then_inc(s["hid_ready"], 1)

        @block.vector
        def _(dve):
            link = Chain(dve, s["route"]).link
            v = nc.vector

            def route(batch, part):
                t0, nt = (0, CT) if batch == 0 else (CT, NT - CT)
                flat = lambda buf, width: buf[:, 0:nt * width]
                by = lambda buf, width: flat(buf, width).rearrange("p (t e) -> p t e", t=nt)
                score, ch, masked, picked, fits, cw = (by(b, NE) for b in (m.score16, m.choice, m.masked, m.picked, m.fits, m.cw))
                count = m.count[:, :, 0:nt, :]
                cw3 = m.cw3[:, t0:t0 + nt, :]
                if part == 0:
                    dve.wait_ge(s["exp_ready"], batch + 1)
                    link(v.tensor_scalar(flat(m.route_s, NE), flat(m.route_e, NE) if batch == 0 else m.route_e[:, CT * NE:NT * NE],
                                         1.0, None, ALU.add))
                    link(v.reciprocal(flat(m.score16, NE), flat(m.route_s, NE)))
                    link(v.tensor_tensor(ch, score, w.bias16.unsqueeze(1).broadcast_to([P, nt, NE]), ALU.add))
                    pair = flat(m.choice, NE).rearrange("p (x z) -> p x z", z=2)
                    v.tensor_tensor(flat(m.pair_hi, NE // 2), pair[:, :, 0], pair[:, :, 1], ALU.max)
                    link(v.tensor_tensor(flat(m.pair_lo, NE // 2), pair[:, :, 0], pair[:, :, 1], ALU.min))
                    hi = flat(m.pair_hi, NE // 2).rearrange("p (x z) -> p x z", z=2)
                    lo = flat(m.pair_lo, NE // 2).rearrange("p (x z) -> p x z", z=2)
                    v.tensor_tensor(flat(m.top1, NG), hi[:, :, 0], hi[:, :, 1], ALU.max)
                    v.tensor_tensor(flat(m.second_a, NG), hi[:, :, 0], hi[:, :, 1], ALU.min)
                    link(v.tensor_tensor(flat(m.second_b, NG), lo[:, :, 0], lo[:, :, 1], ALU.max))
                if part == 1:
                    link(v.tensor_tensor(flat(m.second_a, NG), flat(m.second_a, NG), flat(m.second_b, NG), ALU.max))
                    link(v.tensor_tensor(flat(m.group_score, NG), flat(m.top1, NG), flat(m.second_a, NG), ALU.add))
                    gs = by(m.group_score, NG)
                    theirs = gs.unsqueeze(2).broadcast_to([P, nt, NG, NG])
                    own = gs.unsqueeze(3).broadcast_to([P, nt, NG, NG])
                    pairs = lambda buf: flat(buf, NG * NG).rearrange("p (t g j) -> p t g j", g=NG, j=NG)
                    v.tensor_tensor(pairs(m.above), theirs, own, ALU.is_gt)
                    link(v.tensor_tensor(pairs(m.level), theirs, own, ALU.is_equal))
                    link(v.tensor_tensor(by(m.level, NG * NG), by(m.level, NG * NG),
                                         w.ahead.unsqueeze(1).broadcast_to([P, nt, NG * NG]), ALU.mult))
                    link(v.tensor_tensor(flat(m.above, NG * NG), flat(m.above, NG * NG), flat(m.level, NG * NG), ALU.add))
                if part == 2:
                    rank = flat(m.rank, NG)
                    link(v.tensor_reduce(rank, flat(m.above, NG * NG).rearrange("p (x j) -> p x j", j=NG), AX.X, ALU.add))
                    link(v.tensor_scalar(rank, rank, TOPG - 0.5, None, ALU.is_lt))
                    link(v.tensor_tensor(flat(m.masked, NE).rearrange("p (x e) -> p x e", e=NE // NG),
                                         flat(m.choice, NE).rearrange("p (x e) -> p x e", e=NE // NG),
                                         rank.unsqueeze(2).broadcast_to([P, nt * NG, NE // NG]), ALU.mult))
                    for t in range(nt):
                        op = v.max(m.top8[:, t, :], masked[:, t, :])
                    link(op)
                    fourth = m.top8[:, 0:nt, TOPK - 1:TOPK].broadcast_to([P, nt, NE])
                    v.tensor_tensor(picked, masked, fourth, ALU.is_gt)
                    link(v.tensor_tensor(count[:, 0, :, NE // 2:], masked, fourth, ALU.is_equal))
                room = m.room[:, 0:nt]
                shifts = ((0, 1, 1), (1, 2, 2), (2, 1, 4), (1, 2, 8))

                def add_shifted(src, dst, shift):
                    link(v.tensor_tensor(count[:, dst, :, NE // 2:], count[:, src, :, NE // 2:],
                                         count[:, src, :, NE // 2 - shift:NE // 2 - shift + NE], ALU.add))
                if part == 3:
                    link(v.tensor_reduce(room, picked, AX.X, ALU.add))
                    link(v.tensor_scalar(room, room, -1.0, float(TOPK), ALU.mult, ALU.add))
                    for shift in shifts[:3]:
                        add_shifted(*shift)
                if part == 4:
                    add_shifted(*shifts[3])
                    link(v.tensor_tensor(fits, count[:, shifts[3][1], :, NE // 2:], room.unsqueeze(2).broadcast_to([P, nt, NE]), ALU.is_le))
                    link(v.tensor_tensor(fits, fits, count[:, 0, :, NE // 2:], ALU.mult))
                    link(v.tensor_tensor(picked, picked, fits, ALU.add))
                    link(v.tensor_tensor(picked, picked, score, ALU.mult))
                total = m.total[:, 0:nt]
                if part == 5:
                    link(v.tensor_reduce(total, picked, AX.X, ALU.add))
                    link(v.tensor_scalar(total, total, 1e-20, None, ALU.add))
                    link(v.reciprocal(total, total))
                    link(v.scalar_tensor_tensor(out=cw, in0=picked, scalar=2.5, in1=total.unsqueeze(2).broadcast_to([P, nt, NE]),
                                                op0=ALU.mult, op1=ALU.mult))
                if part == 6:
                    link(v.tensor_copy(cw3[:, :, 0:NE], cw))
                    link(v.tensor_tensor(cw, cw, cw3[:, :, 0:NE], ALU.subtract))
                    link(v.tensor_copy(cw3[:, :, 32:32 + NE], cw))
                    v.tensor_tensor(cw3[:, :, 64:64 + NE], cw, cw3[:, :, 32:32 + NE], ALU.subtract).then_inc(s["cw_ready"], 1)

            def residual(c):
                dve.wait_ge(s["y_psum"], MM * (c + 1))
                wait(dve, s["x_new"], c)
                v.tensor_tensor(m.r4[:, 0, :, :].rearrange("p t d -> p (t d)"), psY[:, :],
                                m.X[:, CT * c:CT * (c + 1), :].rearrange("p t d -> p (t d)"), ALU.add).then_inc(s["r_done"], 1)
                dve.wait_ge(s["r_done"], c + 1)
                for t in range(CT):
                    op = v.bn_stats(m.bn24[:, t, :], m.r4[:, 0, t, :])
                link(op)
                for t in range(CT):
                    op = v.bn_aggr(m.meanvar4[:, 0, t, :], m.bn24[:, t, :])
                op.then_inc(s["var_ready"], 1)

            def apply(c):
                dve.wait_ge(s["rstd_ready"], c + 1)
                for t in range(CT):
                    op = v.tensor_scalar(m.X[:, CT * c + t, :], m.r4[:, 0, t, :], m.meanvar4[:, 0, t, 0:1], m.rstd4[:, 0, t:t + 1],
                                         ALU.subtract, ALU.mult)
                op.then_inc(s["x_new"], 1)

            dve.wait_ge(s["zeros"], 1)
            for part in range(7):
                route(0, part)
            for c in range(NC):
                for j in range(NM):
                    g, n = NM * c + j, MM * c + j
                    dve.wait_ge(s["gate_psum"], g + 1)
                    dve.wait_ge(s["relu_ready"], n + 1)
                    last = g - 2
                    wait(dve, s["hid_ready"], MM * (last // NM) + last % NM + 1 if last >= 0 else 0)
                    v.tensor_tensor(m.gated[:, g % 2, :], m.relu[:, n % DEEP, :], psW[g % 2][:, :], ALU.mult).then_inc(s["gated"], 1)
                    if j == LAG - 1 and c > 0:
                        residual(c - 1)
                    if j == LAG + 2 and c > 0:
                        apply(c - 1)
                    if c == 0 and j < 7:
                        route(1, j)
            residual(NC - 1)
            apply(NC - 1)



MAGIC = 12582912.0
QMAX = 32767.0
SIG = 65536.0
NJ = 3


def quantised(nc, m, w, prefix):
    with ExitStack() as ctx:
        s = m.stages.semaphores(prefix,
                       "step wT_psum wT_ready xT_psum col_psum col_ready row_ready all_psum scaled x_shifted x_ready gu_psum gu_copied"
                       " g_shifted g_int pool_int pool_product sig_ready sig_int product own_product u_shifted u_int q_shifted o_shifted"
                       " last_shifted o_ready o_last y_psum sum_done var_ready ln_done rstd_ready offset_ready act_x_new dve_x_new")
        def sb(name, shape, dt=F32):
            return ctx.enter_context(nc.sbuf_tensor(prefix + name, shape, dt))

        m.xq = sb("xq", [P, NC, CH])
        m.G, m.U = sb("G", [P, NC, NJ, CH]), sb("U", [P, NC, NJ, CH])
        m.S = sb("S", [P, NC, NJ, CH])
        psM = m.bank[7]
        block = ctx.enter_context(nc.Block())

        NP = NJ * NC
        POOL_PRODUCTS = 3
        ON_DVE = (1, 1, 1, 3)
        ORDER = (3, 2, 0, 1)

        def absmax(eng, out, in_):
            return eng.tensor_reduce(out, in_, AX.XY if len(in_.shape) > 2 else AX.X, ALU.max, apply_absolute_value=True)

        @block.sync
        def _(sp):
            for c in range(NC):
                sp.wait_ge(s["act_x_new"], c + 1)
                sp.wait_ge(s["dve_x_new"], c + 1)
                sp.dma_start(w.dram_out[:, CT * c:CT * (c + 1), :], m.X[:, CT * c:CT * (c + 1), :]).then_inc(m.stored, 16)
            sp.wait_ge(m.stored, 16 * NC)

        @block.gpsimd
        def _(pool):
            m.stages.zero_spent(pool)
            for c in range(POOL_PRODUCTS):
                pool.wait_ge(s["g_int"], c + 1)
                pool.wait_ge(s["sig_int"], c + 1)
                nc.gpsimd.tensor_tensor(m.G[:, c, :, :], m.S[:, c, :, :], m.G[:, c, :, :], ALU.mult).then_inc(s["product"], 1)
            for n, c in enumerate(ORDER[0:2]):
                pool.wait_ge(s["pool_int"], n + 1)
                nc.gpsimd.tensor_tensor(m.G[:, c, :, :], m.G[:, c, :, :], m.U[:, c, :, :], ALU.mult).then_inc(s["pool_product"], 1)

        @block.tensor
        def _(pe):
            def turn_max(k):
                pe.wait_ge(s["col_ready"], k + 1)
                nc.tensor.transpose(psM[0:1, 0:P], m.q_col[:, 0:1], m.ident).then_inc(s["col_psum"], 1)

            def spread_max(k):
                pe.wait_ge(s["row_ready"], k + 1)
                nc.tensor.matmul(psM[:, P:P + 1], m.ones_row[0:1, :], m.q_one[0:1, 0:1], start=True,
                                 stop=True).then_inc(s["all_psum"], 1)

            for c in range(NC):
                for t in range(CT):
                    mm = nc.tensor.transpose(m.bank[c][:, t * P:(t + 1) * P], m.X[:, CT * c + t, :], m.ident)
                mm.then_inc(s["xT_psum"], 1)
            for n in range(3 * NJ):
                mm = nc.tensor.transpose(m.bank[4 + n // 3][:, n % 3 * P:(n % 3 + 1) * P], m.qw[:, 4 * n:4 * n + 4, :], m.ident)
            mm.then_inc(s["wT_psum"], 1)
            turn_max(0)
            spread_max(0)
            for n in range(2 * NP):
                which, j, c = n // NP, n % NP // NC, n % NC
                if n < NC:
                    pe.wait_ge(s["x_ready"], n + 1)
                    pe.wait_ge(s["wT_ready"], 3)
                wait(pe, s["gu_copied"], n - 2)
                nc.tensor.matmul(m.bank[4 + n % 3][:, :], (w.gate, w.up)[which][:, j, :], m.xq[:, c, :], start=True,
                                 stop=True).then_inc(s["gu_psum"], 1)
                if n == NP + 1:
                    turn_max(1)
                if n == NP + 2:
                    spread_max(1)
            for k in range(2, 5):
                turn_max(k)
                spread_max(k)
            for c in range(NC):
                pe.wait_ge(s["o_ready"] if c < NC - 1 else s["o_last"], c + 1 if c < NC - 1 else 1)
                for t in range(CT):
                    for j in range(NJ):
                        mm = nc.tensor.matmul(m.bank[c][:, t * D:(t + 1) * D], m.G[:, c, j, t * P:(t + 1) * P], w.down[:, j, :],
                                              start=(j == 0), stop=(j == NJ - 1))
                mm.then_inc(s["y_psum"], 1)

        @block.scalar
        def _(act):
            def shift(out, in_, scale):
                return nc.scalar.activation(out, in_, ACT.Identity, bias=m.magic[:, 0:1], scale=scale)

            def copy_piece(n):
                act.wait_ge(s["gu_psum"], n + 1)
                dst = (m.G if n < NP else m.U)[:, n % NC, n % NP // NC, :]
                nc.scalar.activation(dst, m.bank[4 + n % 3][:, :], ACT.Copy).then_inc(s["gu_copied"], 1)

            def sigmoid(c):
                act.wait_ge(s["g_int"], c + 1)
                nc.scalar.activation(m.S[:, c, :, :], m.G[:, c, :, :], ACT.Sigmoid, scale=m.q_s[:, 1:2]).then_inc(s["sig_ready"], 1)

            def apply(c):
                act.wait_ge(s["offset_ready"], c + 1)
                for t in range(ON_DVE[c], CT):
                    x = m.X[:, CT * c + t, :]
                    op = nc.scalar.activation(x, x, ACT.Identity, bias=m.offset16[:, c, t:t + 1], scale=m.rstd16[:, c, t:t + 1])
                op.then_inc(s["act_x_new"], 1)

            act.wait_ge(s["wT_psum"], 1)
            for n in range(3):
                nc.scalar.activation(m.qwT[:, 3 * n:3 * n + 3, :].rearrange("p n o -> p (n o)"), m.bank[4 + n][:, 0:3 * P],
                                     ACT.Copy).then_inc(s["wT_ready"], 1)
            act.wait_ge(s["scaled"], 1)
            for c in range(NC):
                act.wait_ge(s["xT_psum"], c + 1)
                shift(m.xq[:, c, :], m.bank[c][:, :], m.q_k[:, 0:1]).then_inc(s["x_shifted"], 1)
            for n in range(NP + 4):
                copy_piece(n)
            act.wait_ge(s["scaled"], 2)
            for c in range(NC):
                shift(m.G[:, c, :, :], m.G[:, c, :, :], m.q_k[:, 1:2]).then_inc(s["g_shifted"], 1)
                for n in range(NP + 4 + 2 * c, NP + 6 + 2 * c):
                    copy_piece(n)
                if c > 0:
                    sigmoid(c - 1)
            sigmoid(NC - 1)
            act.wait_ge(s["scaled"], 3)
            for c in ORDER:
                shift(m.U[:, c, :, :], m.U[:, c, :, :], m.q_k[:, 2:3]).then_inc(s["u_shifted"], 1)
            act.wait_ge(s["scaled"], 4)
            for c in ORDER:
                shift(m.G[:, c, :, :], m.G[:, c, :, :], m.q_k[:, 3:4]).then_inc(s["q_shifted"], 1)
            act.wait_ge(s["scaled"], 5)
            for c in range(NC - 1):
                shift(m.G[:, c, :, :], m.G[:, c, :, :], m.q_k[:, 4:5]).then_inc(s["o_shifted"], 1)
            act.preload_act_table_set("natural_log_exp_and_others")
            for c in range(NC):
                if c > 0:
                    apply(c - 1)
                act.wait_ge(s["var_ready"], c + 1)
                nc.scalar.activation(m.lnvar16[:, c, :], m.meanvar16[:, c, :, 1], ACT.Ln, bias=m.eps[:, 0:1]).then_inc(s["ln_done"], 1)
                act.wait_ge(s["ln_done"], c + 1)
                nc.scalar.activation(m.rstd16[:, c, :], m.lnvar16[:, c, :], ACT.Exp, scale=-0.5).then_inc(s["rstd_ready"], 1)
            apply(NC - 1)

        @block.vector
        def _(dve):
            v = nc.vector
            link = Chain(dve, s["step"]).link

            def scale(k, parts, unit, meanwhile=()):
                v.tensor_reduce(m.q_col[:, 0:1], parts, AX.X, ALU.max).then_inc(s["col_ready"], 1)
                for step in meanwhile[0:1]:
                    step()
                dve.wait_ge(s["col_psum"], k + 1)
                v.tensor_reduce(m.q_one[0:1, 0:1], psM[0:1, 0:P], AX.X, ALU.max).then_inc(s["row_ready"], 1)
                for step in meanwhile[1:]:
                    step()
                dve.wait_ge(s["all_psum"], k + 1)
                if unit is None:
                    link(v.tensor_scalar(m.q_s[:, k:k + 1], psM[:, P:P + 1], 1.0 / QMAX, 1e-12, ALU.mult, ALU.max))
                    v.reciprocal(m.q_k[:, k:k + 1], m.q_s[:, k:k + 1]).then_inc(s["scaled"], 1)
                else:
                    link(v.tensor_scalar(m.q_t[:, 0:1], psM[:, P:P + 1], unit, 1.0 / QMAX, ALU.mult, ALU.mult))
                    link(v.tensor_scalar(m.q_s[:, k:k + 1], m.q_t[:, 0:1], 1e-12, None, ALU.max))
                    link(v.reciprocal(m.q_t[:, 0:1], m.q_s[:, k:k + 1]))
                    v.tensor_tensor(m.q_k[:, k:k + 1], m.q_t[:, 0:1], unit, ALU.mult).then_inc(s["scaled"], 1)

            def piece_max(n):
                dve.wait_ge(s["gu_copied"], n + 1)
                return absmax(v, m.q_parts[:, n:n + 1], (m.G if n < NP else m.U)[:, n % NC, n % NP // NC, :])

            def gate_integers(c):
                dve.wait_ge(s["g_shifted"], c + 1)
                v.tensor_scalar(m.G[:, c, :, :], m.G[:, c, :, :], MAGIC, None, ALU.subtract).then_inc(s["g_int"], 1)

            def sigmoid_integers(c):
                dve.wait_ge(s["sig_ready"], c + 1)
                link(v.tensor_scalar(m.S[:, c, :, :], m.S[:, c, :, :], SIG, MAGIC, ALU.mult, ALU.add))
                v.tensor_scalar(m.S[:, c, :, :], m.S[:, c, :, :], MAGIC + SIG - 1, MAGIC, ALU.min, ALU.subtract).then_inc(s["sig_int"], 1)

            def up_integers(n):
                c = ORDER[n]
                dve.wait_ge(s["u_shifted"], n + 1)
                v.tensor_scalar(m.U[:, c, :, :], m.U[:, c, :, :], MAGIC, None, ALU.subtract).then_inc(s["u_int"], 1)

            link(absmax(v, m.q_parts[:, 0:1], m.X[:, :, :]))
            scale(0, m.q_parts[:, 0:1], None)
            for c in range(NC):
                dve.wait_ge(s["x_shifted"], c + 1)
                v.tensor_scalar(m.xq[:, c, :], m.xq[:, c, :], MAGIC, None, ALU.subtract).then_inc(s["x_ready"], 1)
            for n in range(NP):
                op = piece_max(n)
            link(op)
            scale(1, m.q_parts[:, 0:NP], m.q_s[:, 0:1])
            for c in range(NC):
                gate_integers(c)
                for n in range(NP + NJ * c, NP + NJ * (c + 1)):
                    op = piece_max(n)
                if c == NC - 1:
                    link(op)
                if c >= 2:
                    sigmoid_integers(c - 2)
            scale(2, m.q_parts[:, NP:2 * NP], m.q_s[:, 0:1], [lambda: sigmoid_integers(2)])
            for c in range(NC):
                if c >= POOL_PRODUCTS:
                    dve.wait_ge(s["sig_int"], c + 1)
                    v.tensor_tensor(m.G[:, c, :, :], m.S[:, c, :, :], m.G[:, c, :, :], ALU.mult).then_inc(s["own_product"], 1)
                    dve.wait_ge(s["own_product"], c + 1 - POOL_PRODUCTS)
                else:
                    if c + 2 < NC and c > 0:
                        sigmoid_integers(c + 2)
                    dve.wait_ge(s["product"], c + 1)
                op = absmax(v, m.q_parts[:, c:c + 1], m.G[:, c, :, :])
            link(op)
            link(v.tensor_scalar(m.q_u[:, 0:1], m.q_s[:, 1:2], 1.0 / SIG, None, ALU.mult))
            scale(3, m.q_parts[:, 0:NC], m.q_u[:, 0:1], [lambda: up_integers(0), lambda: up_integers(1)])
            for n, c in enumerate(ORDER):
                dve.wait_ge(s["q_shifted"], n + 1)
                if n < 2:
                    dve.wait_ge(s["u_int"], n + 1)
                    v.tensor_scalar(m.G[:, c, :, :], m.G[:, c, :, :], MAGIC, None, ALU.subtract).then_inc(s["pool_int"], 1)
                    up_integers(n + 2)
                else:
                    dve.wait_ge(s["u_int"], n + 1)
                    link(v.scalar_tensor_tensor(out=m.G[:, c, :, :], in0=m.G[:, c, :, :], scalar=MAGIC, in1=m.U[:, c, :, :],
                                                op0=ALU.subtract, op1=ALU.mult))
                    absmax(v, m.q_parts[:, c:c + 1], m.G[:, c, :, :])
            for n, c in enumerate(ORDER[0:2]):
                dve.wait_ge(s["pool_product"], n + 1)
                op = absmax(v, m.q_parts[:, c:c + 1], m.G[:, c, :, :])
            link(op)
            link(v.tensor_tensor(m.q_u[:, 1:2], m.q_s[:, 3:4], m.q_s[:, 2:3], ALU.mult))
            scale(4, m.q_parts[:, 0:NC], m.q_u[:, 1:2])
            last = m.G[:, NC - 1, :, :]
            dve.wait_ge(s["scaled"], 5)
            v.tensor_scalar(last, last, m.q_k[:, 4:5], MAGIC, ALU.mult, ALU.add).then_inc(s["last_shifted"], 1)
            for c in range(NC - 1):
                dve.wait_ge(s["o_shifted"], c + 1)
                v.tensor_scalar(m.G[:, c, :, :], m.G[:, c, :, :], MAGIC, None, ALU.subtract).then_inc(s["o_ready"], 1)
            dve.wait_ge(s["last_shifted"], 1)
            v.tensor_scalar(last, last, MAGIC, None, ALU.subtract).then_inc(s["o_last"], 1)

            def offset(c):
                dve.wait_ge(s["rstd_ready"], c + 1)
                v.scalar_tensor_tensor(out=m.offset16[:, c, :], in0=m.meanvar16[:, c, :, 0], scalar=-1.0,
                                       in1=m.rstd16[:, c, :], op0=ALU.mult, op1=ALU.mult).then_inc(s["offset_ready"], 1)

            def apply(c):
                for t in range(ON_DVE[c]):
                    x = m.X[:, CT * c + t, :]
                    op = v.tensor_scalar(x, x, m.meanvar16[:, c, t, 0:1], m.rstd16[:, c, t:t + 1], ALU.subtract, ALU.mult)
                op.then_inc(s["dve_x_new"], 1)

            for c in range(NC):
                dve.wait_ge(s["y_psum"], c + 1)
                x = m.X[:, CT * c:CT * (c + 1), :].rearrange("p t d -> p (t d)")
                op = v.scalar_tensor_tensor(out=x, in0=m.bank[c][:, :], scalar=m.q_s[:, 4:5], in1=x, op0=ALU.mult, op1=ALU.add)
                op.then_inc(s["sum_done"], 1)
                if c > 0:
                    offset(c - 1)
                    apply(c - 1)
                dve.wait_ge(s["sum_done"], c + 1)
                for t in range(CT):
                    op = v.bn_stats(m.bn24[:, t, :], m.X[:, CT * c + t, :])
                link(op)
                for t in range(CT):
                    op = v.bn_aggr(m.meanvar16[:, c, t, :], m.bn24[:, t, :])
                op.then_inc(s["var_ready"], 1)
            offset(NC - 1)
            apply(NC - 1)



HEAD_COLS = [("ident", P), ("mask_ac", 4), ("mask_ca", 4), ("mask_i", NI), ("causal", T), ("w0_q", D), ("w0_k", D), ("w0_v", D), ("w0_o", D),
             ("w0_bias", D)]
MID_COLS = [("cos", T), ("sin", T), ("x0_q", D), ("x0_qr", D), ("x0_k", D), ("x0_kr", D), ("x0_v", D), ("x0_o", D)]
BODY_COLS = [("x1_q", D), ("x1_k", D), ("x1_v", D), ("x1_o", D), ("x1_qr", D), ("x1_kr", D),
             ("x1_bq", 1), ("x1_bk", 1), ("x1_bqr", 1), ("x1_bkr", 1), ("x1_bv", 1),
             ("x1_of", D), ("x1_bo", D),
             ("l_dq", LC), ("l_df", LC + LR), ("l_uq", LH * (LC + 1)), ("l_uk", LH * (LC + 1)), ("l_uv", LH * LC),
             ("l_buv", LH), ("l_o", LH * D), ("l_bo", D), ("l_bl", 1),
             ("e_router", NE), ("e_bias", NE), ("e_ahead", NG * NG), ("e_w1", NE * 64), ("e_w2", NM * D), ("e_s1", D), ("e_s2", D),
             ("e_spread", NM * P), ("q_w", 9 * D)]
ROW64_COLS = [("l_qr", LH * LR),
              ("l_bq", 1), ("l_bf", 1)]


BODY_PARTS = 4


def columns(cols):
    at, out = 0, {}
    for name, n in cols:
        out[name] = (at, n)
        at += n
    return out, at


def decoder(nc, x, ctxT, mask, head, mid, body, row64, out):
    with ExitStack() as ctx:
        m = Names()

        def sb(name, shape, dt=F32):
            return ctx.enter_context(nc.sbuf_tensor(name, shape, dt))

        m.bank = [ctx.enter_context(nc.psum_tensor(f"bank{i}", [P, 512], F32)) for i in range(8)]
        m.ctxT_dram = ctxT
        m.stages = Stages(nc)
        m.X = sb("X", [P, NT, D])
        head_at, head_n = columns(HEAD_COLS)
        mid_at, mid_n = columns(MID_COLS)
        body_at, body_n = columns(BODY_COLS)
        row64_at, row64_n = columns(ROW64_COLS)
        head_sb = sb("head_sb", [P, head_n])
        mid_sb = sb("mid_sb", [P, mid_n])
        body_sb = sb("body_sb", [P, body_n])
        row64_sb = sb("row64_sb", [T, row64_n])

        def h(name):
            at, n = head_at[name]
            return head_sb[:, at:at + n]

        def mi(name):
            at, n = mid_at[name]
            return mid_sb[:, at:at + n]

        def bd(name):
            at, n = body_at[name]
            return body_sb[:, at:at + n]

        def r64(name):
            at, n = row64_at[name]
            return row64_sb[:, at:at + n]

        m.ident, m.mask_ac, m.mask_ca, m.mask_i, m.causal = h("ident"), h("mask_ac"), h("mask_ca"), h("mask_i"), h("causal")
        m.cos, m.sin = mi("cos"), mi("sin")
        m.mask_u8 = sb("mask_u8", [1, NSEQ * T], U8)
        m.mask_row = sb("mask_row", [1, NSEQ * T], BF16)
        m.ones_bf = sb("ones_bf", [1, P], BF16)
        m.one = sb("one", [P, 1])
        m.eps = sb("eps", [P, 1])
        m.xs = sb("xs", [P, 2, P])
        m.xb = sb("xb", [P, 2, P])
        m.xT = sb("xT", [P, 2, SB, 2, T])
        m.kvT = sb("kvT", [P, 2, SB, 2, T])
        m.qk = sb("qk", [P, 2, 2, P])
        m.vals = sb("vals", [P, 2, SB, NI, 2, 2, HD + 1])
        m.rowmax = sb("rowmax", [P, SB, 8])
        m.den = sb("den", [P, 16])
        m.rden = sb("rden", [P, 16])
        m.o = sb("o", [P, 2, SB, T])
        m.oT = sb("oT", [P, 2, P])
        m.r = sb("r", [P, D])
        m.bn6 = sb("bn6", [P, 6])
        m.meanvar = sb("meanvar", [P, 2])
        m.lnvar = sb("lnvar", [P, 1])
        m.rstd = sb("rstd", [P, 1])
        m.f = sb("f", [P, 2, P])
        m.cq = sb("cq", [P, 2, P])
        m.g = sb("g", [P, 2, SB, LH, T])
        m.lvals = sb("lvals", [P, 2, SB, 2, LC + 1])
        m.lprob = sb("lprob", [P, 2, SB, 2, P])
        m.lprobT = sb("lprobT", [P, 512])
        m.lo = sb("lo", [P, 2, SB, P])
        m.ones_row = sb("ones_row", [1, P])
        m.l_score = sb("l_score", [P, LH, P])
        m.l_out = sb("l_out", [P, 2, D])
        m.made_bias = sb("made_bias", [P, 2 * D])
        m.r4, m.bn24, m.meanvar4 = sb("r4", [P, 1, CT, D]), sb("bn24", [P, CT, 6]), sb("meanvar4", [P, 1, CT, 2])
        m.lnvar4, m.rstd4 = sb("lnvar4", [P, 1, CT]), sb("rstd4", [P, 1, CT])
        m.meanvar16, m.offset16 = sb("meanvar16", [P, NC, CT, 2]), sb("offset16", [P, NC, CT])
        m.lnvar16, m.rstd16 = sb("lnvar16", [P, NC, CT]), sb("rstd16", [P, NC, CT])
        m.magic = sb("magic", [P, 1])
        m.q_col, m.q_one, m.q_t, m.q_u = sb("q_col", [P, 1]), sb("q_one", [1, 1]), sb("q_t", [P, 1]), sb("q_u", [P, 2])
        m.q_s, m.q_k, m.q_parts = sb("q_s", [P, 5]), sb("q_k", [P, 5]), sb("q_parts", [P, 2 * NJ * NC])
        m.qw = sb("qw", [P, 9 * 4, 32])
        m.qwT = sb("qwT", [P, 9, D])
        m.qw_s, m.qw_i = sb("qw_s", [P, 36]), sb("qw_i", [P, 36])

        m.load = {n: ctx.enter_context(nc.semaphore("load_" + n)) for n in ("head", "x_first", "x_rest", "mid", "mask", "body")}
        m.x_dram = x.rearrange("(t p) c -> p t c", p=P)
        with ExitStack() as c2:
            s = m.stages.semaphores("i_", "zeros memset")
            block = c2.enter_context(nc.Block())

            @block.sync
            def _(sp):
                sp.dma_start(m.mask_u8[:, :], mask).then_inc(m.load["mask"], 16)
                sp.dma_start(m.X[:, 0:2, :], m.x_dram[:, 0:2, :]).then_inc(m.load["x_first"], 16)
                sp.dma_start(head_sb[:, :], head).then_inc(m.load["head"], 16)
                sp.dma_start(m.X[:, 2:, :], m.x_dram[:, 2:, :]).then_inc(m.load["x_rest"], 16)
                sp.wait_ge(m.load["x_first"], 16)
                sp.wait_ge(m.load["head"], 16)

            @block.gpsimd
            def _(pool):
                pool.memset(m.ones_bf[:, :], 1.0)
                pool.memset(m.one[:, :], 1.0)
                pool.memset(m.eps[:, :], EPS)
                pool.memset(m.magic[:, :], MAGIC)
                pool.memset(m.ones_row[:, :], 1.0)
                pool.memset(m.lvals[:, :, :, :, :], 0.0)
                pool.memset(m.vals[:, :, :, :, :, :, :], 0.0).then_inc(s["zeros"], 1)
                pool.wait_ge(s["zeros"], 1)
                for a in range(2):
                    for par in range(2):
                        pool.memset(m.vals[a * T:a * T + T, par, :, :, a, :, HD], 1.0)
                        pool.memset(m.lvals[a * T:a * T + T, par, :, a, LC], 1.0)

            @block.vector
            def _(dve):
                nc.vector.memset(m.l_score[:, :, :], 0.0)
                nc.vector.memset(m.cq[:, :, :], 0.0)
                nc.vector.memset(m.f[LC + LR:, :, :], 0.0).then_inc(s["memset"], 1)
                dve.wait_ge(s["memset"], 1)
                nc.vector.memset(m.cq[LC:LC + 1, :, :], 1.0)
                nc.vector.memset(m.f[LC + LR:LF, :, :], 1.0)
                dve.wait_ge(m.load["mask"], 16)
                nc.vector.tensor_scalar(m.mask_row[:, :], m.mask_u8[:, :], 1.0, BIG, ALU.subtract, ALU.mult)

        def wait_for_x_rest(sp):
            sp.wait_ge(m.load["x_rest"], 16)

        def load_mid(sp):
            sp.dma_start(mid_sb[:, :], mid).then_inc(m.load["mid"], 16)

        def load_body_part(n):
            cols = slice(body_n * n // BODY_PARTS, body_n * (n + 1) // BODY_PARTS)
            return lambda sp: sp.dma_start(body_sb[:, cols], body[:, cols]).then_inc(m.load["body"], 16)

        def load_row64(sp):
            sp.dma_start(row64_sb[:, :], row64).then_inc(m.load["body"], 16)

        loads = {2: [wait_for_x_rest], 3: [load_mid], 4: [load_row64, load_body_part(0)], 5: [load_body_part(1)], 6: [load_body_part(2)], 7: [load_body_part(3)]}

        w = Names()
        w.wq, w.wk, w.wv, w.wo, w.bias_tile, w.mask_row = h("w0_q"), h("w0_k"), h("w0_v"), h("w0_o"), h("w0_bias"), None
        v = Names()
        v.wq, v.wk, v.wv, v.wo, v.bias_tile, v.mask_row = mi("x0_q"), mi("x0_k"), mi("x0_v"), mi("x0_o"), None, m.mask_row
        v.wqr, v.wkr = mi("x0_qr"), mi("x0_kr")
        v.bq = v.bqr = v.bk = v.bkr = 0.0
        causal_then_cross(nc, m, w, v, loads, "a0_")

        w = Names()
        w.router, w.bias16, w.ahead = bd("e_router"), bd("e_bias"), bd("e_ahead")
        w.w1, w.w2, w.shared1, w.shared2 = bd("e_w1"), bd("e_w2"), bd("e_s1"), bd("e_s2")
        w.uq, w.uk, w.uv = (bd(n).rearrange("p (h l) -> p h l", h=LH) for n in ("l_uq", "l_uk", "l_uv"))
        w.up_o, w.buv, w.b_latent, w.l_bo = bd("l_o").rearrange("p (h o) -> p h o", h=LH), bd("l_buv"), bd("l_bl"), bd("l_bo")[0:1, :]
        w.x1_bv, w.x1_o, w.x1_bo, w.qr, w.spread = bd("x1_bv"), bd("x1_of"), bd("x1_bo")[0:1, :], r64("l_qr")[0:LC + 1, :], bd("e_spread")
        experts(nc, m, w, "e_")
        w = Names()
        w.dq, w.df, w.b_q, w.b_f = bd("l_dq"), bd("l_df"), r64("l_bq")[0:LC, :], r64("l_bf")
        w.q_w = bd("q_w")
        w.score, w.out, w.bias_tile = m.l_score, m.l_out, m.made_bias[:, 0:D]
        v = Names()
        v.wq, v.wk, v.wv, v.wo, v.bias_tile, v.mask_row = bd("x1_q"), bd("x1_k"), bd("x1_v"), bd("x1_o"), m.made_bias[:, D:2 * D], None
        v.wqr, v.wkr = bd("x1_qr"), bd("x1_kr")
        v.bq, v.bk, v.bqr, v.bkr = bd("x1_bq"), bd("x1_bk"), bd("x1_bqr"), bd("x1_bkr")
        latent_then_cross(nc, m, w, v, "l1_")
        w = Names()
        m.stored = ctx.enter_context(nc.semaphore("stored"))
        w.dram_out = out.rearrange("(t p) c -> p t c", p=P)
        w.gate, w.up, w.down = m.qwT[:, 0:3, :], m.qwT[:, 3:6, :], m.qwT[:, 6:9, :]
        quantised(nc, m, w, "q_")


def host_constants():
    import numpy as np
    c = {"ident": np.eye(P, dtype=np.float32)}
    p = np.arange(P)
    c["mask_ac"] = (p[:, None] // HD % 4 == np.arange(4)).astype(np.float32)
    c["mask_ca"] = np.ascontiguousarray(c["mask_ac"][:, [0, 2, 1, 3]])
    c["mask_i"] = (p[:, None] // (4 * HD) == np.arange(NI)).astype(np.float32)
    c["causal"] = np.where(p[:, None] % T <= np.arange(T), 0.0, -1e30).astype(np.float32)
    gj = np.arange(NG * NG)
    c["e_ahead"] = np.broadcast_to((gj % NG < gj // NG).astype(np.float32), (P, NG * NG))
    c["e_spread"] = (p[:, None] % 32 == np.arange(NM * P) // 64).astype(np.float32)
    d = p % HD
    inv = (1.0 / 10000.0 ** (np.arange(0, HD, 2, dtype=np.float32) / np.float32(HD))).astype(np.float32)
    ang = (np.arange(T, dtype=np.float32)[None, :] * inv[d % 4][:, None]).astype(np.float32)
    c["cos"] = np.cos(ang)
    c["sin"] = np.sin(ang) * np.where(d < HD // 2, -1, 1).astype(np.float32)[:, None]
    return c


def kernel(**inputs):
    import numpy as np
    import concourse.bacc as bacc
    from concourse.bass_utils import run_bass_kernel_spmd

    g = {k: np.asarray(v) for k, v in inputs.items()}
    parts = host_constants()

    def small_out(wT):
        return wT.reshape(NI, 2, 2, HD, D).transpose(2, 0, 1, 3, 4).reshape(P, D)

    qkv = g["L0_attn_w_qkv"]
    parts["w0_q"], parts["w0_k"], parts["w0_v"] = qkv[:D].T, qkv[D:2 * D].T, qkv[2 * D:].T
    parts["w0_bias"] = np.broadcast_to(g["L0_attn_b_proj"], (P, D))
    parts["w0_o"] = small_out(g["L0_attn_w_proj"].T)
    parts["x0_q"], parts["x0_k"], parts["x0_v"] = g["L0_xattn_Wq"], g["L0_xattn_Wkv"][:, :D], g["L0_xattn_Wkv"][:, D:]
    swapped = (np.arange(D) // HD) * HD + (np.arange(D) + HD // 2) % HD
    parts["x0_qr"], parts["x0_kr"] = parts["x0_q"][:, swapped], parts["x0_k"][:, swapped]
    parts["x0_o"] = small_out(g["L0_xattn_Wout"])
    for n in "qk":
        wt = g["L1_xattn_W" + n]
        parts["x1_" + n], parts["x1_" + n + "r"] = wt.T, wt.T[:, swapped]
        parts["x1_b" + n] = g["L1_xattn_b" + n].reshape(D, 1)
        parts["x1_b" + n + "r"] = parts["x1_b" + n][swapped]
    parts["x1_v"] = g["L1_xattn_Wv"].T
    parts["e_router"] = g["L0_ffn_Wg"].T
    parts["e_bias"] = np.broadcast_to(g["L0_ffn_bias_corr"], (P, NE))
    parts["e_w1"] = g["L0_ffn_W1"].reshape(NE * 64, D).T
    parts["e_w2"] = g["L0_ffn_W2"].transpose(0, 2, 1).reshape(NM, P, D).transpose(1, 0, 2).reshape(P, NM * D)
    parts["e_s1"], parts["e_s2"] = g["L0_ffn_Ws1"].T, g["L0_ffn_Ws2"].T

    def side_by_side(wt):
        return wt.reshape(-1, P, wt.shape[1]).transpose(1, 0, 2).reshape(P, -1)

    parts["q_w"] = np.concatenate([side_by_side(g["L1_ffn_w_gate"]), side_by_side(g["L1_ffn_w_up"]), g["L1_ffn_w_down"]], axis=1)
    parts["x1_bv"] = g["L1_xattn_bv"].reshape(D, 1)
    parts["x1_of"] = g["L1_xattn_Wo"].T
    parts["x1_bo"] = np.broadcast_to(g["L1_xattn_bo"], (P, D))

    def up(n):
        both = np.concatenate([g["L1_attn_W_" + n], g["L1_attn_b_" + n][None]], axis=0)
        return both.reshape(LC + 1, LH, D).transpose(2, 1, 0).reshape(D, LH * (LC + 1))

    def rows64(v):
        return np.concatenate([v, np.zeros((T - v.shape[0], v.shape[1]), np.float32)], axis=0)

    parts["l_dq"] = g["L1_attn_W_DQ"]
    parts["l_df"] = np.concatenate([g["L1_attn_W_DKV"], g["L1_attn_W_KR"]], axis=1)
    parts["l_uq"], parts["l_uk"] = up("UQ"), up("UK")
    parts["l_uv"] = g["L1_attn_W_UV"].reshape(LC, LH, D).transpose(2, 1, 0).reshape(D, LH * LC)
    parts["l_buv"] = g["L1_attn_b_UV"].reshape(LH, D).T
    parts["l_o"] = g["L1_attn_W_O"].reshape(LH, D, D).transpose(1, 0, 2).reshape(D, LH * D)
    parts["l_bo"] = np.broadcast_to(g["L1_attn_b_O"], (P, D))
    parts["l_qr"] = rows64(np.concatenate([g["L1_attn_W_QR"], g["L1_attn_b_QR"][None]], axis=0))
    parts["l_bq"] = rows64(g["L1_attn_b_DQ"][:, None])
    parts["l_bf"] = np.concatenate([g["L1_attn_b_DKV"], g["L1_attn_b_KR"]])[:, None]
    parts["l_bl"] = np.tile(g["L1_attn_b_DKV"], P // LC)[:, None]
    parts["x1_o"] = small_out(g["L1_xattn_Wo"].T)

    def pack(cols):
        return np.concatenate([parts[n] for n, _ in cols], axis=1)

    arrays = {
        "x": g["x"].reshape(NSEQ * T, D),
        "ctxT": g["ctx_1024"].reshape(NSEQ * T, D).T.reshape(D, NSEQ, T),
        "mask": g["mask_BxS2_bf1"].reshape(1, NSEQ * T).view(np.uint8),
        "head": pack(HEAD_COLS), "mid": pack(MID_COLS), "body": pack(BODY_COLS), "row64": pack(ROW64_COLS),
    }
    arrays = {f"in_{k}": np.ascontiguousarray(v) for k, v in arrays.items()}
    nc = bacc.Bacc("TRN2", target_bir_lowering=False, num_devices=1)
    args = [nc.dram_tensor(k, v.shape, mybir.dt.from_np(v.dtype), kind="ExternalInput").ap() for k, v in arrays.items()]
    out = nc.dram_tensor("out", (NSEQ * T, D), F32, kind="ExternalOutput").ap()
    decoder(nc, *args, out)
    r = run_bass_kernel_spmd(nc, [arrays], core_ids=[0])
    return r.results[0]["out"].reshape(NSEQ, T, D)
```
